# Optimizing a Trainium2 kernel written in Bass

```python
import numpy as np
import jax
import jax.numpy as jnp

def _softmax(x, axis=-1):
    return jax.nn.softmax(x, axis=axis)

def _gelu(x):
    return jax.nn.gelu(x, approximate=True)

def _silu(x):
    return jax.nn.silu(x)

def _sigmoid(x):
    return jax.nn.sigmoid(x)

def _layernorm(x, axis=-1, eps=1e-05):
    m = jnp.mean(x, axis=axis, keepdims=True)
    v = jnp.var(x, axis=axis, keepdims=True)
    return (x - m) / jnp.sqrt(v + eps)

def _scatter_add(tgt, idx, src, axis=0):
    return tgt.at[idx].add(src)

def _segment_sum(src, seg, n):
    return jax.ops.segment_sum(src, seg, n)
kernel_name = 'mk_xattn_ffn_d1_seqx_r2_7bd3d2'

def setup_inputs(seed: int=0):
    np.random.seed(seed)
    _w = jnp.asarray

    def _rec_inputs():
        import jax
        import jax.numpy as jnp
        _rk = jax.random.key(seed)
        x = -0.0003929 + 0.9999 * jax.random.normal(jax.random.fold_in(_rk, 1), (4, 1024, 1024), jnp.float32)
        _lenS = 1024 - jax.random.randint(jax.random.fold_in(_rk, 7), (4,), 0, max(1, 1024 // 4) + 1, jnp.int32)
        _lenS2 = 1024 - jax.random.randint(jax.random.fold_in(_rk, 8), (4,), 0, max(1, 1024 // 4) + 1, jnp.int32)
        _ctx_2048P = jax.random.normal(jax.random.fold_in(_rk, 11), (4, 16, 1024), jnp.float32)
        _ctx_2048c = jax.random.dirichlet(jax.random.fold_in(_rk, 511), 0.3 * jnp.ones((16,), jnp.float32), (4, 1024))
        _ctx_2048t = jnp.einsum('bsk,bkd->bsd', _ctx_2048c, _ctx_2048P)
        _ctx_2048t = _ctx_2048t * jax.lax.rsqrt(jnp.mean(jnp.square(_ctx_2048t)) + 1e-12) * 0.953939
        ctx_2048 = -0.000514642 + 1.00011 * (_ctx_2048t + 0.3 * jax.random.normal(jax.random.fold_in(_rk, 611), (4, 1024, 1024), jnp.float32))
        _validS = jnp.arange(1024)[None, :] < _lenS[:, None]
        _validS2 = jnp.arange(1024)[None, :] < _lenS2[:, None]
        _causal = jnp.tril(jnp.ones((1024, 1024), dtype=bool))
        mask_BxS2_ik0 = jnp.where(jnp.broadcast_to(_validS2[:, :], (4, 1024)), 0, 1).astype(jnp.int32)
        return (x, ctx_2048, mask_BxS2_ik0)
    x, ctx_2048, mask_BxS2_ik0 = _rec_inputs()

    def _L0_xattn_setup():
        import jax, jax.numpy as jnp
        import numpy as np
        import math
        H = 1024
        NH = 16
        HD = H // NH
        EPS_LN = 1e-05
        RES_SCALE_MAX = 0.3

        def _nan_clean(x, lim=10000.0):
            return jnp.nan_to_num(x, nan=0.0, posinf=lim, neginf=-lim)
        key = jax.random.key(seed)
        ks = jax.random.split(key, 12)
        B, S, T = (4, 1024, 128)
        std = 1.0 / math.sqrt(H)
        return {'hidden_states': jax.random.normal(ks[0], (B, S, H), jnp.float32), 'audio_tokens': jax.random.normal(ks[1], (B, T, H), jnp.float32), 'attention_mask': jax.random.randint(ks[2], (B, T), 0, 2, jnp.int32), 'Wq': jax.random.normal(ks[3], (H, H), jnp.float32) * std, 'bq': jnp.zeros((H,), jnp.float32), 'Wk': jax.random.normal(ks[4], (H, H), jnp.float32) * std, 'bk': jnp.zeros((H,), jnp.float32), 'Wv': jax.random.normal(ks[5], (H, H), jnp.float32) * std, 'bv': jnp.zeros((H,), jnp.float32), 'Wo': jax.random.normal(ks[6], (H, H), jnp.float32) * std, 'bo': jnp.zeros((H,), jnp.float32), 'ln_gamma': jnp.ones((H,), jnp.float32), 'ln_beta': jnp.zeros((H,), jnp.float32), 'residual_scale': jnp.float32(0.05)}
    _L0_xattn_all = _L0_xattn_setup()
    _L0_xattn_in = {k: v for k, v in _L0_xattn_all.items() if k in ('Wq', 'bq', 'Wk', 'bk', 'Wv', 'bv', 'Wo', 'bo', 'ln_gamma', 'ln_beta', 'residual_scale')}
    del _L0_xattn_all

    def _L0_ffn_setup():
        import jax, jax.numpy as jnp
        import numpy as np
        B, S, H = (2, 1024, 1024)
        E, K, I = (64, 8, 384)

        def _moe_forward(hidden_states, gate_weight, w_gate, w_up, w_down):
            b, s, h = hidden_states.shape
            x = hidden_states.reshape(-1, h)
            logits = x.astype(jnp.float32) @ gate_weight.astype(jnp.float32).T
            scores = jax.nn.softmax(logits, axis=-1)
            topk_w, topk_idx = jax.lax.top_k(scores, K)
            topk_w = topk_w / jnp.sum(topk_w, axis=-1, keepdims=True)
            flat_ids = topk_idx.reshape(-1)
            expanded = jnp.repeat(x, K, axis=0)
            order = jnp.argsort(flat_ids)
            sorted_tokens = expanded[order]
            group_sizes = jnp.zeros((E,), jnp.int32).at[flat_ids].add(1)
            g = jax.lax.ragged_dot(sorted_tokens, w_gate, group_sizes)
            u = jax.lax.ragged_dot(sorted_tokens, w_up, group_sizes)
            out = jax.lax.ragged_dot(jax.nn.silu(g) * u, w_down, group_sizes)
            inv = jnp.argsort(order)
            outs = out[inv].reshape(-1, K, h)
            y = jnp.sum(outs * topk_w[:, :, None], axis=1)
            return y.reshape(b, s, h)
        key = jax.random.key(seed)
        k0, k1, k2, k3, k4 = jax.random.split(key, 5)
        hidden_states = jax.random.normal(k0, (B, S, H), dtype=jnp.float32)
        gate_weight = jax.random.normal(k1, (E, H), dtype=jnp.float32) * 0.02
        w_gate = jax.random.normal(k2, (E, H, I), dtype=jnp.float32) * 0.02
        w_up = jax.random.normal(k3, (E, H, I), dtype=jnp.float32) * 0.02
        w_down = jax.random.normal(k4, (E, I, H), dtype=jnp.float32) * 0.02
        return {'hidden_states': hidden_states, 'gate_weight': gate_weight, 'w_gate': w_gate, 'w_up': w_up, 'w_down': w_down}
    _L0_ffn_all = _L0_ffn_setup()
    _L0_ffn_in = {k: v for k, v in _L0_ffn_all.items() if k in ('gate_weight', 'w_gate', 'w_up', 'w_down')}
    del _L0_ffn_all
    return {'x': x, 'ctx_2048': ctx_2048, 'mask_BxS2_ik0': mask_BxS2_ik0, 'L0_xattn_Wq': _L0_xattn_in['Wq'], 'L0_xattn_bq': _L0_xattn_in['bq'], 'L0_xattn_Wk': _L0_xattn_in['Wk'], 'L0_xattn_bk': _L0_xattn_in['bk'], 'L0_xattn_Wv': _L0_xattn_in['Wv'], 'L0_xattn_bv': _L0_xattn_in['bv'], 'L0_xattn_Wo': _L0_xattn_in['Wo'], 'L0_xattn_bo': _L0_xattn_in['bo'], 'L0_xattn_ln_gamma': _L0_xattn_in['ln_gamma'], 'L0_xattn_ln_beta': _L0_xattn_in['ln_beta'], 'L0_xattn_residual_scale': _L0_xattn_in['residual_scale'], 'L0_ffn_gate_weight': _L0_ffn_in['gate_weight'], 'L0_ffn_w_gate': _L0_ffn_in['w_gate'], 'L0_ffn_w_up': _L0_ffn_in['w_up'], 'L0_ffn_w_down': _L0_ffn_in['w_down']}

def reference(x, ctx_2048, mask_BxS2_ik0, L0_xattn_Wq, L0_xattn_bq, L0_xattn_Wk, L0_xattn_bk, L0_xattn_Wv, L0_xattn_bv, L0_xattn_Wo, L0_xattn_bo, L0_xattn_ln_gamma, L0_xattn_ln_beta, L0_xattn_residual_scale, L0_ffn_gate_weight, L0_ffn_w_gate, L0_ffn_w_up, L0_ffn_w_down):
    import jax
    import jax.numpy as jnp

    def _L0_xattn_ref(hidden_states, audio_tokens, attention_mask, Wq, bq, Wk, bk, Wv, bv, Wo, bo, ln_gamma, ln_beta, residual_scale):
        import jax, jax.numpy as jnp
        import numpy as np
        import math
        H = 1024
        NH = 16
        HD = H // NH
        EPS_LN = 1e-05
        RES_SCALE_MAX = 0.3

        def _nan_clean(x, lim=10000.0):
            return jnp.nan_to_num(x, nan=0.0, posinf=lim, neginf=-lim)
        B, S, _ = hidden_states.shape
        T = audio_tokens.shape[1]
        hs = _nan_clean(hidden_states).astype(jnp.float32)
        at = _nan_clean(audio_tokens).astype(jnp.float32)

        def proj(x, W, b, L):
            y = x @ W.T + b
            return y.reshape(B, L, NH, HD).transpose(0, 2, 1, 3)
        q = _nan_clean(proj(hs, Wq, bq, S))
        k = _nan_clean(proj(at, Wk, bk, T))
        v = _nan_clean(proj(at, Wv, bv, T))
        scale = max(math.sqrt(HD), 1e-08)
        scores = jnp.einsum('bhsd,bhtd->bhst', q, k) / scale
        scores = jnp.clip(scores, -50.0, 50.0)
        scores = jnp.nan_to_num(scores, nan=0.0, posinf=50.0, neginf=-50.0)
        attend = (attention_mask.astype(jnp.float32) > 0.5)[:, None, None, :]
        scores = jnp.where(attend, scores, -10000.0)
        scores = jnp.clip(scores, -50.0, 50.0)
        probs = jax.nn.softmax(scores, axis=-1)
        probs = jnp.nan_to_num(probs, nan=0.0, posinf=1.0, neginf=0.0)
        probs = probs / (probs.sum(axis=-1, keepdims=True) + 1e-08)
        ctx = jnp.einsum('bhst,bhtd->bhsd', probs, v)
        ctx = ctx.transpose(0, 2, 1, 3).reshape(B, S, H)
        delta = _nan_clean(ctx @ Wo.T + bo)
        rs = jnp.clip(residual_scale, 0.0, RES_SCALE_MAX)
        delta = rs * delta
        mu = delta.mean(axis=-1, keepdims=True)
        var = jnp.mean((delta - mu) ** 2, axis=-1, keepdims=True)
        delta = (delta - mu) / jnp.sqrt(var + EPS_LN) * ln_gamma + ln_beta
        return delta

    def _L0_ffn_ref(hidden_states, gate_weight, w_gate, w_up, w_down):
        import jax, jax.numpy as jnp
        import numpy as np
        B, S, H = (2, 1024, 1024)
        E, K, I = (64, 8, 384)

        def _moe_forward(hidden_states, gate_weight, w_gate, w_up, w_down):
            b, s, h = hidden_states.shape
            x = hidden_states.reshape(-1, h)
            logits = x.astype(jnp.float32) @ gate_weight.astype(jnp.float32).T
            scores = jax.nn.softmax(logits, axis=-1)
            topk_w, topk_idx = jax.lax.top_k(scores, K)
            topk_w = topk_w / jnp.sum(topk_w, axis=-1, keepdims=True)
            flat_ids = topk_idx.reshape(-1)
            expanded = jnp.repeat(x, K, axis=0)
            order = jnp.argsort(flat_ids)
            sorted_tokens = expanded[order]
            group_sizes = jnp.zeros((E,), jnp.int32).at[flat_ids].add(1)
            g = jax.lax.ragged_dot(sorted_tokens, w_gate, group_sizes)
            u = jax.lax.ragged_dot(sorted_tokens, w_up, group_sizes)
            out = jax.lax.ragged_dot(jax.nn.silu(g) * u, w_down, group_sizes)
            inv = jnp.argsort(order)
            outs = out[inv].reshape(-1, K, h)
            y = jnp.sum(outs * topk_w[:, :, None], axis=1)
            return y.reshape(b, s, h)
        return _moe_forward(hidden_states, gate_weight, w_gate, w_up, w_down)
    x = x + _L0_xattn_ref(_layernorm(x, axis=-1), ctx_2048, mask_BxS2_ik0, L0_xattn_Wq, L0_xattn_bq, L0_xattn_Wk, L0_xattn_bk, L0_xattn_Wv, L0_xattn_bv, L0_xattn_Wo, L0_xattn_bo, L0_xattn_ln_gamma, L0_xattn_ln_beta, L0_xattn_residual_scale)
    x = x + _L0_ffn_ref(_layernorm(x, axis=-1), L0_ffn_gate_weight, L0_ffn_w_gate, L0_ffn_w_up, L0_ffn_w_down)
    return x

_drawn_inputs = setup_inputs


def setup_inputs(seed=0):
    import zlib

    import numpy as np

    out = dict(_drawn_inputs(seed))
    spreads = {'L0_xattn_bq': (0.0, 0.288),
     'L0_xattn_bk': (0.0, 0.8),
     'L0_xattn_bv': (0.0, 0.1),
     'L0_xattn_bo': (0.0, 0.1),
     'L0_xattn_ln_gamma': (1.0, 0.2),
     'L0_xattn_ln_beta': (0.0, 0.1)}
    factors = {}
    for name, (base, spread) in spreads.items():
        noise = np.random.default_rng([zlib.crc32(name.encode()), seed]).standard_normal(out[name].shape)
        drawn = base * np.exp(spread * noise) if base else spread * noise
        out[name] = jnp.asarray(drawn.astype(out[name].dtype))
    for name, factor in factors.items():
        out[name] = (out[name] * factor).astype(out[name].dtype)
    return out
```

```python
from contextlib import ExitStack
import math

import numpy as np
import concourse.bass as bass
from concourse import mybir

F32, F32R = mybir.dt.float32, mybir.dt.float32r
I32, U32 = mybir.dt.int32, mybir.dt.uint32
ALU, ACT, AX = mybir.AluOpType, mybir.ActivationFunctionType, mybir.AxisListType

P = 128
HD = 64
HALF = 512
TOPK = 8
REGION = 4096
EPS = 1e-5
CLIP = 50.0
RES_SCALE_MAX = 0.3
BIG = 3.0e38


class Scope:

    def __init__(self, nc, stack, name):
        self.nc, self.stack, self.name, self.sems = nc, stack, name, []
        stack.callback(self.clear)

    def sb(self, name, shape, dt=F32):
        return self.stack.enter_context(self.nc.sbuf_tensor(f"{self.name}_{name}", shape, dt))

    def ps(self, name, shape, dt=F32):
        return self.stack.enter_context(self.nc.psum_tensor(f"{self.name}_ps_{name}", shape, dt))

    def sem(self, name):
        self.sems.append(self.nc.alloc_semaphore(f"{self.name}_{name}"))
        return self.sems[-1]

    def clear(self):
        self.nc.clear_and_free_semaphores(self.sems)
        self.nc.all_engine_barrier()


def f32(ap):
    return ap.bitcast(F32)


def row_broadcast(dram_row, n):
    return dram_row.broadcast_to([P, n])


def layernorm_pass(nc, x, xnT):
    T, H = x.shape
    C, NT = H // P, T // P
    with ExitStack() as st:
        s = Scope(nc, st, "ln")
        xin, xn = s.sb("xin", [P, 2, H]), s.sb("xn", [P, 2, H])
        stats, mv = s.sb("stats", [P, 2, H // HALF, 6]), s.sb("mv", [P, 2, 2])
        std, rstd = s.sb("std", [P, 2, 1]), s.sb("rstd", [P, 2, 1])
        ident, eps = s.sb("ident", [P, P]), s.sb("eps", [P, 1])
        xT = s.sb("xT", [P, 2, C, P])
        tps = s.ps("tps", [P, 2, C, P])
        x_in = [s.sem("x_in0"), s.sem("x_in1")]
        stored = [s.sem("stored0"), s.sem("stored1")]
        zeroed, consts, eps_done, dve_passed = s.sem("zeroed"), s.sem("consts"), s.sem("eps_done"), s.sem("dve_passed")
        stats_done, mv_done, std_done, rstd_done = s.sem("stats_done"), s.sem("mv_done"), s.sem("std_done"), s.sem("rstd_done")
        xn_done, t_done, xT_done = s.sem("xn_done"), s.sem("t_done"), s.sem("xT_done")
        SB = H // HALF
        out = xnT.rearrange("(c p) t -> p c t", p=P)
        with nc.Block() as block:
            @block.sync
            def _(sp):
                with sp.Fori(0, NT // 2) as i:
                    for b in range(2):
                        sp.wait_ge(xn_done, 2 * i)
                        sp.dma_start(xin[:, b], x[bass.ds((2 * i + b) * P, P), :]).then_inc(x_in[b], 16)

            @block.gpsimd
            def _(pool):
                nc.gpsimd.memset(ident[:], 0.0).then_inc(zeroed, 1)
                pool.wait_ge(zeroed, 1)
                nc.gpsimd.affine_select(out=ident[:], in_=ident[:], compare_op=ALU.not_equal, fill=1.0, base=0,
                                        pattern=[[-1, P]], channel_multiplier=1).then_inc(consts, 1)
                with pool.Fori(0, NT // 2) as i:
                    for b in range(2):
                        pool.wait_ge(xT_done, 2 * i + b + 1)
                        pool.dma_start(out[:, :, bass.ds((2 * i + b) * P, P)], xT[:, b]).then_inc(stored[b], 16)
                for b in range(2):
                    pool.wait_ge(stored[b], 16 * (NT // 2))

            @block.vector
            def _(dve):
                nc.vector.memset(eps[:], EPS).then_inc(eps_done, 1)
                dve.wait_ge(eps_done, 1)
                with dve.Fori(0, NT // 2) as i:
                    for b in range(2):
                        t = 2 * i + b
                        dve.wait_ge(x_in[b], 16 * (i + 1))
                        for k in range(SB):
                            nc.vector.bn_stats(stats[:, b, k], xin[:, b, k * HALF:(k + 1) * HALF]).then_inc(stats_done, 1)
                        dve.wait_ge(stats_done, SB * (t + 1))
                        dve.sem_inc(dve_passed, 1)
                        nc.vector.bn_aggr(mv[:, b], stats[:, b]).then_inc(mv_done, 1)
                        dve.wait_ge(std_done, t + 1)
                        nc.vector.reciprocal(rstd[:, b], std[:, b]).then_inc(rstd_done, 1)
                        dve.wait_ge(rstd_done, t + 1)
                        if b == 0:
                            dve.wait_ge(t_done, 2 * i)
                        nc.vector.tensor_scalar(xn[:, b], xin[:, b], mv[:, b, 0:1], rstd[:, b],
                                                ALU.subtract, ALU.mult).then_inc(xn_done, 1)

            @block.scalar
            def _(act):
                act.wait_ge(eps_done, 1)
                with act.Fori(0, NT // 2) as i:
                    for b in range(2):
                        t = 2 * i + b
                        act.wait_ge(mv_done, t + 1)
                        nc.scalar.activation(std[:, b], mv[:, b, 1:2], ACT.Sqrt, bias=eps[:]).then_inc(std_done, 1)
                        act.wait_ge(t_done, t + 1)
                        act.wait_ge(stored[b], 16 * i)
                        nc.scalar.copy(xT[:, b], tps[:, b]).then_inc(xT_done, 1)

            @block.tensor
            def _(pe):
                pe.wait_ge(consts, 1)
                with pe.Fori(0, NT // 2) as i:
                    for b in range(2):
                        t = 2 * i + b
                        pe.wait_ge(xn_done, t + 1)
                        if b == 0:
                            pe.wait_ge(xT_done, 2 * i)
                        for c in range(C):
                            last = nc.tensor.transpose(tps[:, b, c], xn[:, b, c * P:(c + 1) * P], ident[:])
                        last.then_inc(t_done, 1)


def projection_pass(nc, kind, actT, wT, bias, out):
    H, T = actT.shape
    C = H // P
    NB = T // HALF
    G = C if kind != "v" else (HALF // P) * (H // HALF)
    BANKS = 4
    S = out.shape[-1] if kind != "v" else None
    NH = H // HD
    with ExitStack() as st:
        s = Scope(nc, st, "proj_" + kind)
        w_raw = s.sb("w_raw", [P, 4, H])
        w_hi, w_lo = s.sb("w_hi", [P, C, H], F32R), s.sb("w_lo", [P, C, H], F32R)
        a_raw = s.sb("a_raw", [P, 2, C, HALF])
        a_hi, a_lo = s.sb("a_hi", [P, 2, C, HALF], F32R), s.sb("a_lo", [P, 2, C, HALF], F32R)
        if kind == "v":
            bias_sb, v32 = s.sb("bias", [P, H]), s.sb("v32", [P, 2, HALF])
            o = s.sb("o", [P, 2, HALF // HD, 2, HD], F32R)
        else:
            bias_sb = s.sb("bias", [P, C])
            o_hi, o_lo = s.sb("o_hi", [P, 2, HALF], F32R), s.sb("o_lo", [P, 2, HALF], F32R)
        acc = s.ps("acc", [P, BANKS, HALF])
        w_in = [s.sem(f"w_in{i}") for i in range(4)]
        a_in = [s.sem(f"a_in{i}") for i in range(2)]
        bias_in, bank_free = s.sem("bias_in"), s.sem("bank_free")
        w_hi_done, w_lo_done = s.sem("w_hi_done"), s.sem("w_lo_done")
        a_hi_done, a_lo_done = s.sem("a_hi_done"), s.sem("a_lo_done")
        product_done, v32_done, o_hi_done, o_lo_done = s.sem("product_done"), s.sem("v32_done"), s.sem("o_hi_done"), s.sem("o_lo_done")
        stored = [s.sem(f"stored{i}") for i in range(2)]
        STORES = 1 if kind == "v" else 4
        act_v = actT.rearrange("(c p) t -> p c t", p=P)

        with nc.Block() as block:
            @block.gpsimd
            def _(pool):
                if kind == "v":
                    pool.dma_start(bias_sb[:], row_broadcast(bias, H)).then_inc(bias_in, 16)
                else:
                    pool.dma_start(bias_sb[:], bias).then_inc(bias_in, 16)
                with pool.Fori(0, NB // 2) as i:
                    for b in range(2):
                        pool.wait_ge(a_lo_done, 2 * i)
                        pool.dma_start(a_raw[:, b], act_v[:, :, bass.ds((2 * i + b) * HALF, HALF)]).then_inc(a_in[b], 16)

            @block.sync
            def _(sp):
                for c in range(C):
                    if c >= 4:
                        sp.wait_ge(w_lo_done, c - 3)
                    sp.dma_start(w_raw[:, c % 4], wT[c * P:(c + 1) * P, :]).then_inc(w_in[c % 4], 16)
                with sp.Fori(0, NB // 2) as i:
                    for b in range(2):
                        for g in range(G):
                            sp.wait_ge(o_lo_done, (2 * i + b) * G + g + 1)
                            q = g % 2
                            if kind == "v":
                                row = (2 * i + b) * HALF + (g // (H // HALF)) * P
                                h0 = (g % (H // HALF)) * (HALF // HD)
                                sp.dma_start(out[bass.ds(row, P), h0:h0 + HALF // HD, :],
                                             f32(o[:, q]).rearrange("p h two d -> p h (two d)")).then_inc(stored[q], 16)
                                continue
                            if S == 2 * HALF:
                                bh, t0 = i * NH + 2 * g, b * HALF
                            else:
                                bh, t0 = (2 * i + b) * NH + 2 * g, 0
                            for hh in range(2):
                                for k, tile in enumerate((o_hi, o_lo)):
                                    if kind == "k":
                                        dst = out[bass.ds(bh + hh, 1), k * HD:(k + 1) * HD, t0:t0 + HALF]
                                        dst = dst.rearrange("o d t -> (o d) t")
                                    else:
                                        dst = out[bass.ds(bh + hh, 1), k, :, t0:t0 + HALF].rearrange("o d t -> (o d) t")
                                    sp.dma_start(dst, f32(tile[hh * HD:(hh + 1) * HD, q])).then_inc(stored[q], 16)
                for q in range(2):
                    sp.wait_ge(stored[q], 16 * STORES * NB * G // 2)

            @block.scalar
            def _(act):
                def split(t, b, n):
                    act.wait_ge(a_in[b], 16 * (n + 1))
                    if not (isinstance(t, int) and t < 2):
                        act.wait_ge(product_done, (t - 1) * G)
                    nc.scalar.copy(a_hi[:, b], a_raw[:, b]).then_inc(a_hi_done, 1)

                def evacuate(t, b):
                    for g in range(G):
                        n, q = t * G + g, g % 2
                        act.wait_ge(stored[q], 16 * STORES * (t * (G // 2) + g // 2))
                        if kind == "v":
                            act.wait_ge(v32_done, n + 1)
                            nc.scalar.copy(o[:, q, :, 0], v32[:, q].rearrange("p (h d) -> p h d", d=HD)).then_inc(o_hi_done, 1)
                        else:
                            act.wait_ge(product_done, n + 1)
                            nc.scalar.activation(o_hi[:, q], acc[:, g % BANKS], ACT.Identity,
                                                 bias=bias_sb[:, g:g + 1]).then_inc(o_hi_done, 1)

                for c in range(C):
                    act.wait_ge(w_in[c % 4], 16 * (c // 4 + 1))
                    nc.scalar.copy(w_hi[:, c], w_raw[:, c % 4]).then_inc(w_hi_done, 1)
                    if c == 1:
                        split(0, 0, 0)
                act.wait_ge(bias_in, 16)
                with act.Fori(0, NB // 2 - 1) as i:
                    split(2 * i + 1, 1, i)
                    evacuate(2 * i, 0)
                    split(2 * i + 2, 0, i + 1)
                    evacuate(2 * i + 1, 1)
                split(NB - 1, 1, NB // 2 - 1)
                evacuate(NB - 2, 0)
                evacuate(NB - 1, 1)

            @block.vector
            def _(dve):
                def split(t, b):
                    dve.wait_ge(a_hi_done, t + 1)
                    nc.vector.tensor_tensor(a_lo[:, b], a_raw[:, b], f32(a_hi[:, b]), ALU.subtract).then_inc(a_lo_done, 1)

                def evacuate(t, b):
                    for g in range(G):
                        n, q = t * G + g, g % 2
                        if kind == "v":
                            half = g % (H // HALF)
                            dve.wait_ge(product_done, n + 1)
                            nc.vector.tensor_tensor(v32[:, q], acc[:, g % BANKS],
                                                    bias_sb[:, half * HALF:(half + 1) * HALF], ALU.add).then_inc(v32_done, 1)
                            dve.wait_ge(o_hi_done, n + 1)
                            nc.vector.tensor_tensor(o[:, q, :, 1], v32[:, q].rearrange("p (h d) -> p h d", d=HD),
                                                    f32(o[:, q, :, 0]), ALU.subtract).then_inc(o_lo_done, 1)
                        else:
                            dve.wait_ge(o_hi_done, n + 1)
                            nc.vector.scalar_tensor_tensor(
                                out=o_lo[:, q], in0=acc[:, g % BANKS], scalar=bias_sb[:, g:g + 1], in1=f32(o_hi[:, q]),
                                op0=ALU.add, op1=ALU.subtract).then_inc(o_lo_done, 1)

                for c in range(C):
                    dve.wait_ge(w_hi_done, c + 1)
                    nc.vector.tensor_tensor(w_lo[:, c], w_raw[:, c % 4], f32(w_hi[:, c]), ALU.subtract).then_inc(w_lo_done, 1)
                    if c == 1:
                        split(0, 0)
                dve.wait_ge(bias_in, 16)
                with dve.Fori(0, NB // 2 - 1) as i:
                    split(2 * i + 1, 1)
                    evacuate(2 * i, 0)
                    split(2 * i + 2, 0)
                    evacuate(2 * i + 1, 1)
                split(NB - 1, 1)
                evacuate(NB - 2, 0)
                evacuate(NB - 1, 1)

            @block.tensor
            def _(pe):
                def tiles(t, b, first):
                    pe.wait_ge(a_lo_done, t + 1)
                    for g in range(G):
                        if not first or g >= BANKS:
                            pe.wait_ge(o_lo_done, t * G + g - BANKS + 1)
                        for c in range(C):
                            if first and g == 0:
                                pe.wait_ge(w_lo_done, c + 1)
                            if kind == "v":
                                r, half = g // (H // HALF), g % (H // HALF)
                                hi, lo = (a[:, b, c, r * P:(r + 1) * P] for a in (a_hi, a_lo))
                                mhi, mlo = (w[:, c, half * HALF:(half + 1) * HALF] for w in (w_hi, w_lo))
                            else:
                                hi, lo = (w[:, c, g * P:(g + 1) * P] for w in (w_hi, w_lo))
                                mhi, mlo = a_hi[:, b, c], a_lo[:, b, c]
                            o_ = acc[:, g % BANKS]
                            nc.tensor.matmul(o_, hi, mhi, start=(c == 0), stop=False)
                            nc.tensor.matmul(o_, hi, mlo, start=False, stop=False)
                            last = nc.tensor.matmul(o_, lo, mhi, start=False, stop=(c == C - 1))
                        last.then_inc(product_done, 1)

                tiles(0, 0, True)
                tiles(1, 1, False)
                with pe.Fori(1, NB // 2) as i:
                    tiles(2 * i, 0, False)
                    tiles(2 * i + 1, 1, False)


def attention_pass(nc, kst, qst, vst, mask, ctxst, sums, B, S):
    NHB = kst.shape[0]
    NH, C, HV = NHB // B, S // P, S // HALF
    NPAIR = NHB // 2
    with ExitStack() as st:
        s = Scope(nc, st, "att")
        kt = s.sb("kt", [P, 2, S], F32R)
        qh, ql = s.sb("qh", [P, 2, S], F32R), s.sb("ql", [P, 2, S], F32R)
        v = s.sb("v", [P, 2, C, 4 * HD], F32R)
        e32, p32 = s.sb("e32", [P, 2, S]), s.sb("p32", [P, 2, S])
        p_hi, p_lo = s.sb("p_hi", [P, 2, S], F32R), s.sb("p_lo", [P, 2, S], F32R)
        c32 = s.sb("c32", [P, 2, S])
        m_int, m32, upper = s.sb("m_int", [P, B, C], I32), s.sb("m32", [P, B, C]), s.sb("upper", [P, B, C])
        sc = s.ps("sc", [P, 2, S])
        o = s.ps("o", [P, 2, S])
        kq_in = [s.sem(f"kq_in{i}") for i in range(2)]
        v_in = [s.sem(f"v_in{i}") for i in range(2)]
        mask_in, m_done, upper_ready, const_ready = s.sem("mask_in"), s.sem("m_done"), s.sem("upper_ready"), s.sem("const_ready")
        scores_done, exp_done, clip_done, hi_done, lo_done = s.sem("scores_done"), s.sem("exp_done"), s.sem("clip_done"), s.sem("hi_done"), s.sem("lo_done")
        values_done, c_done = s.sem("values_done"), s.sem("c_done")
        stored = [s.sem(f"stored{i}") for i in range(2)]
        U = 2 * C
        vst_v = vst.rearrange("(b c p) h d -> b p c h d", b=B, p=P)

        def stationary(b, c, k):
            return v[:, b, c, 2 * k * HD:2 * (k + 1) * HD]

        with nc.Block() as block:
            @block.sync
            def _(sp):
                sp.dma_start(m_int[:], mask).then_inc(mask_in, 16)

                def load(i, bt):
                    for b in range(2):
                        bh = bt * NH + 2 * i + b
                        if not (isinstance(bh, int) and bh < 2):
                            sp.wait_ge(values_done, (bh - 1) * C)
                        sp.dma_start(f32(kt[:, b]), kst[bass.ds(bh, 1)].rearrange("o p t -> (o p) t")).then_inc(kq_in[b], 16)
                        for k, q in enumerate((qh, ql)):
                            for r in range(2):
                                sp.dma_start(f32(q[r * HD:(r + 1) * HD, b]),
                                             qst[bass.ds(bh, 1), k].rearrange("o p t -> (o p) t")).then_inc(kq_in[b], 16)
                        for k in range(2):
                            src = vst_v[bt, :, :, bass.ds(2 * i + b, 1), k * HD:(k + 1) * HD]
                            sp.dma_start(f32(v[:, b, :, (2 * k + b) * HD:(2 * k + b + 1) * HD]),
                                         src.rearrange("p c o d -> p c (o d)")).then_inc(v_in[b], 16)

                load(0, 0)
                for bt in range(B):
                    with sp.Fori(0 if bt else 1, NH // 2) as i:
                        load(i, bt)

            @block.gpsimd
            def _(pool):
                for bt in range(B):
                    with pool.Fori(0, NH // 2) as i:
                        for b in range(2):
                            head = bt * NH + 2 * i + b
                            pool.wait_ge(c_done, head + 1)
                            pool.dma_start(ctxst[bass.ds((2 * i + b) * HD, HD), bt * S:(bt + 1) * S],
                                           c32[b * HD:(b + 1) * HD, b]).then_inc(stored[b], 16)
                            other = (1 - b) * HD
                            pool.dma_start(sums[bass.ds(2 * i + b, 1), bt * S:(bt + 1) * S], c32[other:other + 1, b]).then_inc(stored[b], 16)
                for b in range(2):
                    pool.wait_ge(stored[b], 32 * NPAIR)

            def pairs(eng, body):
                n = NH // 2
                body(0, 0, 0, True)
                for bt in range(B):
                    first = 0 if bt else 1
                    if n - 1 > first:
                        with eng.Fori(first, n - 1) as i:
                            body(bt * n + i, bt, bt, False)
                    body(bt * n + n - 1, bt, bt + 1 if bt < B - 1 else None, False)

            @block.tensor
            def _(pe):
                def scores(pair, u):
                    b, c = (u % U) // C, u % C
                    if c == 0:
                        pe.wait_ge(kq_in[b], 5 * 16 * (pair + 1))
                    n = pair * U + u
                    if not (isinstance(n, int) and n < 2):
                        pe.wait_ge(exp_done, n - 1)
                    for h in range(HV):
                        cols = slice(h * HALF, (h + 1) * HALF)
                        nc.tensor.matmul(sc[:, u % 2, cols], kt[:, b, c * P:(c + 1) * P], qh[:, b, cols], start=True, stop=False)
                        last = nc.tensor.matmul(sc[:, u % 2, cols], kt[:, b, c * P:(c + 1) * P], ql[:, b, cols], start=False, stop=True)
                    last.then_inc(scores_done, 1)

                def values(pair, u, first):
                    b, c = u // C, u % C
                    if c == 0:
                        pe.wait_ge(v_in[b], 32 * (pair + 1))
                        if not first:
                            pe.wait_ge(c_done, 2 * pair + b - 1)
                    pe.wait_ge(lo_done, pair * U + u + 1)
                    for h in range(HV):
                        cols = slice(h * HALF, (h + 1) * HALF)
                        nc.tensor.matmul(o[:, b, cols], stationary(b, c, 0), p_hi[:, u % 2, cols], start=(c == 0), stop=False)
                        nc.tensor.matmul(o[:, b, cols], stationary(b, c, 0), p_lo[:, u % 2, cols], start=False, stop=False)
                        last = nc.tensor.matmul(o[:, b, cols], stationary(b, c, 1), p_hi[:, u % 2, cols], start=False, stop=(c == C - 1))
                    last.then_inc(values_done, 1)

                pe.wait_ge(const_ready, 1)
                scores(0, 0)
                scores(0, 1)

                def body(pair, bt, next_bt, first):
                    for u in range(U):
                        if u + 2 < U:
                            scores(pair, u + 2)
                        elif next_bt is not None:
                            scores(pair + 1, u + 2 - U)
                        values(pair, u, first)
                pairs(pe, body)

            @block.scalar
            def _(act):
                def exponential(n, u):
                    act.wait_ge(scores_done, n + 1)
                    if not (isinstance(n, int) and n < 2):
                        act.wait_ge(clip_done, n - 1)
                    nc.scalar.activation(e32[:, u % 2], sc[:, u % 2], ACT.Exp, scale=1.0 / math.sqrt(HD)).then_inc(exp_done, 1)

                def high(n, u):
                    act.wait_ge(clip_done, n + 1)
                    if not (isinstance(n, int) and n < 2):
                        act.wait_ge(values_done, n - 1)
                    nc.scalar.copy(p_hi[:, u % 2], p32[:, u % 2]).then_inc(hi_done, 1)

                exponential(0, 0)

                def body(pair, bt, next_bt, first):
                    for u in range(U):
                        n = pair * U + u
                        if u < U - 1 or next_bt is not None:
                            exponential(n + 1, u + 1)
                        high(n, u)
                pairs(act, body)

            @block.vector
            def _(dve):
                def clip(n, u, bt):
                    dve.wait_ge(exp_done, n + 1)
                    if not (isinstance(n, int) and n < 2):
                        dve.wait_ge(lo_done, n - 1)
                    nc.vector.tensor_scalar(p32[:, u % 2], e32[:, u % 2], math.exp(-CLIP), upper[:, bt, u % C:u % C + 1],
                                            ALU.max, ALU.min).then_inc(clip_done, 1)

                def low(n, u):
                    dve.wait_ge(hi_done, n + 1)
                    nc.vector.tensor_tensor(p_lo[:, u % 2], p32[:, u % 2], f32(p_hi[:, u % 2]), ALU.subtract).then_inc(lo_done, 1)

                def context(pair, b):
                    dve.wait_ge(values_done, (2 * pair + b + 1) * C)
                    dve.wait_ge(stored[b], 32 * pair)
                    nc.vector.tensor_copy(c32[:, b], o[:, b]).then_inc(c_done, 1)

                for b in range(2):
                    z = (1 - b) * HD
                    nc.vector.memset(f32(v[:, b, :, z:z + HD]), float(np.float32(1.0 + 1e-8)))
                    last = nc.vector.memset(f32(v[:, b, :, z + 2 * HD:z + 3 * HD]), 0.0)
                last.then_inc(const_ready, 1)
                dve.wait_ge(mask_in, 16)
                nc.vector.tensor_copy(m32[:], m_int[:]).then_inc(m_done, 1)
                dve.wait_ge(m_done, 1)
                nc.vector.tensor_scalar(m32[:], m32[:], 0.5, math.exp(CLIP), ALU.is_gt, ALU.mult).then_inc(m_done, 1)
                dve.wait_ge(m_done, 2)
                nc.vector.tensor_scalar(upper[:], m32[:], math.exp(-CLIP), None, ALU.max).then_inc(upper_ready, 1)
                dve.wait_ge(upper_ready, 1)
                clip(0, 0, 0)

                def body(pair, bt, next_bt, first):
                    for u in range(U):
                        n = pair * U + u
                        if u + 1 < U:
                            clip(n + 1, u + 1, bt)
                        elif next_bt is not None:
                            clip(n + 1, 0, next_bt)
                        low(n, u)
                        if u == 2 and not first:
                            context(pair - 1, 1)
                        if u == C + 2:
                            context(pair, 0)

                pairs(dve, body)
                context(NPAIR - 1, 1)


def reciprocal_pass(nc, sums, rsums):
    with ExitStack() as st:
        s = Scope(nc, st, "rec")
        n = sums.shape[0] * sums.shape[1] // P
        t, r = s.sb("t", [P, n]), s.sb("r", [P, n])
        loaded, inverted, stored = s.sem("loaded"), s.sem("inverted"), s.sem("stored")
        src = sums.rearrange("h (k n) -> (h k) n", n=n)
        dst = rsums.rearrange("h (k n) -> (h k) n", n=n)
        with nc.Block() as block:
            @block.sync
            def _(sp):
                sp.dma_start(t[:], src).then_inc(loaded, 16)
                sp.wait_ge(inverted, 1)
                sp.dma_start(dst, r[:]).then_inc(stored, 16)
                sp.wait_ge(stored, 16)

            @block.vector
            def _(dve):
                dve.wait_ge(loaded, 16)
                nc.vector.reciprocal(r[:], t[:]).then_inc(inverted, 1)


def directory(E):
    n_at, base_at, last_at, row_at = 0, E, 2 * E, 2 * E + 1
    return n_at, base_at, last_at, row_at


def table_regions(E):
    return E + 4


def output_pass(nc, ctxst, rsums, woT, bo, gamma, beta, rscale, x, gateT, acc, h2st, table, dirst):
    H, T = ctxst.shape
    C, NT, E, HV = H // P, T // P, gateT.shape[1], H // HALF
    NCOL = 3
    n_at, base_at, last_at, row_at = directory(E)
    with ExitStack() as st:
        s = Scope(nc, st, "out")
        w_raw = s.sb("w_raw", [P, 4, H])
        w_hi, w_lo = s.sb("w_hi", [P, C, H], F32R), s.sb("w_lo", [P, C, H], F32R)
        c_raw, r_t, cn = s.sb("c_raw", [P, 2, C, P]), s.sb("r_t", [P, 2, C, P]), s.sb("cn", [P, 2, C, P])
        c_hi, c_lo = s.sb("c_hi", [P, 2, C, P], F32R), s.sb("c_lo", [P, 2, C, P], F32R)
        x_t, d, x1, h2 = s.sb("x_t", [P, 2, H]), s.sb("d", [P, 2, H]), s.sb("x1", [P, 2, H]), s.sb("h2", [P, 2, H])
        scaled, normed, h2T = s.sb("scaled", [P, H]), s.sb("normed", [P, H]), s.sb("h2T", [P, C, P])
        gamma_sb, beta_sb, gate_sb = s.sb("gamma", [P, H]), s.sb("beta", [P, H]), s.sb("gate", [P, C, E])
        bo_row = s.sb("bo_row", [1, H])
        bo_hi, bo_lo = s.sb("bo_hi", [1, H], F32R), s.sb("bo_lo", [1, H], F32R)
        rs_raw, rs_sb, eps = s.sb("rs_raw", [P, 1]), s.sb("rs", [P, 1]), s.sb("eps", [P, 1])
        ident, ones, before = s.sb("ident", [P, P]), s.sb("ones", [P, P]), s.sb("before", [P, P])
        ones_row = s.sb("ones_row", [1, P], F32R)
        stats, mv, std, rstd = s.sb("stats", [P, 2, HV, 6]), s.sb("mv", [P, 2, 2]), s.sb("std", [P, 2, 1]), s.sb("rstd", [P, 2, 1])
        logits, top, top_i, top_f, diff = s.sb("logits", [P, E]), s.sb("top", [P, TOPK]), s.sb("top_i", [P, TOPK], U32), s.sb("top_f", [P, TOPK]), s.sb("diff", [P, TOPK])
        e8, esum, rsum, iota_e, rowbase = s.sb("e8", [P, TOPK]), s.sb("esum", [P, 1]), s.sb("rsum", [P, 1]), s.sb("iota_e", [P, E]), s.sb("rowbase", [P, E])
        onehot, prod = s.sb("onehot", [P, 2, TOPK, E]), s.sb("prod", [P, TOPK, E])
        mask, seen = s.sb("mask", [P, 2, E]), s.sb("seen", [P, 2, E])
        token, slot_f, slot = s.sb("token", [P, 1]), s.sb("slot_f", [P, TOPK]), s.sb("slot", [P, 2, TOPK], I32)
        row_e, record = s.sb("row_e", [P, E]), s.sb("record", [P, 2, TOPK, 2])
        fill, zeros = s.sb("fill", [P, P, 2]), s.sb("zeros", [P, H])
        tile_id, cmp, started = s.sb("tile_id", [P, NCOL]), s.sb("cmp", [P, NCOL, E]), s.sb("started", [P, NCOL])
        first_of, row_f, row_i = s.sb("first_of", [P, NCOL]), s.sb("row_f", [P, NCOL]), s.sb("row_i", [P, NCOL], I32)
        cnt, tiles_i, tiles_f, upto, base = s.sb("cnt", [P, E]), s.sb("tiles_i", [P, E], I32), s.sb("tiles_f", [P, E]), s.sb("upto", [P, E]), s.sb("base", [P, E])
        dir_sb = s.sb("dir", [1, row_at + 1], I32)
        o = s.ps("o", [P, 2, H])
        tps, lps, pps = s.ps("tps", [P, C, P]), s.ps("lps", [P, HALF]), s.ps("pps", [P, HALF])

        w_in = [s.sem(f"w_in{i}") for i in range(4)]
        c_in, x_in = [s.sem(f"c_in{i}") for i in range(2)], [s.sem(f"x_in{i}") for i in range(2)]
        consts_in, set_up, filled = s.sem("consts_in"), s.sem("set_up"), s.sem("filled")
        masks_ready, rs_ready, bo_ready, fill_ready = s.sem("masks_ready"), s.sem("rs_ready"), s.sem("bo_ready"), s.sem("fill_ready")
        w_hi_done, w_lo_done = s.sem("w_hi_done"), s.sem("w_lo_done")
        cn_done, c_hi_done, c_lo_done, gemm_done, d_done = s.sem("cn_done"), s.sem("c_hi_done"), s.sem("c_lo_done"), s.sem("gemm_done"), s.sem("d_done")
        norm_step, mv_ready, std_ready, x1_done, h2_done = s.sem("norm_step"), s.sem("mv_ready"), s.sem("std_ready"), s.sem("x1_done"), s.sem("h2_done")
        t_done, h2T_done, logits_done, diff_done, e8_done = s.sem("t_done"), s.sem("h2T_done"), s.sem("logits_done"), s.sem("diff_done"), s.sem("e8_done")
        route_step, mask_done, record_done, pos_done, slot_step, slot_done = s.sem("route_step"), s.sem("mask_done"), s.sem("record_done"), s.sem("pos_done"), s.sem("slot_step"), s.sem("slot_done")
        stored, scattered = [s.sem(f"stored{i}") for i in range(2)], [s.sem(f"scattered{i}") for i in range(2)]
        pool_passed, dve_passed = s.sem("pool_passed"), s.sem("dve_passed")
        seen_ready, seen_done = s.sem("seen_ready"), s.sem("seen_done")
        count_done, dir_step, dir_done, dir_stored = s.sem("count_done"), s.sem("dir_step"), s.sem("dir_done"), s.sem("dir_stored")

        ctx_v = ctxst.rearrange("(c p) t -> p c t", p=P)
        r_v = rsums.rearrange("(c k) t -> k c t", k=2)
        REGIONS = table_regions(E)
        FILLS = REGIONS * REGION // (P * P)
        CONSTS = 5

        def known(v):
            return isinstance(v, int)

        def tiles(eng, body):
            body(0, 0, True, True, False, False)
            body(1, 1, True, True, True, False)
            with eng.Fori(1, NT // 2 - 1) as h:
                body(2 * h, 0, True, True, True, True)
                body(2 * h + 1, 1, True, True, True, True)
            body(NT - 2, 0, True, True, True, True)
            body(NT - 1, 1, True, False, True, True)
            body(NT, 0, False, False, True, True)
            body(NT + 1, 1, False, False, False, True)

        with nc.Block() as block:
            @block.sync
            def _(sp):
                def load_context(i, b):
                    sp.dma_start(c_raw[:, b], ctx_v[:, :, bass.ds(i * P, P)]).then_inc(c_in[b], 16)
                    for k in range(2):
                        src = r_v[k, :, bass.ds(i * P, P)].partition_broadcast(HD)
                        sp.dma_start(r_t[k * HD:(k + 1) * HD, b], src).then_inc(c_in[b], 16)

                def load_x(i, b):
                    sp.dma_start(x_t[:, b], x[bass.ds(i * P, P), :]).then_inc(x_in[b], 16)

                for b in range(2):
                    load_context(b, b)
                    load_x(b, b)
                for c in range(C):
                    if c >= 4:
                        sp.wait_ge(w_lo_done, c - 3)
                    sp.dma_start(w_raw[:, c % 4], woT[c * P:(c + 1) * P, :]).then_inc(w_in[c % 4], 16)

                def body(i, b, more):
                    if more:
                        sp.wait_ge(cn_done, i + 1)
                        load_context(i + 2, b)
                    sp.wait_ge(x1_done, i + 1)
                    if more:
                        load_x(i + 2, b)
                    sp.dma_start(acc[bass.ds(i * P, P), :], x1[:, b]).then_inc(stored[b], 16)
                    sp.wait_ge(h2_done, i + 1)
                    sp.dma_start(h2st[bass.ds(i * P, P), :], h2[:, b]).then_inc(stored[b], 16)

                with sp.Fori(0, NT // 2 - 1) as h:
                    body(2 * h, 0, True)
                    body(2 * h + 1, 1, True)
                body(NT - 2, 0, False)
                body(NT - 1, 1, False)
                for b in range(2):
                    sp.wait_ge(stored[b], 32 * (NT // 2))
                sp.wait_ge(dir_done, 1)
                sp.dma_start(dirst[0:1, 0:row_at + 1], dir_sb[:]).then_inc(dir_stored, 16)
                for k in range(NCOL):
                    at = row_at + 1 + k * P
                    sp.dma_start(dirst[0:1, at:at + P].rearrange("o (p q) -> (o p) q", q=1), row_i[:, k:k + 1]).then_inc(dir_stored, 16)
                sp.wait_ge(dir_stored, 16 * (NCOL + 1))

            @block.gpsimd
            def _(pool):
                nc.gpsimd.memset(ident[:], 0.0).then_inc(set_up, 1)
                nc.gpsimd.memset(before[:], 1.0).then_inc(set_up, 1)
                nc.gpsimd.memset(ones[:], 1.0).then_inc(masks_ready, 1)
                nc.gpsimd.memset(f32(ones_row[:]), 1.0).then_inc(masks_ready, 1)
                nc.gpsimd.memset(fill[:], 0.0).then_inc(set_up, 1)
                nc.gpsimd.memset(zeros[:], 0.0).then_inc(fill_ready, 1)
                pool.wait_ge(set_up, 3)
                nc.gpsimd.affine_select(out=ident[:], in_=ident[:], compare_op=ALU.not_equal, fill=1.0, base=0,
                                        pattern=[[-1, P]], channel_multiplier=1).then_inc(masks_ready, 1)
                nc.gpsimd.affine_select(out=before[:], in_=before[:], compare_op=ALU.is_gt, fill=0.0, base=0,
                                        pattern=[[1, P]], channel_multiplier=-1).then_inc(masks_ready, 1)
                nc.gpsimd.iota(iota_e[:], pattern=[[1, E]], base=0, channel_multiplier=0,
                               allow_small_or_imprecise_dtypes=True).then_inc(masks_ready, 1)
                nc.gpsimd.iota(token[:], pattern=[[0, 1]], base=0, channel_multiplier=1,
                               allow_small_or_imprecise_dtypes=True).then_inc(masks_ready, 1)
                nc.gpsimd.iota(tile_id[:], pattern=[[P, NCOL]], base=0, channel_multiplier=1,
                               allow_small_or_imprecise_dtypes=True).then_inc(masks_ready, 1)
                nc.gpsimd.iota(fill[:].bitcast(I32)[:, :, 0], pattern=[[1, P]], base=T, channel_multiplier=0).then_inc(fill_ready, 1)
                for dst, src in ((gamma_sb, row_broadcast(gamma, H)), (beta_sb, row_broadcast(beta, H)),
                                 (gate_sb, gateT.rearrange("(c p) e -> p c e", p=P)), (bo_row, bo),
                                 (rs_raw, rscale.broadcast_to([P, 1]))):
                    pool.dma_start(dst[:], src).then_inc(consts_in, 16)
                pool.wait_ge(fill_ready, 2)
                for k in range(FILLS):
                    rows = table[k * P * P:(k + 1) * P * P, :].rearrange("(p r) w -> p (r w)", p=P)
                    pool.dma_start(rows, fill[:].rearrange("p r w -> p (r w)")).then_inc(filled, 16)
                for dst in (acc, h2st):
                    pool.dma_start(dst[T:T + P, :], zeros[:]).then_inc(filled, 16)
                pool.wait_ge(filled, 16 * (FILLS + 2))

                def scatter(j, b):
                    pool.wait_ge(slot_done, j + 1)
                    pool.sem_inc(pool_passed, 1)
                    for k in range(TOPK):
                        nc.gpsimd.indirect_dma_start(
                            out=table[:, :], out_offset=bass.IndirectOffsetOnAxis(ap=slot[:, b, k:k + 1], axis=0),
                            in_=record[:, b, k, :], in_offset=None).then_inc(scattered[b], 16)

                with pool.Fori(0, NT // 2) as h:
                    scatter(2 * h, 0)
                    scatter(2 * h + 1, 1)
                for b in range(2):
                    pool.wait_ge(scattered[b], 16 * TOPK * (NT // 2))

            @block.tensor
            def _(pe):
                pe.wait_ge(masks_ready, 7)
                pe.wait_ge(bo_ready, 2)
                pe.wait_ge(consts_in, 16 * CONSTS)

                def product(i, b, first):
                    pe.wait_ge(c_lo_done, i + 1)
                    if not (known(i) and i < 2):
                        pe.wait_ge(d_done, i - 1)
                    for h in range(HV):
                        cols = slice(h * HALF, (h + 1) * HALF)
                        for c in range(C):
                            if first and h == 0:
                                pe.wait_ge(w_lo_done, c + 1)
                            nc.tensor.matmul(o[:, b, cols], c_hi[:, b, c], w_hi[:, c, cols], start=(c == 0), stop=False)
                            nc.tensor.matmul(o[:, b, cols], c_hi[:, b, c], w_lo[:, c, cols], start=False, stop=False)
                            nc.tensor.matmul(o[:, b, cols], c_lo[:, b, c], w_hi[:, c, cols], start=False, stop=False)
                        nc.tensor.matmul(o[:, b, cols], ones_row[:], bo_hi[:, cols], start=False, stop=False)
                        last = nc.tensor.matmul(o[:, b, cols], ones_row[:], bo_lo[:, cols], start=False, stop=True)
                    last.then_inc(gemm_done, 1)

                def route(j, b):
                    pe.wait_ge(h2_done, j + 1)
                    for c in range(C):
                        last = nc.tensor.transpose(tps[:, c], h2[:, b, c * P:(c + 1) * P], ident[:])
                    last.then_inc(t_done, 1)
                    pe.wait_ge(h2T_done, j + 1)
                    for c in range(C):
                        last = nc.tensor.matmul(lps[:, 0:E], h2T[:, c], gate_sb[:, c], start=(c == 0), stop=(c == C - 1))
                    last.then_inc(logits_done, 1)

                def positions(j, b):
                    pe.wait_ge(mask_done, j + 1)
                    nc.tensor.matmul(pps[:, 0:E], before[:], mask[:, b], start=True, stop=False)
                    nc.tensor.matmul(pps[:, 0:E], ones[:], seen[:, b], start=False, stop=True).then_inc(pos_done, 1)

                def body(i, b, gemm, more, router, slots):
                    if gemm:
                        product(i, b, known(i) and i == 0)
                    if slots:
                        positions(i - 2, b)
                    if router:
                        route(i - 1, 1 - b)
                tiles(pe, body)
                pe.wait_ge(slot_done, NT)
                nc.tensor.matmul(pps[:, 0:E], ones[:], seen[:, NT % 2], start=True, stop=True).then_inc(count_done, 1)

            @block.scalar
            def _(act):
                for c in range(C):
                    act.wait_ge(w_in[c % 4], 16 * (c // 4 + 1))
                    nc.scalar.copy(w_hi[:, c], w_raw[:, c % 4]).then_inc(w_hi_done, 1)
                    if c == 1:
                        act.wait_ge(cn_done, 1)
                        nc.scalar.copy(c_hi[:, 0], cn[:, 0]).then_inc(c_hi_done, 1)
                act.wait_ge(consts_in, 16 * CONSTS)
                nc.scalar.copy(bo_hi[:], bo_row[:]).then_inc(bo_ready, 1)
                act.wait_ge(rs_ready, 2)

                def body(i, b, gemm, more, router, slots):
                    if more:
                        act.wait_ge(cn_done, i + 2)
                        if not (known(i) and i < 1):
                            act.wait_ge(gemm_done, i)
                        nc.scalar.copy(c_hi[:, 1 - b], cn[:, 1 - b]).then_inc(c_hi_done, 1)
                    if gemm:
                        act.wait_ge(gemm_done, i + 1)
                        if not (known(i) and i < 2):
                            act.wait_ge(x1_done, i - 1)
                        nc.scalar.activation(d[:, b], o[:, b], ACT.Copy, scale=rs_sb[:]).then_inc(d_done, 1)
                    if router:
                        act.wait_ge(t_done, i)
                        nc.scalar.copy(h2T[:], tps[:]).then_inc(h2T_done, 1)
                        act.wait_ge(diff_done, i)
                        nc.scalar.activation(e8[:], diff[:], ACT.Exp, accum_out=esum[:]).then_inc(e8_done, 1)
                    if gemm:
                        for k in range(2):
                            act.wait_ge(mv_ready, 2 * i + k + 1)
                            nc.scalar.activation(std[:, k], mv[:, k, 1:2], ACT.Sqrt, bias=eps[:]).then_inc(std_ready, 1)
                tiles(act, body)

            @block.vector
            def _(dve):
                def prepare(i, b):
                    dve.wait_ge(c_in[b], 48 * (i // 2 + 1) if known(i) else 48 * pair_of(i, b) + 48)
                    nc.vector.tensor_tensor(cn[:, b], c_raw[:, b], r_t[:, b], ALU.mult).then_inc(cn_done, 1)
                    dve.wait_ge(c_hi_done, i + 1)
                    nc.vector.tensor_tensor(c_lo[:, b], cn[:, b], f32(c_hi[:, b]), ALU.subtract).then_inc(c_lo_done, 1)

                def carry_wait():
                    dve.sem_inc(dve_passed, 1)

                half_of = {}

                def pair_of(i, b):
                    return half_of[b]

                NORM_STEPS = 2 * (HV + 1) + 2

                def moments(i, k, src, at):
                    for h in range(HV):
                        nc.vector.bn_stats(stats[:, k, h], src[:, h * HALF:(h + 1) * HALF]).then_inc(norm_step, 1)
                    dve.wait_ge(norm_step, NORM_STEPS * i + at + HV)
                    carry_wait()
                    nc.vector.bn_aggr(mv[:, k], stats[:, k]).then_inc(mv_ready, 1)
                    dve.wait_ge(std_ready, 2 * i + k + 1)
                    nc.vector.reciprocal(rstd[:, k], std[:, k]).then_inc(norm_step, 1)
                    dve.wait_ge(norm_step, NORM_STEPS * i + at + HV + 1)

                def normalize(i, b, x_count):
                    dve.wait_ge(d_done, i + 1)
                    moments(i, 0, d[:, b], 0)
                    nc.vector.scalar_tensor_tensor(out=scaled[:], in0=d[:, b], scalar=mv[:, 0, 0:1], in1=gamma_sb[:],
                                                   op0=ALU.subtract, op1=ALU.mult).then_inc(norm_step, 1)
                    dve.wait_ge(norm_step, NORM_STEPS * i + HV + 2)
                    dve.wait_ge(x_in[b], x_count)
                    nc.vector.scalar_tensor_tensor(out=normed[:], in0=scaled[:], scalar=rstd[:, 0], in1=x_t[:, b],
                                                   op0=ALU.mult, op1=ALU.add).then_inc(norm_step, 1)
                    dve.wait_ge(norm_step, NORM_STEPS * i + HV + 3)
                    if not (known(i) and i < 2):
                        dve.wait_ge(stored[b], 2 * x_count - 32)
                    nc.vector.tensor_tensor(x1[:, b], normed[:], beta_sb[:], ALU.add).then_inc(x1_done, 1)
                    dve.wait_ge(x1_done, i + 1)
                    moments(i, 1, x1[:, b], HV + 3)
                    if not (known(i) and i < 2):
                        dve.wait_ge(t_done, i - 1)
                    nc.vector.tensor_scalar(h2[:, b], x1[:, b], mv[:, 1, 0:1], rstd[:, 1],
                                            ALU.subtract, ALU.mult).then_inc(h2_done, 1)

                ROUTE_STEPS = 6

                def route(j, b, done_before):
                    def step(k):
                        dve.wait_ge(route_step, ROUTE_STEPS * j + k)
                    dve.wait_ge(logits_done, j + 1)
                    nc.vector.tensor_copy(logits[:], lps[:, 0:E]).then_inc(route_step, 1)
                    step(1)
                    carry_wait()
                    nc.vector.max(top[:], logits[:]).then_inc(route_step, 1)
                    step(2)
                    carry_wait()
                    nc.vector.max_index(top_i[:], top[:], logits[:]).then_inc(route_step, 1)
                    nc.vector.tensor_scalar(diff[:], top[:], top[:, 0:1], None, ALU.subtract).then_inc(diff_done, 1)
                    step(3)
                    nc.vector.tensor_copy(top_f[:], top_i[:]).then_inc(route_step, 1)
                    step(4)
                    nc.vector.tensor_tensor(onehot[:, b], top_f[:].unsqueeze(2).broadcast_to([P, TOPK, E]),
                                            iota_e[:].unsqueeze(1).broadcast_to([P, TOPK, E]), ALU.is_equal).then_inc(route_step, 1)
                    step(5)
                    nc.vector.tensor_reduce(mask[:, b], onehot[:, b].rearrange("p k e -> p e k"), AX.X, ALU.add).then_inc(mask_done, 1)
                    dve.wait_ge(mask_done, j + 1)
                    if not (known(j) and j < 1):
                        dve.wait_ge(pos_done, j)
                    nc.vector.tensor_tensor(seen[:, 1 - b], seen[:, b], mask[:, b], ALU.add).then_inc(seen_done, 1)
                    dve.wait_ge(seen_done, j + 1)
                    dve.wait_ge(e8_done, j + 1)
                    nc.vector.reciprocal(rsum[:], esum[:]).then_inc(route_step, 1)
                    step(6)
                    dve.wait_ge(scattered[b], 16 * TOPK * done_before)
                    nc.vector.tensor_scalar(record[:, b, :, 1], e8[:], rsum[:], None, ALU.mult).then_inc(record_done, 1)
                    nc.vector.tensor_copy(record[:].bitcast(I32)[:, b, :, 0], token[:].broadcast_to([P, TOPK])).then_inc(record_done, 1)
                    dve.wait_ge(record_done, 3 * j + 2)
                    nc.vector.tensor_scalar(token[:], token[:], float(P), None, ALU.add).then_inc(record_done, 1)

                def slots(j, b):
                    dve.wait_ge(pos_done, j + 1)
                    nc.vector.tensor_tensor(row_e[:], pps[:, 0:E], rowbase[:], ALU.add).then_inc(slot_step, 1)
                    dve.wait_ge(slot_step, 3 * j + 1)
                    nc.vector.tensor_tensor(prod[:], onehot[:, b], row_e[:].unsqueeze(1).broadcast_to([P, TOPK, E]), ALU.mult).then_inc(slot_step, 1)
                    dve.wait_ge(slot_step, 3 * j + 2)
                    nc.vector.tensor_reduce(slot_f[:], prod[:], AX.X, ALU.add).then_inc(slot_step, 1)
                    dve.wait_ge(slot_step, 3 * j + 3)
                    nc.vector.tensor_copy(slot[:, b], slot_f[:]).then_inc(slot_done, 1)

                nc.vector.memset(eps[:], EPS).then_inc(rs_ready, 1)
                nc.vector.memset(seen[:, 0], 0.0).then_inc(seen_ready, 1)
                dve.wait_ge(c_in[0], 48)
                for c in range(C):
                    if c == 1:
                        prepare(0, 0)
                    dve.wait_ge(w_hi_done, c + 1)
                    nc.vector.tensor_tensor(w_lo[:, c], w_raw[:, c % 4], f32(w_hi[:, c]), ALU.subtract).then_inc(w_lo_done, 1)
                dve.wait_ge(consts_in, 16 * CONSTS)
                nc.vector.tensor_scalar(rs_sb[:], rs_raw[:], 0.0, RES_SCALE_MAX, ALU.max, ALU.min).then_inc(rs_ready, 1)
                dve.wait_ge(bo_ready, 1)
                nc.vector.tensor_tensor(bo_lo[:], bo_row[:], f32(bo_hi[:]), ALU.subtract).then_inc(bo_ready, 1)
                dve.wait_ge(masks_ready, 7)
                nc.vector.tensor_scalar(rowbase[:], iota_e[:], float(REGION), float(REGION), ALU.mult, ALU.add).then_inc(seen_ready, 1)
                dve.wait_ge(seen_ready, 2)

                def body(i, b, gemm, more, router, slot):
                    n = i // 2 if known(i) else half[0]
                    if more:
                        half_of[1 - b] = n + (1 if b else 0)
                        prepare(i + 1, 1 - b)
                    if slot:
                        slots(i - 2, b)
                    if router:
                        route(i - 1, 1 - b, (n - 1 if b == 0 else n))
                    if gemm:
                        normalize(i, b, 16 * (n + 1))

                half = [None]
                body(0, 0, True, True, False, False)
                body(1, 1, True, True, True, False)
                with dve.Fori(1, NT // 2 - 1) as h:
                    half[0] = h
                    body(2 * h, 0, True, True, True, True)
                    body(2 * h + 1, 1, True, True, True, True)
                body(NT - 2, 0, True, True, True, True)
                body(NT - 1, 1, True, False, True, True)
                body(NT, 0, False, False, True, True)
                body(NT + 1, 1, False, False, False, True)

                steps = [0]

                def step(instruction):
                    instruction.then_inc(dir_step, 1)
                    steps[0] += 1
                    dve.wait_ge(dir_step, steps[0])

                dve.wait_ge(count_done, 1)
                step(nc.vector.tensor_scalar(cnt[:], pps[:, 0:E], float(P - 1), None, ALU.add))
                step(nc.vector.tensor_copy(tiles_i[:], cnt[:]))
                step(nc.vector.tensor_scalar(tiles_i[:], tiles_i[:], P.bit_length() - 1, None, ALU.arith_shift_right))
                step(nc.vector.tensor_copy(tiles_f[:], tiles_i[:]))
                step(nc.vector.tensor_scalar(tiles_f[:], tiles_f[:], 1.0, None, ALU.max))
                step(nc.vector.tensor_tensor_scan(upto[:], ones[:, 0:E], tiles_f[:], 0.0, ALU.mult, ALU.add))
                step(nc.vector.tensor_tensor(base[:], upto[:], tiles_f[:], ALU.subtract))
                step(nc.vector.tensor_tensor(cmp[:], base[:].unsqueeze(1).broadcast_to([P, NCOL, E]),
                                             tile_id[:].unsqueeze(2).broadcast_to([P, NCOL, E]), ALU.is_le))
                step(nc.vector.tensor_reduce(started[:], cmp[:], AX.X, ALU.add))
                step(nc.vector.tensor_tensor(cmp[:], cmp[:], base[:].unsqueeze(1).broadcast_to([P, NCOL, E]), ALU.mult))
                step(nc.vector.tensor_reduce(first_of[:], cmp[:], AX.X, ALU.max))
                step(nc.vector.tensor_tensor(row_f[:], tile_id[:], first_of[:], ALU.subtract))
                step(nc.vector.tensor_scalar(row_f[:], row_f[:], float(P), None, ALU.mult))
                step(nc.vector.tensor_scalar(started[:], started[:], float(REGION), None, ALU.mult))
                step(nc.vector.tensor_tensor(row_f[:], row_f[:], started[:], ALU.add))
                step(nc.vector.tensor_copy(row_i[:], row_f[:]))
                step(nc.vector.tensor_copy(dir_sb[0:1, n_at:n_at + E], tiles_f[0:1, :]))
                step(nc.vector.tensor_copy(dir_sb[0:1, base_at:base_at + E], base[0:1, :]))
                step(nc.vector.tensor_scalar(dir_sb[0:1, last_at:last_at + 1], upto[0:1, E - 1:E], -1.0, None, ALU.add))
                nc.vector.memset(dir_sb[0:1, row_at:row_at + 1], 0).then_inc(dir_done, 1)


def experts_pass(nc, h2st, table, dirst, w_gate, w_up, w_down, acc):
    E, H, I = w_gate.shape
    C, CI, HV = H // P, I // P, H // HALF
    n_at, base_at, last_at, row_at = directory(E)
    NDIR = dirst.shape[1]
    MAX_TILES = NDIR - row_at - 1
    with ExitStack() as st:
        s = Scope(nc, st, "moe")
        raw_g, raw_u, raw_d = s.sb("raw_g", [P, C, I]), s.sb("raw_u", [P, C, I]), s.sb("raw_d", [P, CI, H])
        gu_hi, gu_lo = s.sb("gu_hi", [P, 2, 2, C, I], F32R), s.sb("gu_lo", [P, 2, 2, C, I], F32R)
        d_hi, d_lo = s.sb("d_hi", [P, 2, CI, H], F32R), s.sb("d_lo", [P, 2, CI, H], F32R)
        tokens, xT_hi, xT_lo = s.sb("tokens", [P, H]), s.sb("xT_hi", [P, C, P], F32R), s.sb("xT_lo", [P, C, P], F32R)
        silu, hidden = s.sb("silu", [P, I]), s.sb("hidden", [P, I])
        hT_hi, hT_lo = s.sb("hT_hi", [P, CI, P], F32R), s.sb("hT_lo", [P, CI, P], F32R)
        y = s.sb("y", [P, H])
        ident, rec_g, rec_s = s.sb("ident", [P, P]), s.sb("rec_g", [P, 2]), s.sb("rec_s", [P, 2])
        dir_sb = s.sb("dir", [1, NDIR], I32)
        gate_ps, up_ps, hT_ps = s.ps("gate", [P, HALF]), s.ps("up", [P, HALF]), s.ps("hT", [P, HALF // P, P])[:, 0:CI]
        xT_ps, y_ps = s.ps("xT", [P, C, P]), s.ps("y", [P, H])

        raw_in = [s.sem(f"raw_in{i}") for i in range(3)]
        dir_in, set_up, ready, pool_passed, sp_passed = s.sem("dir_in"), s.sem("set_up"), s.sem("ready"), s.sem("pool_passed"), s.sem("sp_passed")
        w_hi_done, w_lo_done = s.sem("w_hi_done"), s.sem("w_lo_done")
        rec_g_in, rec_s_in, gathered, added = s.sem("rec_g_in"), s.sem("rec_s_in"), s.sem("gathered"), s.sem("added")
        xT_done, xT_hi_done, xT_lo_done = s.sem("xT_done"), s.sem("xT_hi_done"), s.sem("xT_lo_done")
        gu_done, silu_done, hidden_done = s.sem("gu_done"), s.sem("silu_done"), s.sem("hidden_done")
        hT_done, hT_hi_done, hT_lo_done = s.sem("hT_done"), s.sem("hT_hi_done"), s.sem("hT_lo_done")
        down_done, y_done = s.sem("down_done"), s.sem("y_done")

        def pieces(b):
            for k, raw in enumerate((raw_g, raw_u)):
                for c in range(0, C, 2):
                    yield raw[:, c:c + 2], raw_in[k], gu_hi[:, b, k, c:c + 2], gu_lo[:, b, k, c:c + 2]
            for c in range(CI):
                yield raw_d[:, c], raw_in[2], d_hi[:, b, c], d_lo[:, b, c]
        PIECES = C + CI
        EARLY = 3

        def experts(eng, body):
            with eng.Fori(0, E // 2 - 1) as h:
                body(2 * h, 0, True, True)
                body(2 * h + 1, 1, True, True)
            body(E - 2, 0, True, False)
            body(E - 1, 1, False, False)

        def expert_tiles(eng, e, first_tile, tile):
            n = eng.value_load(dir_sb[0:1, bass.ds(n_at + e, 1)], min_val=1, max_val=REGION // P)
            base = eng.value_load(dir_sb[0:1, bass.ds(base_at + e, 1)], min_val=0, max_val=MAX_TILES)
            first_tile(base)
            with eng.If(n > 1):
                with eng.Fori(1, n) as j:
                    tile(base + j)

        with nc.Block() as block:
            @block.sync
            def _(sp):
                sp.dma_start(dir_sb[:], dirst).then_inc(dir_in, 16)
                sp.wait_ge(dir_in, 16)
                last_tile = sp.value_load(dir_sb[0:1, last_at:last_at + 1], min_val=E - 1, max_val=MAX_TILES - 2)

                def record(dst, t, sem):
                    row = sp.value_load(dir_sb[0:1, bass.ds(row_at + 1 + t, 1)], min_val=0, max_val=table.shape[0] - P)
                    sp.dma_start(dst[:], table[bass.ds(row, P), :]).then_inc(sem, 16)

                record(rec_g, 0, rec_g_in)
                sp.wait_ge(gathered, 16)
                record(rec_g, 1, rec_g_in)
                with sp.Fori(0, last_tile) as t:
                    sp.wait_ge(gathered, 16 * (t + 2))
                    record(rec_g, t + 2, rec_g_in)
                    sp.wait_ge(added, 16 * t)
                    record(rec_s, t - 1, rec_s_in)
                sp.wait_ge(added, 16 * last_tile)
                record(rec_s, last_tile - 1, rec_s_in)
                sp.wait_ge(added, 16 * last_tile + 16)
                record(rec_s, last_tile, rec_s_in)
                sp.wait_ge(added, 16 * last_tile + 32)
                sp.sem_inc(sp_passed, 1)

            @block.gpsimd
            def _(pool):
                nc.gpsimd.memset(ident[:], 0.0).then_inc(set_up, 1)
                pool.wait_ge(set_up, 1)
                nc.gpsimd.affine_select(out=ident[:], in_=ident[:], compare_op=ALU.not_equal, fill=1.0, base=0,
                                        pattern=[[-1, P]], channel_multiplier=1).then_inc(ready, 1)
                pool.wait_ge(dir_in, 16)
                last_tile = pool.value_load(dir_sb[0:1, last_at:last_at + 1], min_val=E - 1, max_val=MAX_TILES - 2)

                def gather(t):
                    pool.wait_ge(rec_g_in, 16 * (t + 1))
                    pool.wait_ge(xT_done, t)
                    pool.sem_inc(pool_passed, 1)
                    nc.gpsimd.indirect_dma_start(
                        out=tokens[:], out_offset=None, in_=h2st[:, :],
                        in_offset=bass.IndirectOffsetOnAxis(ap=rec_g[:].bitcast(I32)[:, 0:1], axis=0)).then_inc(gathered, 16)

                def add(t):
                    pool.wait_ge(y_done, t + 2)
                    pool.sem_inc(pool_passed, 1)
                    nc.gpsimd.indirect_dma_start(
                        out=acc[:, :], out_offset=bass.IndirectOffsetOnAxis(ap=rec_s[:].bitcast(I32)[:, 0:1], axis=0),
                        in_=y[:], in_offset=None, compute_op=ALU.add).then_inc(added, 16)

                gather(0)
                gather(1)
                with pool.Fori(0, last_tile) as t:
                    gather(t + 2)
                    add(t - 1)
                add(last_tile - 1)
                add(last_tile)

            @block.tensor
            def _(pe):
                pe.wait_ge(ready, 4)
                pe.wait_ge(dir_in, 16)

                def transpose_tokens(t):
                    pe.wait_ge(gathered, 16 * (t + 1))
                    for c in range(C):
                        last = nc.tensor.transpose(xT_ps[:, c], tokens[:, c * P:(c + 1) * P], ident[:])
                    last.then_inc(xT_done, 1)

                def down(t, b):
                    pe.wait_ge(hT_lo_done, t + 1)
                    pe.wait_ge(y_done, t + 1)
                    for h in range(HV):
                        cols = slice(h * HALF, (h + 1) * HALF)
                        for c in range(CI):
                            nc.tensor.matmul(y_ps[:, cols], hT_hi[:, c], d_hi[:, b, c, cols], start=(c == 0), stop=False)
                            nc.tensor.matmul(y_ps[:, cols], hT_hi[:, c], d_lo[:, b, c, cols], start=False, stop=False)
                            last = nc.tensor.matmul(y_ps[:, cols], hT_lo[:, c], d_hi[:, b, c, cols], start=False, stop=(c == CI - 1))
                    last.then_inc(down_done, 1)

                def tile(t, b, b_before):
                    pe.wait_ge(xT_lo_done, t + 1)
                    pe.wait_ge(hidden_done, t)
                    for k, o in enumerate((gate_ps, up_ps)):
                        for c in range(C):
                            nc.tensor.matmul(o[:, 0:I], xT_hi[:, c], gu_hi[:, b, k, c], start=(c == 0), stop=False)
                            nc.tensor.matmul(o[:, 0:I], xT_hi[:, c], gu_lo[:, b, k, c], start=False, stop=False)
                            last = nc.tensor.matmul(o[:, 0:I], xT_lo[:, c], gu_hi[:, b, k, c], start=False, stop=(c == C - 1))
                        last.then_inc(gu_done, 1)
                    transpose_tokens(t + 1)
                    down(t - 1, b_before)
                    pe.wait_ge(hidden_done, t + 1)
                    for c in range(CI):
                        last = nc.tensor.transpose(hT_ps[:, c], hidden[:, c * P:(c + 1) * P], ident[:])
                    last.then_inc(hT_done, 1)

                transpose_tokens(0)

                def expert(e, b, has_next, has_second):
                    pe.wait_ge(w_lo_done, PIECES * (e + 1))
                    expert_tiles(pe, e, lambda t: tile(t, b, 1 - b), lambda t: tile(t, b, b))
                experts(pe, expert)
                last_tile = pe.value_load(dir_sb[0:1, last_at:last_at + 1], min_val=E - 1, max_val=MAX_TILES - 2)
                down(last_tile, (E - 1) % 2)

            @block.scalar
            def _(act):
                def load_weights(e):
                    for k, (raw, src) in enumerate(((raw_g, w_gate), (raw_u, w_up), (raw_d, w_down))):
                        act.dma_start(raw[:], src[bass.ds(e, 1)].rearrange("o (c p) i -> p (o c) i", p=P)).then_inc(raw_in[k], 16)

                def split(e, b, lo, hi):
                    for n, (raw, loaded, high, low) in enumerate(pieces(b)):
                        if lo <= n < hi:
                            act.wait_ge(loaded, 16 * (e + 1))
                            nc.scalar.copy(high, raw).then_inc(w_hi_done, 1)

                def tokens_high(t):
                    act.wait_ge(xT_done, t + 1)
                    nc.scalar.copy(xT_hi[:], xT_ps[:]).then_inc(xT_hi_done, 1)

                def output(t):
                    act.wait_ge(down_done, t + 2)
                    act.wait_ge(rec_s_in, 16 * (t + 2))
                    nc.scalar.activation(y[:], y_ps[:], ACT.Copy, scale=rec_s[:, 1:2]).then_inc(y_done, 1)

                def tile(t, e=None, b=None):
                    act.wait_ge(gu_done, 2 * t + 1)
                    act.wait_ge(hidden_done, t)
                    nc.scalar.activation(silu[:], gate_ps[:, 0:I], ACT.Silu).then_inc(silu_done, 1)
                    tokens_high(t + 1)
                    if e is not None:
                        split(e, b, 0, EARLY)
                    output(t - 1)
                    act.wait_ge(hT_done, t + 1)
                    nc.scalar.copy(hT_hi[:], hT_ps).then_inc(hT_hi_done, 1)
                    if e is not None:
                        split(e, b, EARLY, PIECES)

                load_weights(0)
                act.wait_ge(dir_in, 16)
                split(0, 0, 0, PIECES)
                act.wait_ge(w_lo_done, PIECES)
                load_weights(1)
                tokens_high(0)

                def expert(e, b, has_next, has_second):
                    def first(t):
                        if has_next:
                            tile(t, e + 1, 1 - b)
                        else:
                            tile(t)
                        if has_second:
                            act.wait_ge(w_lo_done, PIECES * (e + 2))
                            load_weights(e + 2)
                    expert_tiles(act, e, first, tile)
                experts(act, expert)
                last_tile = act.value_load(dir_sb[0:1, last_at:last_at + 1], min_val=E - 1, max_val=MAX_TILES - 2)
                output(last_tile)

            @block.vector
            def _(dve):
                def split(e, b, lo, hi):
                    for n, (raw, loaded, high, low) in enumerate(pieces(b)):
                        if lo <= n < hi:
                            dve.wait_ge(w_hi_done, PIECES * e + n + 1)
                            nc.vector.tensor_tensor(low, raw, f32(high), ALU.subtract).then_inc(w_lo_done, 1)

                def tokens_low(t):
                    dve.wait_ge(xT_hi_done, t + 1)
                    nc.vector.tensor_tensor(xT_lo[:], xT_ps[:], f32(xT_hi[:]), ALU.subtract).then_inc(xT_lo_done, 1)

                def tile(t, e=None, b=None):
                    dve.wait_ge(silu_done, t + 1)
                    dve.wait_ge(gu_done, 2 * t + 2)
                    dve.wait_ge(hT_done, t)
                    nc.vector.tensor_tensor(hidden[:], silu[:], up_ps[:, 0:I], ALU.mult).then_inc(hidden_done, 1)
                    tokens_low(t + 1)
                    if e is not None:
                        split(e, b, 0, EARLY)
                    dve.wait_ge(hT_hi_done, t + 1)
                    nc.vector.tensor_tensor(hT_lo[:], hT_ps, f32(hT_hi[:]), ALU.subtract).then_inc(hT_lo_done, 1)
                    if e is not None:
                        split(e, b, EARLY, PIECES)

                nc.vector.memset(f32(d_hi[:, 1]), 0.0).then_inc(ready, 1)
                nc.vector.memset(f32(d_lo[:, 1]), 0.0).then_inc(ready, 1)
                nc.vector.memset(f32(hT_hi[:]), 0.0)
                nc.vector.memset(f32(hT_lo[:]), 0.0).then_inc(ready, 1)
                dve.wait_ge(dir_in, 16)
                split(0, 0, 0, PIECES)
                tokens_low(0)

                def expert(e, b, has_next, has_second):
                    if has_next:
                        expert_tiles(dve, e, lambda t: tile(t, e + 1, 1 - b), tile)
                    else:
                        expert_tiles(dve, e, tile, tile)
                experts(dve, expert)


def cross_attention_and_experts(nc, x, ctxT, mask, wqT, bq, wkT, bk, wvT, bv, woT, bo, gamma, beta, rscale,
                                gateT, w_gate, w_up, w_down, out):
    H, T = ctxT.shape
    B, E = mask.shape[1], w_gate.shape[0]
    S, NH = T // B, H // HD

    def scratch(name, shape, dt=F32):
        return nc.dram_tensor(name, shape, dt, kind="Internal").ap()

    xnT = scratch("xnT", (H, T))
    kst, qst, vst = scratch("kst", (B * NH, 2 * HD, S)), scratch("qst", (B * NH, 2, HD, S)), scratch("vst", (T, NH, 2 * HD))
    ctxst, sums, rsums = scratch("ctxst", (H, T)), scratch("sums", (NH, T)), scratch("rsums", (NH, T))
    h2st, table = scratch("h2st", (T + P, H)), scratch("table", (table_regions(E) * REGION, 2))
    dirst = scratch("dirst", (1, directory(E)[-1] + 1 + 3 * P), I32)
    layernorm_pass(nc, x, xnT)
    projection_pass(nc, "k", ctxT, wkT, bk, kst)
    projection_pass(nc, "v", ctxT, wvT, bv, vst)
    projection_pass(nc, "q", xnT, wqT, bq, qst)
    attention_pass(nc, kst, qst, vst, mask, ctxst, sums, B, S)
    reciprocal_pass(nc, sums, rsums)
    output_pass(nc, ctxst, rsums, woT, bo, gamma, beta, rscale, x, gateT, out, h2st, table, dirst)
    experts_pass(nc, h2st, table, dirst, w_gate, w_up, w_down, out)


def kernel(**inputs):
    from concourse import bacc
    from concourse.bass_utils import run_bass_kernel_spmd

    given = {name: np.asarray(value) for name, value in inputs.items()}
    x, mask = given["x"], given["mask_BxS2_ik0"]
    B, S, H = x.shape
    T = B * S

    def transposed(name):
        return given[name].reshape(-1, H).T

    def by_feature(name):
        return given[name].reshape(H // P, P).T

    def row(name):
        return given[name].reshape(1, -1)

    laid = {
        "x": x.reshape(T, H), "ctxT": transposed("ctx_2048"),
        "mask": mask.reshape(B, S // P, P).transpose(2, 0, 1),
        "wqT": transposed("L0_xattn_Wq"), "bq": by_feature("L0_xattn_bq"),
        "wkT": transposed("L0_xattn_Wk"), "bk": by_feature("L0_xattn_bk"),
        "wvT": transposed("L0_xattn_Wv"), "bv": row("L0_xattn_bv"),
        "woT": transposed("L0_xattn_Wo"), "bo": row("L0_xattn_bo"),
        "gamma": row("L0_xattn_ln_gamma"), "beta": row("L0_xattn_ln_beta"),
        "rscale": given["L0_xattn_residual_scale"].reshape(1, 1),
        "gateT": transposed("L0_ffn_gate_weight"),
        "w_gate": given["L0_ffn_w_gate"], "w_up": given["L0_ffn_w_up"], "w_down": given["L0_ffn_w_down"],
    }
    nc = bacc.Bacc("TRN2", target_bir_lowering=False, num_devices=1)
    arrays, args = {}, {}
    for name, a in laid.items():
        a = np.ascontiguousarray(a)
        arrays[f"in_{name}"] = a
        args[name] = nc.dram_tensor(f"in_{name}", a.shape, mybir.dt.from_np(a.dtype), kind="ExternalInput").ap()
    out = nc.dram_tensor("out", (T + P, H), F32, kind="ExternalOutput").ap()
    cross_attention_and_experts(nc, out=out, **args)
    result = run_bass_kernel_spmd(nc, [arrays], core_ids=[0])
    return result.results[0]["out"][:T].reshape(B, S, H)
```

```python
from contextlib import ExitStack
import math

import numpy as np
import concourse.bass as bass
from concourse import mybir

F32, F32R = mybir.dt.float32, mybir.dt.float32r
I32, U32 = mybir.dt.int32, mybir.dt.uint32
ALU, ACT, AX = mybir.AluOpType, mybir.ActivationFunctionType, mybir.AxisListType

P = 128
HD = 64
HALF = 512
TOPK = 8
REGION = 4096
EPS = 1e-5
CLIP = 50.0
RES_SCALE_MAX = 0.3
BIG = 3.0e38


class Scope:

    def __init__(self, nc, stack, name):
        self.nc, self.stack, self.name, self.sems = nc, stack, name, []
        stack.callback(self.clear)

    def sb(self, name, shape, dt=F32):
        return self.stack.enter_context(self.nc.sbuf_tensor(f"{self.name}_{name}", shape, dt))

    def ps(self, name, shape, dt=F32):
        return self.stack.enter_context(self.nc.psum_tensor(f"{self.name}_ps_{name}", shape, dt))

    def sem(self, name):
        self.sems.append(self.nc.alloc_semaphore(f"{self.name}_{name}"))
        return self.sems[-1]

    def clear(self):
        self.nc.clear_and_free_semaphores(self.sems)
        self.nc.all_engine_barrier()


def f32(ap):
    return ap.bitcast(F32)


def row_broadcast(dram_row, n):
    return dram_row.broadcast_to([P, n])


def projection_pass(nc, kind, actT, wT, bias, out, x=None, xnT=None):
    H, T = actT.shape
    C = H // P
    NB = T // HALF
    G = C if kind != "v" else (HALF // P) * (H // HALF)
    BANKS = 4
    S = out.shape[-1] if kind != "v" else None
    NH = H // HD
    RAW = 3
    LN = HALF // P if x is not None else 0
    HV = H // HALF
    with ExitStack() as st:
        s = Scope(nc, st, "proj_" + kind)
        w_raw = s.sb("w_raw", [P, RAW, H])
        w_hi, w_lo = s.sb("w_hi", [P, C, H], F32R), s.sb("w_lo", [P, C, H], F32R)
        a_raw = s.sb("a_raw", [P, 2, C, HALF])
        a_hi, a_lo = s.sb("a_hi", [P, 2, C, HALF], F32R), s.sb("a_lo", [P, 2, C, HALF], F32R)
        if kind == "v":
            bias_sb, v32 = s.sb("bias", [P, H]), s.sb("v32", [P, 2, HALF])
            o = s.sb("o", [P, 2, HALF // HD, 2, HD], F32R)
        else:
            bias_sb = s.sb("bias", [P, C])
            o_hi, o_lo = s.sb("o_hi", [P, 2, HALF], F32R), s.sb("o_lo", [P, 2, HALF], F32R)
        acc = s.ps("acc", [P, BANKS, HALF])
        if LN:
            xin, xn, xT = s.sb("xin", [P, 2, H]), s.sb("xn", [P, 2, H]), s.sb("xT", [P, 2, C, P])
            stats, mv = s.sb("stats", [P, 2, HV, 6]), s.sb("mv", [P, 2, 2])
            std, rstd, eps = s.sb("std", [P, 2, 1]), s.sb("rstd", [P, 2, 1]), s.sb("eps", [P, 1])
            ident = s.sb("ident", [P, P])
            tps = s.ps("tps", [P, 2, C, P])
            x_in, xT_stored = [s.sem("x_in0"), s.sem("x_in1")], [s.sem("xT_stored0"), s.sem("xT_stored1")]
            zeroed, ident_ready, stats_passed = s.sem("zeroed"), s.sem("ident_ready"), s.sem("stats_passed")
            sp_passed = s.sem("sp_passed")
            eps_ready, std_done, rstd_done = s.sem("eps_ready"), s.sem("std_done"), s.sem("rstd_done")
            stats_done, mv_done = s.sem("stats_done"), s.sem("mv_done")
            xn_done, t_done, xT_done = s.sem("xn_done"), s.sem("t_done"), s.sem("xT_done")
            xnT_v = xnT.rearrange("(c p) t -> p c t", p=P)
        w_in = [s.sem(f"w_in{i}") for i in range(RAW)]
        a_in = [s.sem(f"a_in{i}") for i in range(2)]
        bias_in, bank_free = s.sem("bias_in"), s.sem("bank_free")
        w_hi_done, w_lo_done = s.sem("w_hi_done"), s.sem("w_lo_done")
        a_hi_done, a_lo_done = s.sem("a_hi_done"), s.sem("a_lo_done")
        product_done, v32_done, o_hi_done, o_lo_done = s.sem("product_done"), s.sem("v32_done"), s.sem("o_hi_done"), s.sem("o_lo_done")
        stored = [s.sem(f"stored{i}") for i in range(2)]
        STORES = 1 if kind == "v" else 4
        act_v = actT.rearrange("(c p) t -> p c t", p=P)

        def ln_before(t, j):
            return LN * t + max(j - 1, 0)

        with nc.Block() as block:
            @block.gpsimd
            def _(pool):
                if LN:
                    nc.gpsimd.memset(ident[:], 0.0).then_inc(zeroed, 1)
                    pool.wait_ge(zeroed, 1)
                    nc.gpsimd.affine_select(out=ident[:], in_=ident[:], compare_op=ALU.not_equal, fill=1.0, base=0,
                                            pattern=[[-1, P]], channel_multiplier=1).then_inc(ident_ready, 1)
                if kind == "v":
                    pool.dma_start(bias_sb[:], row_broadcast(bias, H)).then_inc(bias_in, 16)
                else:
                    pool.dma_start(bias_sb[:], bias).then_inc(bias_in, 16)

                def load(t, b):
                    pool.dma_start(a_raw[:, b], act_v[:, :, bass.ds(t * HALF, HALF)]).then_inc(a_in[b], 16)

                load(0, 0)
                load(1, 1)
                with pool.Fori(0, NB // 2 - 1) as i:
                    for b in range(2):
                        pool.wait_ge(a_lo_done, 2 * i + b + 1)
                        load(2 * i + b + 2, b)

            @block.sync
            def _(sp):
                for c in range(C):
                    if c >= RAW:
                        sp.wait_ge(w_lo_done, c - RAW + 1)
                    sp.dma_start(w_raw[:, c % RAW], wT[c * P:(c + 1) * P, :]).then_inc(w_in[c % RAW], 16)

                def load_x(t, j):
                    sp.dma_start(xin[:, j % 2], x[bass.ds((LN * t + j) * P, P), :]).then_inc(x_in[j % 2], 16)

                def layernorm(t, g, last):
                    j = g // 2
                    if g % 2:
                        sp.wait_ge(xT_done, LN * t + j + 1)
                        sp.sem_inc(sp_passed, 1)
                        sp.dma_start(xnT_v[:, :, bass.ds((LN * t + j) * P, P)], xT[:, j % 2]).then_inc(xT_stored[j % 2], 16)
                    elif not last or j + 2 < LN:
                        sp.wait_ge(xn_done, LN * t + j + 1)
                        load_x(t, j + 2)

                if LN:
                    load_x(0, 0)
                    load_x(0, 1)

                def store(i, last):
                    for b in range(2):
                        for g in range(G):
                            if LN and g:
                                layernorm(2 * i + b, g - 1, last and b == 1)
                            sp.wait_ge(o_lo_done, (2 * i + b) * G + g + 1)
                            q = g % 2
                            if kind == "v":
                                row = (2 * i + b) * HALF + (g // (H // HALF)) * P
                                h0 = (g % (H // HALF)) * (HALF // HD)
                                sp.dma_start(out[bass.ds(row, P), h0:h0 + HALF // HD, :],
                                             f32(o[:, q]).rearrange("p h two d -> p h (two d)")).then_inc(stored[q], 16)
                                continue
                            if S == 2 * HALF:
                                bh, t0 = i * NH + 2 * g, b * HALF
                            else:
                                bh, t0 = (2 * i + b) * NH + 2 * g, 0
                            for hh in range(2):
                                for k, tile in enumerate((o_hi, o_lo)):
                                    if kind == "k":
                                        dst = out[bass.ds(bh + hh, 1), k * HD:(k + 1) * HD, t0:t0 + HALF]
                                        dst = dst.rearrange("o d t -> (o d) t")
                                    else:
                                        dst = out[bass.ds(bh + hh, 1), k, :, t0:t0 + HALF].rearrange("o d t -> (o d) t")
                                    sp.dma_start(dst, f32(tile[hh * HD:(hh + 1) * HD, q])).then_inc(stored[q], 16)
                        if LN:
                            layernorm(2 * i + b, G - 1, last and b == 1)

                with sp.Fori(0, NB // 2 - 1) as i:
                    store(i, False)
                store(NB // 2 - 1, True)
                for q in range(2):
                    sp.wait_ge(stored[q], 16 * STORES * NB * G // 2)
                    if LN:
                        sp.wait_ge(xT_stored[q], 16 * LN * NB // 2)

            @block.scalar
            def _(act):
                def split(t, b, n):
                    act.wait_ge(a_in[b], 16 * (n + 1))
                    if not (isinstance(t, int) and t < 2):
                        act.wait_ge(product_done, (t - 1) * G)
                    nc.scalar.copy(a_hi[:, b], a_raw[:, b]).then_inc(a_hi_done, 1)

                def evacuate(t, b):
                    for g in range(G):
                        n, q = t * G + g, g % 2
                        act.wait_ge(stored[q], 16 * STORES * (t * (G // 2) + g // 2))
                        if kind == "v":
                            act.wait_ge(v32_done, n + 1)
                            nc.scalar.copy(o[:, q, :, 0], v32[:, q].rearrange("p (h d) -> p h d", d=HD)).then_inc(o_hi_done, 1)
                        else:
                            act.wait_ge(product_done, n + 1)
                            nc.scalar.activation(o_hi[:, q], acc[:, g % BANKS], ACT.Identity,
                                                 bias=bias_sb[:, g:g + 1]).then_inc(o_hi_done, 1)
                        if LN and g % 2 == 0:
                            act.wait_ge(mv_done, LN * t + g // 2 + 1)
                            b_x = g // 2 % 2
                            nc.scalar.activation(std[:, b_x], mv[:, b_x, 1:2], ACT.Sqrt, bias=eps[:]).then_inc(std_done, 1)
                        if LN and g % 2:
                            j = g // 2
                            act.wait_ge(t_done, LN * t + j + 1)
                            act.wait_ge(xT_stored[j % 2], 16 * (LN // 2 * t + j // 2))
                            nc.scalar.copy(xT[:, j % 2], tps[:, j % 2]).then_inc(xT_done, 1)

                for c in range(C):
                    act.wait_ge(w_in[c % RAW], 16 * (c // RAW + 1))
                    nc.scalar.copy(w_hi[:, c], w_raw[:, c % RAW]).then_inc(w_hi_done, 1)
                    if c == 1:
                        split(0, 0, 0)
                if LN:
                    act.wait_ge(eps_ready, 1)
                act.wait_ge(bias_in, 16)
                with act.Fori(0, NB // 2 - 1) as i:
                    split(2 * i + 1, 1, i)
                    evacuate(2 * i, 0)
                    split(2 * i + 2, 0, i + 1)
                    evacuate(2 * i + 1, 1)
                split(NB - 1, 1, NB // 2 - 1)
                evacuate(NB - 2, 0)
                evacuate(NB - 1, 1)

            @block.vector
            def _(dve):
                def split(t, b):
                    dve.wait_ge(a_hi_done, t + 1)
                    nc.vector.tensor_tensor(a_lo[:, b], a_raw[:, b], f32(a_hi[:, b]), ALU.subtract).then_inc(a_lo_done, 1)

                def evacuate(t, b):
                    for g in range(G):
                        n, q = t * G + g, g % 2
                        if kind == "v":
                            half = g % (H // HALF)
                            dve.wait_ge(product_done, n + 1)
                            nc.vector.tensor_tensor(v32[:, q], acc[:, g % BANKS],
                                                    bias_sb[:, half * HALF:(half + 1) * HALF], ALU.add).then_inc(v32_done, 1)
                            dve.wait_ge(o_hi_done, n + 1)
                            nc.vector.tensor_tensor(o[:, q, :, 1], v32[:, q].rearrange("p (h d) -> p h d", d=HD),
                                                    f32(o[:, q, :, 0]), ALU.subtract).then_inc(o_lo_done, 1)
                        else:
                            dve.wait_ge(o_hi_done, n + 1)
                            nc.vector.scalar_tensor_tensor(
                                out=o_lo[:, q], in0=acc[:, g % BANKS], scalar=bias_sb[:, g:g + 1], in1=f32(o_hi[:, q]),
                                op0=ALU.add, op1=ALU.subtract).then_inc(o_lo_done, 1)
                        if LN and g % 2 == 0:
                            layernorm(t, g // 2)

                def layernorm(t, j):
                    n, b = LN * t + j, j % 2
                    dve.wait_ge(x_in[b], 16 * (LN // 2 * t + j // 2 + 1))
                    for k in range(HV):
                        nc.vector.bn_stats(stats[:, b, k], xin[:, b, k * HALF:(k + 1) * HALF]).then_inc(stats_done, 1)
                    dve.wait_ge(stats_done, HV * (n + 1))
                    dve.sem_inc(stats_passed, 1)
                    nc.vector.bn_aggr(mv[:, b], stats[:, b]).then_inc(mv_done, 1)
                    dve.wait_ge(std_done, n + 1)
                    nc.vector.reciprocal(rstd[:, b], std[:, b]).then_inc(rstd_done, 1)
                    dve.wait_ge(rstd_done, n + 1)
                    dve.wait_ge(t_done, ln_before(t, j))
                    nc.vector.tensor_scalar(xn[:, b], xin[:, b], mv[:, b, 0:1], rstd[:, b],
                                            ALU.subtract, ALU.mult).then_inc(xn_done, 1)

                for c in range(C):
                    dve.wait_ge(w_hi_done, c + 1)
                    nc.vector.tensor_tensor(w_lo[:, c], w_raw[:, c % RAW], f32(w_hi[:, c]), ALU.subtract).then_inc(w_lo_done, 1)
                    if c == 1:
                        split(0, 0)
                if LN:
                    nc.vector.memset(eps[:], EPS).then_inc(eps_ready, 1)
                dve.wait_ge(bias_in, 16)
                with dve.Fori(0, NB // 2 - 1) as i:
                    split(2 * i + 1, 1)
                    evacuate(2 * i, 0)
                    split(2 * i + 2, 0)
                    evacuate(2 * i + 1, 1)
                split(NB - 1, 1)
                evacuate(NB - 2, 0)
                evacuate(NB - 1, 1)

            @block.tensor
            def _(pe):
                def tiles(t, b, first):
                    pe.wait_ge(a_lo_done, t + 1)
                    for g in range(G):
                        if not first or g >= BANKS:
                            pe.wait_ge(o_lo_done, t * G + g - BANKS + 1)
                        for c in range(C):
                            if first and g == 0:
                                pe.wait_ge(w_lo_done, c + 1)
                            if kind == "v":
                                r, half = g // (H // HALF), g % (H // HALF)
                                hi, lo = (a[:, b, c, r * P:(r + 1) * P] for a in (a_hi, a_lo))
                                mhi, mlo = (w[:, c, half * HALF:(half + 1) * HALF] for w in (w_hi, w_lo))
                            else:
                                hi, lo = (w[:, c, g * P:(g + 1) * P] for w in (w_hi, w_lo))
                                mhi, mlo = a_hi[:, b, c], a_lo[:, b, c]
                            o_ = acc[:, g % BANKS]
                            nc.tensor.matmul(o_, hi, mhi, start=(c == 0), stop=False)
                            nc.tensor.matmul(o_, hi, mlo, start=False, stop=False)
                            last = nc.tensor.matmul(o_, lo, mhi, start=False, stop=(c == C - 1))
                        last.then_inc(product_done, 1)
                        if LN and g % 2:
                            j = g // 2
                            pe.wait_ge(xn_done, LN * t + j + 1)
                            pe.wait_ge(xT_done, ln_before(t, j))
                            for c in range(C):
                                last = nc.tensor.transpose(tps[:, j % 2, c], xn[:, j % 2, c * P:(c + 1) * P], ident[:])
                            last.then_inc(t_done, 1)

                if LN:
                    pe.wait_ge(ident_ready, 1)
                tiles(0, 0, True)
                tiles(1, 1, False)
                with pe.Fori(1, NB // 2) as i:
                    tiles(2 * i, 0, False)
                    tiles(2 * i + 1, 1, False)


def attention_pass(nc, kst, qst, vst, mask, ctxst, sums, B, S):
    NHB = kst.shape[0]
    NH, C, HV = NHB // B, S // P, S // HALF
    NPAIR = NHB // 2
    with ExitStack() as st:
        s = Scope(nc, st, "att")
        kt = s.sb("kt", [P, 2, S], F32R)
        qh, ql = s.sb("qh", [P, 2, S], F32R), s.sb("ql", [P, 2, S], F32R)
        v = s.sb("v", [P, 2, C, 4 * HD], F32R)
        e32, p32 = s.sb("e32", [P, 2, S]), s.sb("p32", [P, 2, S])
        p_hi, p_lo = s.sb("p_hi", [P, 2, S], F32R), s.sb("p_lo", [P, 2, S], F32R)
        c32 = s.sb("c32", [P, 2, S])
        m_int, m32, upper = s.sb("m_int", [P, B, C], I32), s.sb("m32", [P, B, C]), s.sb("upper", [P, B, C])
        sc = s.ps("sc", [P, 2, S])
        o = s.ps("o", [P, 2, S])
        kq_in = [s.sem(f"kq_in{i}") for i in range(2)]
        v_in = [s.sem(f"v_in{i}") for i in range(2)]
        mask_in, m_done, upper_ready, const_ready = s.sem("mask_in"), s.sem("m_done"), s.sem("upper_ready"), s.sem("const_ready")
        scores_done, exp_done, clip_done, hi_done, lo_done = s.sem("scores_done"), s.sem("exp_done"), s.sem("clip_done"), s.sem("hi_done"), s.sem("lo_done")
        values_done, c_done = s.sem("values_done"), s.sem("c_done")
        stored = [s.sem(f"stored{i}") for i in range(2)]
        U = 2 * C
        AHEAD = 3
        vst_v = vst.rearrange("(b c p) h d -> b p c h d", b=B, p=P)

        def stationary(b, c, k):
            return v[:, b, c, 2 * k * HD:2 * (k + 1) * HD]

        with nc.Block() as block:
            @block.sync
            def _(sp):
                sp.dma_start(m_int[:], mask).then_inc(mask_in, 16)

                def load(i, bt):
                    for b in range(2):
                        bh = bt * NH + 2 * i + b
                        reused = not (isinstance(bh, int) and bh < 2)
                        if reused:
                            sp.wait_ge(scores_done, (bh - 1) * C)
                        sp.dma_start(f32(kt[:, b]), kst[bass.ds(bh, 1)].rearrange("o p t -> (o p) t")).then_inc(kq_in[b], 16)
                        for k, q in enumerate((qh, ql)):
                            for r in range(2):
                                sp.dma_start(f32(q[r * HD:(r + 1) * HD, b]),
                                             qst[bass.ds(bh, 1), k].rearrange("o p t -> (o p) t")).then_inc(kq_in[b], 16)
                        if reused:
                            sp.wait_ge(values_done, (bh - 1) * C)
                        for k in range(2):
                            src = vst_v[bt, :, :, bass.ds(2 * i + b, 1), k * HD:(k + 1) * HD]
                            sp.dma_start(f32(v[:, b, :, (2 * k + b) * HD:(2 * k + b + 1) * HD]),
                                         src.rearrange("p c o d -> p c (o d)")).then_inc(v_in[b], 16)

                load(0, 0)
                for bt in range(B):
                    with sp.Fori(0 if bt else 1, NH // 2) as i:
                        load(i, bt)

            @block.gpsimd
            def _(pool):
                for bt in range(B):
                    with pool.Fori(0, NH // 2) as i:
                        for b in range(2):
                            head = bt * NH + 2 * i + b
                            pool.wait_ge(c_done, head + 1)
                            pool.dma_start(ctxst[bass.ds((2 * i + b) * HD, HD), bt * S:(bt + 1) * S],
                                           c32[b * HD:(b + 1) * HD, b]).then_inc(stored[b], 16)
                            other = (1 - b) * HD
                            pool.dma_start(sums[bass.ds(2 * i + b, 1), bt * S:(bt + 1) * S], c32[other:other + 1, b]).then_inc(stored[b], 16)
                for b in range(2):
                    pool.wait_ge(stored[b], 32 * NPAIR)

            def pairs(eng, body):
                n = NH // 2
                body(0, 0, 0, True)
                for bt in range(B):
                    first = 0 if bt else 1
                    if n - 1 > first:
                        with eng.Fori(first, n - 1) as i:
                            body(bt * n + i, bt, bt, False)
                    body(bt * n + n - 1, bt, bt + 1 if bt < B - 1 else None, False)

            @block.tensor
            def _(pe):
                def scores(pair, u):
                    b, c = (u % U) // C, u % C
                    if c == 0:
                        pe.wait_ge(kq_in[b], 5 * 16 * (pair + 1))
                    n = pair * U + u
                    if not (isinstance(n, int) and n < 2):
                        pe.wait_ge(exp_done, n - 1)
                    for h in range(HV):
                        cols = slice(h * HALF, (h + 1) * HALF)
                        nc.tensor.matmul(sc[:, u % 2, cols], kt[:, b, c * P:(c + 1) * P], qh[:, b, cols], start=True, stop=False)
                        last = nc.tensor.matmul(sc[:, u % 2, cols], kt[:, b, c * P:(c + 1) * P], ql[:, b, cols], start=False, stop=True)
                    last.then_inc(scores_done, 1)

                def values(pair, u, first):
                    b, c = u // C, u % C
                    if c == 0:
                        pe.wait_ge(v_in[b], 32 * (pair + 1))
                        if not first:
                            pe.wait_ge(c_done, 2 * pair + b - 1)
                    pe.wait_ge(lo_done, pair * U + u + 1)
                    for h in range(HV):
                        cols = slice(h * HALF, (h + 1) * HALF)
                        nc.tensor.matmul(o[:, b, cols], stationary(b, c, 0), p_hi[:, u % 2, cols], start=(c == 0), stop=False)
                        nc.tensor.matmul(o[:, b, cols], stationary(b, c, 0), p_lo[:, u % 2, cols], start=False, stop=False)
                        last = nc.tensor.matmul(o[:, b, cols], stationary(b, c, 1), p_hi[:, u % 2, cols], start=False, stop=(c == C - 1))
                    last.then_inc(values_done, 1)

                pe.wait_ge(const_ready, 1)
                for u in range(AHEAD):
                    scores(0, u)

                def body(pair, bt, next_bt, first):
                    for u in range(U):
                        if u + AHEAD < U:
                            scores(pair, u + AHEAD)
                        elif next_bt is not None:
                            scores(pair + 1, u + AHEAD - U)
                        values(pair, u, first)
                pairs(pe, body)

            @block.scalar
            def _(act):
                def exponential(n, u):
                    act.wait_ge(scores_done, n + 1)
                    if not (isinstance(n, int) and n < 2):
                        act.wait_ge(clip_done, n - 1)
                    nc.scalar.activation(e32[:, u % 2], sc[:, u % 2], ACT.Exp, scale=1.0 / math.sqrt(HD)).then_inc(exp_done, 1)

                def high(n, u):
                    act.wait_ge(clip_done, n + 1)
                    if not (isinstance(n, int) and n < 2):
                        act.wait_ge(values_done, n - 1)
                    nc.scalar.copy(p_hi[:, u % 2], p32[:, u % 2]).then_inc(hi_done, 1)

                exponential(0, 0)

                def body(pair, bt, next_bt, first):
                    for u in range(U):
                        n = pair * U + u
                        if u < U - 1 or next_bt is not None:
                            exponential(n + 1, u + 1)
                        high(n, u)
                pairs(act, body)

            @block.vector
            def _(dve):
                def clip(n, u, bt):
                    dve.wait_ge(exp_done, n + 1)
                    if not (isinstance(n, int) and n < 2):
                        dve.wait_ge(lo_done, n - 1)
                    nc.vector.tensor_scalar(p32[:, u % 2], e32[:, u % 2], math.exp(-CLIP), upper[:, bt, u % C:u % C + 1],
                                            ALU.max, ALU.min).then_inc(clip_done, 1)

                def low(n, u):
                    dve.wait_ge(hi_done, n + 1)
                    nc.vector.tensor_tensor(p_lo[:, u % 2], p32[:, u % 2], f32(p_hi[:, u % 2]), ALU.subtract).then_inc(lo_done, 1)

                def context(pair, b):
                    dve.wait_ge(values_done, (2 * pair + b + 1) * C)
                    dve.wait_ge(stored[b], 32 * pair)
                    nc.vector.tensor_copy(c32[:, b], o[:, b]).then_inc(c_done, 1)

                for b in range(2):
                    z = (1 - b) * HD
                    nc.vector.memset(f32(v[:, b, :, z:z + HD]), float(np.float32(1.0 + 1e-8)))
                    last = nc.vector.memset(f32(v[:, b, :, z + 2 * HD:z + 3 * HD]), 0.0)
                last.then_inc(const_ready, 1)
                dve.wait_ge(mask_in, 16)
                nc.vector.tensor_copy(m32[:], m_int[:]).then_inc(m_done, 1)
                dve.wait_ge(m_done, 1)
                nc.vector.tensor_scalar(m32[:], m32[:], 0.5, math.exp(CLIP), ALU.is_gt, ALU.mult).then_inc(m_done, 1)
                dve.wait_ge(m_done, 2)
                nc.vector.tensor_scalar(upper[:], m32[:], math.exp(-CLIP), None, ALU.max).then_inc(upper_ready, 1)
                dve.wait_ge(upper_ready, 1)
                clip(0, 0, 0)

                def body(pair, bt, next_bt, first):
                    for u in range(U):
                        n = pair * U + u
                        if u + 1 < U:
                            clip(n + 1, u + 1, bt)
                        elif next_bt is not None:
                            clip(n + 1, 0, next_bt)
                        low(n, u)
                        if u == 2 and not first:
                            context(pair - 1, 1)
                        if u == C + 2:
                            context(pair, 0)

                pairs(dve, body)
                context(NPAIR - 1, 1)


def reciprocal_pass(nc, sums, rsums):
    with ExitStack() as st:
        s = Scope(nc, st, "rec")
        n = sums.shape[0] * sums.shape[1] // P
        t, r = s.sb("t", [P, n]), s.sb("r", [P, n])
        loaded, inverted, stored = s.sem("loaded"), s.sem("inverted"), s.sem("stored")
        src = sums.rearrange("h (k n) -> (h k) n", n=n)
        dst = rsums.rearrange("h (k n) -> (h k) n", n=n)
        with nc.Block() as block:
            @block.sync
            def _(sp):
                sp.dma_start(t[:], src).then_inc(loaded, 16)
                sp.wait_ge(inverted, 1)
                sp.dma_start(dst, r[:]).then_inc(stored, 16)
                sp.wait_ge(stored, 16)

            @block.vector
            def _(dve):
                dve.wait_ge(loaded, 16)
                nc.vector.reciprocal(r[:], t[:]).then_inc(inverted, 1)


def directory(E):
    n_at, base_at, last_at, row_at = 0, E, 2 * E, 2 * E + 1
    return n_at, base_at, last_at, row_at


def table_regions(E):
    return E + 4


def output_pass(nc, ctxst, rsums, woT, bo, gamma, beta, rscale, x, gateT, acc, h2st, table, dirst):
    H, T = ctxst.shape
    C, NT, E, HV = H // P, T // P, gateT.shape[1], H // HALF
    NCOL = 3
    n_at, base_at, last_at, row_at = directory(E)
    with ExitStack() as st:
        s = Scope(nc, st, "out")
        w_raw = s.sb("w_raw", [P, 4, H])
        w_hi, w_lo = s.sb("w_hi", [P, C, H], F32R), s.sb("w_lo", [P, C, H], F32R)
        c_raw, r_t, cn = s.sb("c_raw", [P, 2, C, P]), s.sb("r_t", [P, 2, C, P]), s.sb("cn", [P, 2, C, P])
        c_hi, c_lo = s.sb("c_hi", [P, 2, C, P], F32R), s.sb("c_lo", [P, 2, C, P], F32R)
        x_t, d, x1, h2 = s.sb("x_t", [P, 2, H]), s.sb("d", [P, 2, H]), s.sb("x1", [P, 2, H]), s.sb("h2", [P, 2, H])
        scaled, normed, h2T = s.sb("scaled", [P, H]), s.sb("normed", [P, H]), s.sb("h2T", [P, C, P])
        gamma_sb, beta_sb, gate_sb = s.sb("gamma", [P, H]), s.sb("beta", [P, H]), s.sb("gate", [P, C, E])
        bo_row = s.sb("bo_row", [1, H])
        bo_hi, bo_lo = s.sb("bo_hi", [1, H], F32R), s.sb("bo_lo", [1, H], F32R)
        rs_raw, rs_sb, eps = s.sb("rs_raw", [P, 1]), s.sb("rs", [P, 1]), s.sb("eps", [P, 1])
        ident, ones, before = s.sb("ident", [P, P]), s.sb("ones", [P, P]), s.sb("before", [P, P])
        ones_row = s.sb("ones_row", [1, P], F32R)
        stats, mv, std, rstd = s.sb("stats", [P, 2, HV, 6]), s.sb("mv", [P, 2, 2]), s.sb("std", [P, 2, 1]), s.sb("rstd", [P, 2, 1])
        logits, top, top_i, top_f, diff = s.sb("logits", [P, E]), s.sb("top", [P, TOPK]), s.sb("top_i", [P, TOPK], U32), s.sb("top_f", [P, TOPK]), s.sb("diff", [P, TOPK])
        e8, esum, rsum, iota_e, rowbase = s.sb("e8", [P, TOPK]), s.sb("esum", [P, 1]), s.sb("rsum", [P, 1]), s.sb("iota_e", [P, E]), s.sb("rowbase", [P, E])
        onehot, prod = s.sb("onehot", [P, 2, TOPK, E]), s.sb("prod", [P, TOPK, E])
        mask, seen = s.sb("mask", [P, 2, E]), s.sb("seen", [P, 2, E])
        token, slot_f, slot = s.sb("token", [P, 1]), s.sb("slot_f", [P, TOPK]), s.sb("slot", [P, 2, TOPK], I32)
        row_e, record = s.sb("row_e", [P, E]), s.sb("record", [P, 2, TOPK, 2])
        fill, zeros = s.sb("fill", [P, P, 2]), s.sb("zeros", [P, H])
        tile_id, cmp, started = s.sb("tile_id", [P, NCOL]), s.sb("cmp", [P, NCOL, E]), s.sb("started", [P, NCOL])
        first_of, row_f, row_i = s.sb("first_of", [P, NCOL]), s.sb("row_f", [P, NCOL]), s.sb("row_i", [P, NCOL], I32)
        cnt, tiles_i, tiles_f, upto, base = s.sb("cnt", [P, E]), s.sb("tiles_i", [P, E], I32), s.sb("tiles_f", [P, E]), s.sb("upto", [P, E]), s.sb("base", [P, E])
        dir_sb = s.sb("dir", [1, row_at + 1], I32)
        o = s.ps("o", [P, 2, H])
        tps, lps, pps = s.ps("tps", [P, C, P]), s.ps("lps", [P, HALF]), s.ps("pps", [P, HALF])

        w_in = [s.sem(f"w_in{i}") for i in range(4)]
        c_in, x_in = [s.sem(f"c_in{i}") for i in range(2)], [s.sem(f"x_in{i}") for i in range(2)]
        consts_in, set_up, filled = s.sem("consts_in"), s.sem("set_up"), s.sem("filled")
        masks_ready, rs_ready, bo_ready, fill_ready = s.sem("masks_ready"), s.sem("rs_ready"), s.sem("bo_ready"), s.sem("fill_ready")
        w_hi_done, w_lo_done = s.sem("w_hi_done"), s.sem("w_lo_done")
        cn_done, c_hi_done, c_lo_done, gemm_done, d_done = s.sem("cn_done"), s.sem("c_hi_done"), s.sem("c_lo_done"), s.sem("gemm_done"), s.sem("d_done")
        norm_step, mv_ready, std_ready, x1_done, h2_done = s.sem("norm_step"), s.sem("mv_ready"), s.sem("std_ready"), s.sem("x1_done"), s.sem("h2_done")
        t_done, h2T_done, logits_done, diff_done, e8_done = s.sem("t_done"), s.sem("h2T_done"), s.sem("logits_done"), s.sem("diff_done"), s.sem("e8_done")
        route_step, mask_done, record_done, pos_done, slot_step, slot_done = s.sem("route_step"), s.sem("mask_done"), s.sem("record_done"), s.sem("pos_done"), s.sem("slot_step"), s.sem("slot_done")
        stored, scattered = [s.sem(f"stored{i}") for i in range(2)], [s.sem(f"scattered{i}") for i in range(2)]
        pool_passed, dve_passed = s.sem("pool_passed"), s.sem("dve_passed")
        seen_ready, seen_done = s.sem("seen_ready"), s.sem("seen_done")
        count_done, dir_step, dir_done, dir_stored = s.sem("count_done"), s.sem("dir_step"), s.sem("dir_done"), s.sem("dir_stored")

        ctx_v = ctxst.rearrange("(c p) t -> p c t", p=P)
        r_v = rsums.rearrange("(c k) t -> k c t", k=2)
        REGIONS = table_regions(E)
        FILLS = REGIONS * REGION // (P * P)
        CONSTS = 5

        def known(v):
            return isinstance(v, int)

        def tiles(eng, body):
            body(0, 0, 0, True, True, False, False, False)
            body(1, 1, 0, True, True, True, False, False)
            body(2, 0, 1, True, True, True, True, False)
            body(3, 1, 1, True, True, True, True, True)
            with eng.Fori(2, NT // 2 - 1) as h:
                body(2 * h, 0, h, True, True, True, True, True)
                body(2 * h + 1, 1, h, True, True, True, True, True)
            n = NT // 2
            body(NT - 2, 0, n - 1, True, True, True, True, True)
            body(NT - 1, 1, n - 1, True, False, True, True, True)
            body(NT, 0, n, False, False, True, True, True)
            body(NT + 1, 1, n, False, False, False, True, True)
            body(NT + 2, 0, n + 1, False, False, False, False, True)

        with nc.Block() as block:
            @block.sync
            def _(sp):
                def load_context(i, b):
                    sp.dma_start(c_raw[:, b], ctx_v[:, :, bass.ds(i * P, P)]).then_inc(c_in[b], 16)
                    for k in range(2):
                        src = r_v[k, :, bass.ds(i * P, P)].partition_broadcast(HD)
                        sp.dma_start(r_t[k * HD:(k + 1) * HD, b], src).then_inc(c_in[b], 16)

                def load_x(i, b):
                    sp.dma_start(x_t[:, b], x[bass.ds(i * P, P), :]).then_inc(x_in[b], 16)

                for b in range(2):
                    load_context(b, b)
                    load_x(b, b)
                for c in range(C):
                    if c >= 4:
                        sp.wait_ge(w_lo_done, c - 3)
                    sp.dma_start(w_raw[:, c % 4], woT[c * P:(c + 1) * P, :]).then_inc(w_in[c % 4], 16)

                sp.wait_ge(cn_done, 1)
                load_context(2, 0)

                def body(i, b, more_context, more):
                    if more_context:
                        sp.wait_ge(cn_done, i + 2)
                        load_context(i + 3, 1 - b)
                    sp.wait_ge(x1_done, i + 1)
                    if more:
                        load_x(i + 2, b)
                    sp.dma_start(acc[bass.ds(i * P, P), :], x1[:, b]).then_inc(stored[b], 16)
                    sp.wait_ge(h2_done, i + 1)
                    sp.dma_start(h2st[bass.ds(i * P, P), :], h2[:, b]).then_inc(stored[b], 16)

                with sp.Fori(0, NT // 2 - 2) as h:
                    body(2 * h, 0, True, True)
                    body(2 * h + 1, 1, True, True)
                body(NT - 4, 0, True, True)
                body(NT - 3, 1, False, True)
                body(NT - 2, 0, False, False)
                body(NT - 1, 1, False, False)
                for b in range(2):
                    sp.wait_ge(stored[b], 32 * (NT // 2))
                sp.wait_ge(dir_done, 1)
                sp.dma_start(dirst[0:1, 0:row_at + 1], dir_sb[:]).then_inc(dir_stored, 16)
                for k in range(NCOL):
                    at = row_at + 1 + k * P
                    sp.dma_start(dirst[0:1, at:at + P].rearrange("o (p q) -> (o p) q", q=1), row_i[:, k:k + 1]).then_inc(dir_stored, 16)
                sp.wait_ge(dir_stored, 16 * (NCOL + 1))

            @block.gpsimd
            def _(pool):
                nc.gpsimd.memset(ident[:], 0.0).then_inc(set_up, 1)
                nc.gpsimd.memset(before[:], 1.0).then_inc(set_up, 1)
                nc.gpsimd.memset(ones[:], 1.0).then_inc(masks_ready, 1)
                nc.gpsimd.memset(f32(ones_row[:]), 1.0).then_inc(masks_ready, 1)
                nc.gpsimd.memset(fill[:], 0.0).then_inc(set_up, 1)
                nc.gpsimd.memset(zeros[:], 0.0).then_inc(fill_ready, 1)
                pool.wait_ge(set_up, 3)
                nc.gpsimd.affine_select(out=ident[:], in_=ident[:], compare_op=ALU.not_equal, fill=1.0, base=0,
                                        pattern=[[-1, P]], channel_multiplier=1).then_inc(masks_ready, 1)
                nc.gpsimd.affine_select(out=before[:], in_=before[:], compare_op=ALU.is_gt, fill=0.0, base=0,
                                        pattern=[[1, P]], channel_multiplier=-1).then_inc(masks_ready, 1)
                nc.gpsimd.iota(iota_e[:], pattern=[[1, E]], base=0, channel_multiplier=0,
                               allow_small_or_imprecise_dtypes=True).then_inc(masks_ready, 1)
                nc.gpsimd.iota(token[:], pattern=[[0, 1]], base=0, channel_multiplier=1,
                               allow_small_or_imprecise_dtypes=True).then_inc(masks_ready, 1)
                nc.gpsimd.iota(tile_id[:], pattern=[[P, NCOL]], base=0, channel_multiplier=1,
                               allow_small_or_imprecise_dtypes=True).then_inc(masks_ready, 1)
                nc.gpsimd.iota(fill[:].bitcast(I32)[:, :, 0], pattern=[[1, P]], base=T, channel_multiplier=0).then_inc(fill_ready, 1)
                for dst, src in ((gamma_sb, row_broadcast(gamma, H)), (beta_sb, row_broadcast(beta, H)),
                                 (gate_sb, gateT.rearrange("(c p) e -> p c e", p=P)), (bo_row, bo),
                                 (rs_raw, rscale.broadcast_to([P, 1]))):
                    pool.dma_start(dst[:], src).then_inc(consts_in, 16)
                pool.wait_ge(fill_ready, 2)
                for k in range(FILLS):
                    rows = table[k * P * P:(k + 1) * P * P, :].rearrange("(p r) w -> p (r w)", p=P)
                    pool.dma_start(rows, fill[:].rearrange("p r w -> p (r w)")).then_inc(filled, 16)
                for dst in (acc, h2st):
                    pool.dma_start(dst[T:T + P, :], zeros[:]).then_inc(filled, 16)
                pool.wait_ge(filled, 16 * (FILLS + 2))

                def scatter(j, b):
                    pool.wait_ge(slot_done, j + 1)
                    pool.sem_inc(pool_passed, 1)
                    for k in range(TOPK):
                        nc.gpsimd.indirect_dma_start(
                            out=table[:, :], out_offset=bass.IndirectOffsetOnAxis(ap=slot[:, b, k:k + 1], axis=0),
                            in_=record[:, b, k, :], in_offset=None).then_inc(scattered[b], 16)

                with pool.Fori(0, NT // 2) as h:
                    scatter(2 * h, 0)
                    scatter(2 * h + 1, 1)
                for b in range(2):
                    pool.wait_ge(scattered[b], 16 * TOPK * (NT // 2))

            @block.tensor
            def _(pe):
                pe.wait_ge(masks_ready, 7)
                pe.wait_ge(bo_ready, 2)
                pe.wait_ge(consts_in, 16 * CONSTS)

                def product(i, b, first):
                    pe.wait_ge(c_lo_done, i + 1)
                    if not (known(i) and i < 2):
                        pe.wait_ge(d_done, i - 1)
                    for h in range(HV):
                        cols = slice(h * HALF, (h + 1) * HALF)
                        for c in range(C):
                            if first and h == 0:
                                pe.wait_ge(w_lo_done, c + 1)
                            nc.tensor.matmul(o[:, b, cols], c_hi[:, b, c], w_hi[:, c, cols], start=(c == 0), stop=False)
                            nc.tensor.matmul(o[:, b, cols], c_hi[:, b, c], w_lo[:, c, cols], start=False, stop=False)
                            nc.tensor.matmul(o[:, b, cols], c_lo[:, b, c], w_hi[:, c, cols], start=False, stop=False)
                        nc.tensor.matmul(o[:, b, cols], ones_row[:], bo_hi[:, cols], start=False, stop=False)
                        last = nc.tensor.matmul(o[:, b, cols], ones_row[:], bo_lo[:, cols], start=False, stop=True)
                    last.then_inc(gemm_done, 1)

                def route(j, b):
                    pe.wait_ge(h2_done, j + 1)
                    for c in range(C):
                        last = nc.tensor.transpose(tps[:, c], h2[:, b, c * P:(c + 1) * P], ident[:])
                    last.then_inc(t_done, 1)
                    pe.wait_ge(h2T_done, j + 1)
                    for c in range(C):
                        last = nc.tensor.matmul(lps[:, 0:E], h2T[:, c], gate_sb[:, c], start=(c == 0), stop=(c == C - 1))
                    last.then_inc(logits_done, 1)

                def positions(j, b):
                    pe.wait_ge(mask_done, j + 1)
                    nc.tensor.matmul(pps[:, 0:E], before[:], mask[:, b], start=True, stop=False)
                    nc.tensor.matmul(pps[:, 0:E], ones[:], seen[:, b], start=False, stop=True).then_inc(pos_done, 1)

                def body(i, b, n, gemm, more, norm, router, slots):
                    if slots:
                        positions(i - 3, 1 - b)
                    if router:
                        route(i - 2, b)
                    if gemm:
                        product(i, b, known(i) and i == 0)
                tiles(pe, body)
                pe.wait_ge(slot_done, NT)
                nc.tensor.matmul(pps[:, 0:E], ones[:], seen[:, NT % 2], start=True, stop=True).then_inc(count_done, 1)

            @block.scalar
            def _(act):
                for c in range(C):
                    act.wait_ge(w_in[c % 4], 16 * (c // 4 + 1))
                    nc.scalar.copy(w_hi[:, c], w_raw[:, c % 4]).then_inc(w_hi_done, 1)
                    if c == 1:
                        act.wait_ge(cn_done, 1)
                        nc.scalar.copy(c_hi[:, 0], cn[:, 0]).then_inc(c_hi_done, 1)
                act.wait_ge(consts_in, 16 * CONSTS)
                nc.scalar.copy(bo_hi[:], bo_row[:]).then_inc(bo_ready, 1)
                act.wait_ge(rs_ready, 2)

                def body(i, b, n, gemm, more, norm, router, slots):
                    if router:
                        act.wait_ge(t_done, i - 1)
                        nc.scalar.copy(h2T[:], tps[:]).then_inc(h2T_done, 1)
                    if more:
                        act.wait_ge(cn_done, i + 2)
                        if not (known(i) and i < 1):
                            act.wait_ge(gemm_done, i)
                        nc.scalar.copy(c_hi[:, 1 - b], cn[:, 1 - b]).then_inc(c_hi_done, 1)
                    if router:
                        act.wait_ge(diff_done, i - 1)
                        nc.scalar.activation(e8[:], diff[:], ACT.Exp, accum_out=esum[:]).then_inc(e8_done, 1)
                    if norm:
                        for k in range(2):
                            act.wait_ge(mv_ready, 2 * i + k - 1)
                            nc.scalar.activation(std[:, k], mv[:, k, 1:2], ACT.Sqrt, bias=eps[:]).then_inc(std_ready, 1)
                    if gemm:
                        act.wait_ge(gemm_done, i + 1)
                        if not (known(i) and i < 2):
                            act.wait_ge(x1_done, i - 1)
                        nc.scalar.activation(d[:, b], o[:, b], ACT.Copy, scale=rs_sb[:]).then_inc(d_done, 1)
                tiles(act, body)

            @block.vector
            def _(dve):
                def divide(b, n):
                    dve.wait_ge(c_in[b], 48 * (n + 1))
                    nc.vector.tensor_tensor(cn[:, b], c_raw[:, b], r_t[:, b], ALU.mult).then_inc(cn_done, 1)

                def context_low(i, b):
                    dve.wait_ge(c_hi_done, i + 1)
                    nc.vector.tensor_tensor(c_lo[:, b], cn[:, b], f32(c_hi[:, b]), ALU.subtract).then_inc(c_lo_done, 1)

                def carry_wait():
                    dve.sem_inc(dve_passed, 1)

                NORM_STEPS = 2 * (HV + 1) + 2

                def moments(i, k, src, at):
                    for h in range(HV):
                        nc.vector.bn_stats(stats[:, k, h], src[:, h * HALF:(h + 1) * HALF]).then_inc(norm_step, 1)
                    dve.wait_ge(norm_step, NORM_STEPS * i + at + HV)
                    carry_wait()
                    nc.vector.bn_aggr(mv[:, k], stats[:, k]).then_inc(mv_ready, 1)
                    dve.wait_ge(std_ready, 2 * i + k + 1)
                    nc.vector.reciprocal(rstd[:, k], std[:, k]).then_inc(norm_step, 1)
                    dve.wait_ge(norm_step, NORM_STEPS * i + at + HV + 1)

                def normalize(i, b, x_count):
                    dve.wait_ge(d_done, i + 1)
                    moments(i, 0, d[:, b], 0)
                    nc.vector.scalar_tensor_tensor(out=scaled[:], in0=d[:, b], scalar=mv[:, 0, 0:1], in1=gamma_sb[:],
                                                   op0=ALU.subtract, op1=ALU.mult).then_inc(norm_step, 1)
                    dve.wait_ge(norm_step, NORM_STEPS * i + HV + 2)
                    dve.wait_ge(x_in[b], x_count)
                    nc.vector.scalar_tensor_tensor(out=normed[:], in0=scaled[:], scalar=rstd[:, 0], in1=x_t[:, b],
                                                   op0=ALU.mult, op1=ALU.add).then_inc(norm_step, 1)
                    dve.wait_ge(norm_step, NORM_STEPS * i + HV + 3)
                    if not (known(i) and i < 2):
                        dve.wait_ge(stored[b], 2 * x_count - 32)
                    nc.vector.tensor_tensor(x1[:, b], normed[:], beta_sb[:], ALU.add).then_inc(x1_done, 1)
                    dve.wait_ge(x1_done, i + 1)
                    moments(i, 1, x1[:, b], HV + 3)
                    if not (known(i) and i < 2):
                        dve.wait_ge(t_done, i - 1)
                    nc.vector.tensor_scalar(h2[:, b], x1[:, b], mv[:, 1, 0:1], rstd[:, 1],
                                            ALU.subtract, ALU.mult).then_inc(h2_done, 1)

                ROUTE_STEPS = 6

                def route(j, b, done_before):
                    def step(k):
                        dve.wait_ge(route_step, ROUTE_STEPS * j + k)
                    dve.wait_ge(logits_done, j + 1)
                    nc.vector.tensor_copy(logits[:], lps[:, 0:E]).then_inc(route_step, 1)
                    step(1)
                    carry_wait()
                    nc.vector.max(top[:], logits[:]).then_inc(route_step, 1)
                    step(2)
                    carry_wait()
                    nc.vector.max_index(top_i[:], top[:], logits[:]).then_inc(route_step, 1)
                    nc.vector.tensor_scalar(diff[:], top[:], top[:, 0:1], None, ALU.subtract).then_inc(diff_done, 1)
                    step(3)
                    nc.vector.tensor_copy(top_f[:], top_i[:]).then_inc(route_step, 1)
                    step(4)
                    nc.vector.tensor_tensor(onehot[:, b], top_f[:].unsqueeze(2).broadcast_to([P, TOPK, E]),
                                            iota_e[:].unsqueeze(1).broadcast_to([P, TOPK, E]), ALU.is_equal).then_inc(route_step, 1)
                    step(5)
                    nc.vector.tensor_reduce(mask[:, b], onehot[:, b].rearrange("p k e -> p e k"), AX.X, ALU.add).then_inc(mask_done, 1)
                    dve.wait_ge(mask_done, j + 1)
                    if not (known(j) and j < 1):
                        dve.wait_ge(pos_done, j)
                    nc.vector.tensor_tensor(seen[:, 1 - b], seen[:, b], mask[:, b], ALU.add).then_inc(seen_done, 1)
                    dve.wait_ge(seen_done, j + 1)
                    dve.wait_ge(e8_done, j + 1)
                    nc.vector.reciprocal(rsum[:], esum[:]).then_inc(route_step, 1)
                    step(6)
                    dve.wait_ge(scattered[b], 16 * TOPK * done_before)
                    nc.vector.tensor_scalar(record[:, b, :, 1], e8[:], rsum[:], None, ALU.mult).then_inc(record_done, 1)
                    nc.vector.tensor_copy(record[:].bitcast(I32)[:, b, :, 0], token[:].broadcast_to([P, TOPK])).then_inc(record_done, 1)
                    dve.wait_ge(record_done, 3 * j + 2)
                    nc.vector.tensor_scalar(token[:], token[:], float(P), None, ALU.add).then_inc(record_done, 1)

                def slots(j, b):
                    dve.wait_ge(pos_done, j + 1)
                    nc.vector.tensor_tensor(row_e[:], pps[:, 0:E], rowbase[:], ALU.add).then_inc(slot_step, 1)
                    dve.wait_ge(slot_step, 3 * j + 1)
                    nc.vector.tensor_tensor(prod[:], onehot[:, b], row_e[:].unsqueeze(1).broadcast_to([P, TOPK, E]), ALU.mult).then_inc(slot_step, 1)
                    dve.wait_ge(slot_step, 3 * j + 2)
                    nc.vector.tensor_reduce(slot_f[:], prod[:], AX.X, ALU.add).then_inc(slot_step, 1)
                    dve.wait_ge(slot_step, 3 * j + 3)
                    nc.vector.tensor_copy(slot[:, b], slot_f[:]).then_inc(slot_done, 1)

                nc.vector.memset(eps[:], EPS).then_inc(rs_ready, 1)
                nc.vector.memset(seen[:, 0], 0.0).then_inc(seen_ready, 1)
                dve.wait_ge(c_in[0], 48)
                for c in range(C):
                    if c == 1:
                        divide(0, 0)
                        context_low(0, 0)
                    dve.wait_ge(w_hi_done, c + 1)
                    nc.vector.tensor_tensor(w_lo[:, c], w_raw[:, c % 4], f32(w_hi[:, c]), ALU.subtract).then_inc(w_lo_done, 1)
                dve.wait_ge(consts_in, 16 * CONSTS)
                nc.vector.tensor_scalar(rs_sb[:], rs_raw[:], 0.0, RES_SCALE_MAX, ALU.max, ALU.min).then_inc(rs_ready, 1)
                dve.wait_ge(bo_ready, 1)
                nc.vector.tensor_tensor(bo_lo[:], bo_row[:], f32(bo_hi[:]), ALU.subtract).then_inc(bo_ready, 1)
                dve.wait_ge(masks_ready, 7)
                nc.vector.tensor_scalar(rowbase[:], iota_e[:], float(REGION), float(REGION), ALU.mult, ALU.add).then_inc(seen_ready, 1)
                dve.wait_ge(seen_ready, 2)

                def body(i, b, n, gemm, more, norm, router, slot):
                    if more:
                        divide(1 - b, n + b)
                    if slot:
                        slots(i - 3, 1 - b)
                    if more:
                        context_low(i + 1, 1 - b)
                    if router:
                        route(i - 2, b, n - 1)
                    if norm:
                        normalize(i - 1, 1 - b, 16 * (n + b))
                tiles(dve, body)

                steps = [0]

                def step(instruction):
                    instruction.then_inc(dir_step, 1)
                    steps[0] += 1
                    dve.wait_ge(dir_step, steps[0])

                dve.wait_ge(count_done, 1)
                step(nc.vector.tensor_scalar(cnt[:], pps[:, 0:E], float(P - 1), None, ALU.add))
                step(nc.vector.tensor_copy(tiles_i[:], cnt[:]))
                step(nc.vector.tensor_scalar(tiles_i[:], tiles_i[:], P.bit_length() - 1, None, ALU.arith_shift_right))
                step(nc.vector.tensor_copy(tiles_f[:], tiles_i[:]))
                step(nc.vector.tensor_scalar(tiles_f[:], tiles_f[:], 1.0, None, ALU.max))
                step(nc.vector.tensor_tensor_scan(upto[:], ones[:, 0:E], tiles_f[:], 0.0, ALU.mult, ALU.add))
                step(nc.vector.tensor_tensor(base[:], upto[:], tiles_f[:], ALU.subtract))
                step(nc.vector.tensor_tensor(cmp[:], base[:].unsqueeze(1).broadcast_to([P, NCOL, E]),
                                             tile_id[:].unsqueeze(2).broadcast_to([P, NCOL, E]), ALU.is_le))
                step(nc.vector.tensor_reduce(started[:], cmp[:], AX.X, ALU.add))
                step(nc.vector.tensor_tensor(cmp[:], cmp[:], base[:].unsqueeze(1).broadcast_to([P, NCOL, E]), ALU.mult))
                step(nc.vector.tensor_reduce(first_of[:], cmp[:], AX.X, ALU.max))
                step(nc.vector.tensor_tensor(row_f[:], tile_id[:], first_of[:], ALU.subtract))
                step(nc.vector.tensor_scalar(row_f[:], row_f[:], float(P), None, ALU.mult))
                step(nc.vector.tensor_scalar(started[:], started[:], float(REGION), None, ALU.mult))
                step(nc.vector.tensor_tensor(row_f[:], row_f[:], started[:], ALU.add))
                step(nc.vector.tensor_copy(row_i[:], row_f[:]))
                step(nc.vector.tensor_copy(dir_sb[0:1, n_at:n_at + E], tiles_f[0:1, :]))
                step(nc.vector.tensor_copy(dir_sb[0:1, base_at:base_at + E], base[0:1, :]))
                step(nc.vector.tensor_scalar(dir_sb[0:1, last_at:last_at + 1], upto[0:1, E - 1:E], -1.0, None, ALU.add))
                nc.vector.memset(dir_sb[0:1, row_at:row_at + 1], 0).then_inc(dir_done, 1)


def experts_pass(nc, h2st, table, dirst, w_gate, w_up, w_down, acc):
    E, H, I = w_gate.shape
    C, CI, HV = H // P, I // P, H // HALF
    n_at, base_at, last_at, row_at = directory(E)
    NDIR = dirst.shape[1]
    MAX_TILES = NDIR - row_at - 1
    with ExitStack() as st:
        s = Scope(nc, st, "moe")
        raw_g, raw_u, raw_d = s.sb("raw_g", [P, C, I]), s.sb("raw_u", [P, C, I]), s.sb("raw_d", [P, CI, H])
        gu_hi, gu_lo = s.sb("gu_hi", [P, 2, 2, C, I], F32R), s.sb("gu_lo", [P, 2, 2, C, I], F32R)
        d_hi, d_lo = s.sb("d_hi", [P, 2, CI, H], F32R), s.sb("d_lo", [P, 2, CI, H], F32R)
        tokens, xT_hi, xT_lo = s.sb("tokens", [P, H]), s.sb("xT_hi", [P, C, P], F32R), s.sb("xT_lo", [P, C, P], F32R)
        silu, hidden = s.sb("silu", [P, I]), s.sb("hidden", [P, I])
        hT_hi, hT_lo = s.sb("hT_hi", [P, CI, P], F32R), s.sb("hT_lo", [P, CI, P], F32R)
        y = s.sb("y", [P, H])
        ident, rec_g, rec_s = s.sb("ident", [P, P]), s.sb("rec_g", [P, 2]), s.sb("rec_s", [P, 2])
        dir_sb = s.sb("dir", [1, NDIR], I32)
        gate_ps, up_ps, hT_ps = s.ps("gate", [P, HALF]), s.ps("up", [P, HALF]), s.ps("hT", [P, HALF // P, P])[:, 0:CI]
        xT_ps, y_ps = s.ps("xT", [P, C, P]), s.ps("y", [P, H])

        raw_in = [s.sem(f"raw_in{i}") for i in range(3)]
        dir_in, set_up, ready, pool_passed, sp_passed = s.sem("dir_in"), s.sem("set_up"), s.sem("ready"), s.sem("pool_passed"), s.sem("sp_passed")
        w_hi_done, w_lo_done = s.sem("w_hi_done"), s.sem("w_lo_done")
        rec_g_in, rec_s_in, gathered, added = s.sem("rec_g_in"), s.sem("rec_s_in"), s.sem("gathered"), s.sem("added")
        xT_done, xT_hi_done, xT_lo_done = s.sem("xT_done"), s.sem("xT_hi_done"), s.sem("xT_lo_done")
        gu_done, silu_done, hidden_done = s.sem("gu_done"), s.sem("silu_done"), s.sem("hidden_done")
        hT_done, hT_hi_done, hT_lo_done = s.sem("hT_done"), s.sem("hT_hi_done"), s.sem("hT_lo_done")
        down_done, y_done = s.sem("down_done"), s.sem("y_done")

        def pieces(b):
            for k, raw in enumerate((raw_g, raw_u)):
                for c in range(0, C, 2):
                    yield raw[:, c:c + 2], raw_in[k], gu_hi[:, b, k, c:c + 2], gu_lo[:, b, k, c:c + 2]
            for c in range(CI):
                yield raw_d[:, c], raw_in[2], d_hi[:, b, c], d_lo[:, b, c]
        PIECES = C + CI
        EARLY = 3

        def experts(eng, body):
            with eng.Fori(0, E // 2 - 1) as h:
                body(2 * h, 0, True, True)
                body(2 * h + 1, 1, True, True)
            body(E - 2, 0, True, False)
            body(E - 1, 1, False, False)

        def expert_tiles(eng, e, first_tile, tile):
            n = eng.value_load(dir_sb[0:1, bass.ds(n_at + e, 1)], min_val=1, max_val=REGION // P)
            base = eng.value_load(dir_sb[0:1, bass.ds(base_at + e, 1)], min_val=0, max_val=MAX_TILES)
            first_tile(base)
            with eng.If(n > 1):
                with eng.Fori(1, n) as j:
                    tile(base + j)

        with nc.Block() as block:
            @block.sync
            def _(sp):
                sp.dma_start(dir_sb[:], dirst).then_inc(dir_in, 16)
                sp.wait_ge(dir_in, 16)
                last_tile = sp.value_load(dir_sb[0:1, last_at:last_at + 1], min_val=E - 1, max_val=MAX_TILES - 2)

                def record(dst, t, sem):
                    row = sp.value_load(dir_sb[0:1, bass.ds(row_at + 1 + t, 1)], min_val=0, max_val=table.shape[0] - P)
                    sp.dma_start(dst[:], table[bass.ds(row, P), :]).then_inc(sem, 16)

                record(rec_g, 0, rec_g_in)
                sp.wait_ge(gathered, 16)
                record(rec_g, 1, rec_g_in)
                with sp.Fori(0, last_tile) as t:
                    sp.wait_ge(gathered, 16 * (t + 2))
                    record(rec_g, t + 2, rec_g_in)
                    sp.wait_ge(added, 16 * t)
                    record(rec_s, t - 1, rec_s_in)
                sp.wait_ge(added, 16 * last_tile)
                record(rec_s, last_tile - 1, rec_s_in)
                sp.wait_ge(added, 16 * last_tile + 16)
                record(rec_s, last_tile, rec_s_in)
                sp.wait_ge(added, 16 * last_tile + 32)
                sp.sem_inc(sp_passed, 1)

            @block.gpsimd
            def _(pool):
                nc.gpsimd.memset(ident[:], 0.0).then_inc(set_up, 1)
                pool.wait_ge(set_up, 1)
                nc.gpsimd.affine_select(out=ident[:], in_=ident[:], compare_op=ALU.not_equal, fill=1.0, base=0,
                                        pattern=[[-1, P]], channel_multiplier=1).then_inc(ready, 1)
                pool.wait_ge(dir_in, 16)
                last_tile = pool.value_load(dir_sb[0:1, last_at:last_at + 1], min_val=E - 1, max_val=MAX_TILES - 2)

                def gather(t):
                    pool.wait_ge(rec_g_in, 16 * (t + 1))
                    pool.wait_ge(xT_done, t)
                    pool.sem_inc(pool_passed, 1)
                    nc.gpsimd.indirect_dma_start(
                        out=tokens[:], out_offset=None, in_=h2st[:, :],
                        in_offset=bass.IndirectOffsetOnAxis(ap=rec_g[:].bitcast(I32)[:, 0:1], axis=0)).then_inc(gathered, 16)

                def add(t):
                    pool.wait_ge(y_done, t + 2)
                    pool.sem_inc(pool_passed, 1)
                    nc.gpsimd.indirect_dma_start(
                        out=acc[:, :], out_offset=bass.IndirectOffsetOnAxis(ap=rec_s[:].bitcast(I32)[:, 0:1], axis=0),
                        in_=y[:], in_offset=None, compute_op=ALU.add).then_inc(added, 16)

                gather(0)
                gather(1)
                with pool.Fori(0, last_tile) as t:
                    gather(t + 2)
                    add(t - 1)
                add(last_tile - 1)
                add(last_tile)

            @block.tensor
            def _(pe):
                pe.wait_ge(ready, 4)
                pe.wait_ge(dir_in, 16)

                def transpose_tokens(t):
                    pe.wait_ge(gathered, 16 * (t + 1))
                    for c in range(C):
                        last = nc.tensor.transpose(xT_ps[:, c], tokens[:, c * P:(c + 1) * P], ident[:])
                    last.then_inc(xT_done, 1)

                def down(t, b):
                    pe.wait_ge(hT_lo_done, t + 1)
                    pe.wait_ge(y_done, t + 1)
                    for h in range(HV):
                        cols = slice(h * HALF, (h + 1) * HALF)
                        for c in range(CI):
                            nc.tensor.matmul(y_ps[:, cols], hT_hi[:, c], d_hi[:, b, c, cols], start=(c == 0), stop=False)
                            nc.tensor.matmul(y_ps[:, cols], hT_hi[:, c], d_lo[:, b, c, cols], start=False, stop=False)
                            last = nc.tensor.matmul(y_ps[:, cols], hT_lo[:, c], d_hi[:, b, c, cols], start=False, stop=(c == CI - 1))
                    last.then_inc(down_done, 1)

                def tile(t, b, b_before):
                    pe.wait_ge(xT_lo_done, t + 1)
                    pe.wait_ge(hidden_done, t)
                    for k, o in enumerate((gate_ps, up_ps)):
                        for c in range(C):
                            nc.tensor.matmul(o[:, 0:I], xT_hi[:, c], gu_hi[:, b, k, c], start=(c == 0), stop=False)
                            nc.tensor.matmul(o[:, 0:I], xT_hi[:, c], gu_lo[:, b, k, c], start=False, stop=False)
                            last = nc.tensor.matmul(o[:, 0:I], xT_lo[:, c], gu_hi[:, b, k, c], start=False, stop=(c == C - 1))
                        last.then_inc(gu_done, 1)
                    transpose_tokens(t + 1)
                    down(t - 1, b_before)
                    pe.wait_ge(hidden_done, t + 1)
                    for c in range(CI):
                        last = nc.tensor.transpose(hT_ps[:, c], hidden[:, c * P:(c + 1) * P], ident[:])
                    last.then_inc(hT_done, 1)

                transpose_tokens(0)

                def expert(e, b, has_next, has_second):
                    pe.wait_ge(w_lo_done, PIECES * (e + 1))
                    expert_tiles(pe, e, lambda t: tile(t, b, 1 - b), lambda t: tile(t, b, b))
                experts(pe, expert)
                last_tile = pe.value_load(dir_sb[0:1, last_at:last_at + 1], min_val=E - 1, max_val=MAX_TILES - 2)
                down(last_tile, (E - 1) % 2)

            @block.scalar
            def _(act):
                def load_weights(e):
                    for k, (raw, src) in enumerate(((raw_g, w_gate), (raw_u, w_up), (raw_d, w_down))):
                        act.dma_start(raw[:], src[bass.ds(e, 1)].rearrange("o (c p) i -> p (o c) i", p=P)).then_inc(raw_in[k], 16)

                def split(e, b, lo, hi):
                    for n, (raw, loaded, high, low) in enumerate(pieces(b)):
                        if lo <= n < hi:
                            act.wait_ge(loaded, 16 * (e + 1))
                            nc.scalar.copy(high, raw).then_inc(w_hi_done, 1)

                def tokens_high(t):
                    act.wait_ge(xT_done, t + 1)
                    nc.scalar.copy(xT_hi[:], xT_ps[:]).then_inc(xT_hi_done, 1)

                def output(t):
                    act.wait_ge(down_done, t + 2)
                    act.wait_ge(rec_s_in, 16 * (t + 2))
                    nc.scalar.activation(y[:], y_ps[:], ACT.Copy, scale=rec_s[:, 1:2]).then_inc(y_done, 1)

                def tile(t, e=None, b=None):
                    act.wait_ge(gu_done, 2 * t + 1)
                    act.wait_ge(hidden_done, t)
                    nc.scalar.activation(silu[:], gate_ps[:, 0:I], ACT.Silu).then_inc(silu_done, 1)
                    tokens_high(t + 1)
                    if e is not None:
                        split(e, b, 0, EARLY)
                    output(t - 1)
                    act.wait_ge(hT_done, t + 1)
                    nc.scalar.copy(hT_hi[:], hT_ps).then_inc(hT_hi_done, 1)
                    if e is not None:
                        split(e, b, EARLY, PIECES)

                load_weights(0)
                act.wait_ge(dir_in, 16)
                split(0, 0, 0, PIECES)
                act.wait_ge(w_lo_done, PIECES)
                load_weights(1)
                tokens_high(0)

                def expert(e, b, has_next, has_second):
                    def first(t):
                        if has_next:
                            tile(t, e + 1, 1 - b)
                        else:
                            tile(t)
                        if has_second:
                            act.wait_ge(w_lo_done, PIECES * (e + 2))
                            load_weights(e + 2)
                    expert_tiles(act, e, first, tile)
                experts(act, expert)
                last_tile = act.value_load(dir_sb[0:1, last_at:last_at + 1], min_val=E - 1, max_val=MAX_TILES - 2)
                output(last_tile)

            @block.vector
            def _(dve):
                def split(e, b, lo, hi):
                    for n, (raw, loaded, high, low) in enumerate(pieces(b)):
                        if lo <= n < hi:
                            dve.wait_ge(w_hi_done, PIECES * e + n + 1)
                            nc.vector.tensor_tensor(low, raw, f32(high), ALU.subtract).then_inc(w_lo_done, 1)

                def tokens_low(t):
                    dve.wait_ge(xT_hi_done, t + 1)
                    nc.vector.tensor_tensor(xT_lo[:], xT_ps[:], f32(xT_hi[:]), ALU.subtract).then_inc(xT_lo_done, 1)

                def tile(t, e=None, b=None):
                    dve.wait_ge(silu_done, t + 1)
                    dve.wait_ge(gu_done, 2 * t + 2)
                    dve.wait_ge(hT_done, t)
                    nc.vector.tensor_tensor(hidden[:], silu[:], up_ps[:, 0:I], ALU.mult).then_inc(hidden_done, 1)
                    tokens_low(t + 1)
                    if e is not None:
                        split(e, b, 0, EARLY)
                    dve.wait_ge(hT_hi_done, t + 1)
                    nc.vector.tensor_tensor(hT_lo[:], hT_ps, f32(hT_hi[:]), ALU.subtract).then_inc(hT_lo_done, 1)
                    if e is not None:
                        split(e, b, EARLY, PIECES)

                nc.vector.memset(f32(d_hi[:, 1]), 0.0).then_inc(ready, 1)
                nc.vector.memset(f32(d_lo[:, 1]), 0.0).then_inc(ready, 1)
                nc.vector.memset(f32(hT_hi[:]), 0.0)
                nc.vector.memset(f32(hT_lo[:]), 0.0).then_inc(ready, 1)
                dve.wait_ge(dir_in, 16)
                split(0, 0, 0, PIECES)
                tokens_low(0)

                def expert(e, b, has_next, has_second):
                    if has_next:
                        expert_tiles(dve, e, lambda t: tile(t, e + 1, 1 - b), tile)
                    else:
                        expert_tiles(dve, e, tile, tile)
                experts(dve, expert)


def cross_attention_and_experts(nc, x, ctxT, mask, wqT, bq, wkT, bk, wvT, bv, woT, bo, gamma, beta, rscale,
                                gateT, w_gate, w_up, w_down, out):
    H, T = ctxT.shape
    B, E = mask.shape[1], w_gate.shape[0]
    S, NH = T // B, H // HD

    def scratch(name, shape, dt=F32):
        return nc.dram_tensor(name, shape, dt, kind="Internal").ap()

    xnT = scratch("xnT", (H, T))
    kst, qst, vst = scratch("kst", (B * NH, 2 * HD, S)), scratch("qst", (B * NH, 2, HD, S)), scratch("vst", (T, NH, 2 * HD))
    ctxst, sums, rsums = scratch("ctxst", (H, T)), scratch("sums", (NH, T)), scratch("rsums", (NH, T))
    h2st, table = scratch("h2st", (T + P, H)), scratch("table", (table_regions(E) * REGION, 2))
    dirst = scratch("dirst", (1, directory(E)[-1] + 1 + 3 * P), I32)
    projection_pass(nc, "k", ctxT, wkT, bk, kst, x, xnT)
    projection_pass(nc, "v", ctxT, wvT, bv, vst)
    projection_pass(nc, "q", xnT, wqT, bq, qst)
    attention_pass(nc, kst, qst, vst, mask, ctxst, sums, B, S)
    reciprocal_pass(nc, sums, rsums)
    output_pass(nc, ctxst, rsums, woT, bo, gamma, beta, rscale, x, gateT, out, h2st, table, dirst)
    experts_pass(nc, h2st, table, dirst, w_gate, w_up, w_down, out)


def kernel(**inputs):
    from concourse import bacc
    from concourse.bass_utils import run_bass_kernel_spmd

    given = {name: np.asarray(value) for name, value in inputs.items()}
    x, mask = given["x"], given["mask_BxS2_ik0"]
    B, S, H = x.shape
    T = B * S

    def transposed(name):
        return given[name].reshape(-1, H).T

    def by_feature(name):
        return given[name].reshape(H // P, P).T

    def row(name):
        return given[name].reshape(1, -1)

    laid = {
        "x": x.reshape(T, H), "ctxT": transposed("ctx_2048"),
        "mask": mask.reshape(B, S // P, P).transpose(2, 0, 1),
        "wqT": transposed("L0_xattn_Wq"), "bq": by_feature("L0_xattn_bq"),
        "wkT": transposed("L0_xattn_Wk"), "bk": by_feature("L0_xattn_bk"),
        "wvT": transposed("L0_xattn_Wv"), "bv": row("L0_xattn_bv"),
        "woT": transposed("L0_xattn_Wo"), "bo": row("L0_xattn_bo"),
        "gamma": row("L0_xattn_ln_gamma"), "beta": row("L0_xattn_ln_beta"),
        "rscale": given["L0_xattn_residual_scale"].reshape(1, 1),
        "gateT": transposed("L0_ffn_gate_weight"),
        "w_gate": given["L0_ffn_w_gate"], "w_up": given["L0_ffn_w_up"], "w_down": given["L0_ffn_w_down"],
    }
    nc = bacc.Bacc("TRN2", target_bir_lowering=False, num_devices=1)
    arrays, args = {}, {}
    for name, a in laid.items():
        a = np.ascontiguousarray(a)
        arrays[f"in_{name}"] = a
        args[name] = nc.dram_tensor(f"in_{name}", a.shape, mybir.dt.from_np(a.dtype), kind="ExternalInput").ap()
    out = nc.dram_tensor("out", (T + P, H), F32, kind="ExternalOutput").ap()
    cross_attention_and_experts(nc, out=out, **args)
    result = run_bass_kernel_spmd(nc, [arrays], core_ids=[0])
    return result.results[0]["out"][:T].reshape(B, S, H)
```

```python
from contextlib import ExitStack
import math

import numpy as np
import concourse.bass as bass
from concourse import mybir

F32, F32R = mybir.dt.float32, mybir.dt.float32r
I32, U32 = mybir.dt.int32, mybir.dt.uint32
ALU, ACT, AX = mybir.AluOpType, mybir.ActivationFunctionType, mybir.AxisListType

P = 128
HD = 64
HALF = 512
TOPK = 8
REGION = 4096
EPS = 1e-5
CLIP = 50.0
RES_SCALE_MAX = 0.3
BIG = 3.0e38


class Scope:

    def __init__(self, nc, stack, name):
        self.nc, self.stack, self.name, self.sems = nc, stack, name, []
        stack.callback(self.clear)

    def sb(self, name, shape, dt=F32):
        return self.stack.enter_context(self.nc.sbuf_tensor(f"{self.name}_{name}", shape, dt))

    def ps(self, name, shape, dt=F32):
        return self.stack.enter_context(self.nc.psum_tensor(f"{self.name}_ps_{name}", shape, dt))

    def sem(self, name):
        self.sems.append(self.nc.alloc_semaphore(f"{self.name}_{name}"))
        return self.sems[-1]

    def clear(self):
        self.nc.clear_and_free_semaphores(self.sems)
        self.nc.all_engine_barrier()


def f32(ap):
    return ap.bitcast(F32)


def row_broadcast(dram_row, n):
    return dram_row.broadcast_to([P, n])


def projection_pass(nc, kind, actT, wT, bias, out, x=None, xnT=None):
    H, T = actT.shape
    C = H // P
    NB = T // HALF
    G = C if kind != "v" else (HALF // P) * (H // HALF)
    BANKS = 4
    S = out.shape[-1] if kind != "v" else None
    NH = H // HD
    RAW = 3 if x is not None else 6
    PIECES = 4
    CP = C // PIECES
    LN = HALF // P if x is not None else 0
    HV = H // HALF
    with ExitStack() as st:
        s = Scope(nc, st, "proj_" + kind)
        w_raw = s.sb("w_raw", [P, RAW, H])
        w_hi, w_lo = s.sb("w_hi", [P, C, H], F32R), s.sb("w_lo", [P, C, H], F32R)
        a_raw = s.sb("a_raw", [P, 2, C, HALF])
        a_hi, a_lo = s.sb("a_hi", [P, 2, C, HALF], F32R), s.sb("a_lo", [P, 2, C, HALF], F32R)
        if kind == "v":
            bias_sb, v32 = s.sb("bias", [P, H]), s.sb("v32", [P, 2, HALF])
            o = s.sb("o", [P, 2, HALF // HD, 2, HD], F32R)
        else:
            bias_sb = s.sb("bias", [P, C])
            o_hi, o_lo = s.sb("o_hi", [P, 2, HALF], F32R), s.sb("o_lo", [P, 2, HALF], F32R)
        acc = s.ps("acc", [P, BANKS, HALF])
        if LN:
            xin, xn, xT = s.sb("xin", [P, 2, H]), s.sb("xn", [P, 2, H]), s.sb("xT", [P, 2, C, P])
            stats, mv = s.sb("stats", [P, 2, HV, 6]), s.sb("mv", [P, 2, 2])
            std, rstd, eps = s.sb("std", [P, 2, 1]), s.sb("rstd", [P, 2, 1]), s.sb("eps", [P, 1])
            ident = s.sb("ident", [P, P])
            tps = s.ps("tps", [P, 2, C, P])
            x_in, xT_stored = [s.sem("x_in0"), s.sem("x_in1")], [s.sem("xT_stored0"), s.sem("xT_stored1")]
            zeroed, ident_ready, stats_passed = s.sem("zeroed"), s.sem("ident_ready"), s.sem("stats_passed")
            sp_passed = s.sem("sp_passed")
            eps_ready, std_done, rstd_done = s.sem("eps_ready"), s.sem("std_done"), s.sem("rstd_done")
            stats_done, mv_done = s.sem("stats_done"), s.sem("mv_done")
            xn_done, t_done, xT_done = s.sem("xn_done"), s.sem("t_done"), s.sem("xT_done")
            xnT_v = xnT.rearrange("(c p) t -> p c t", p=P)
        w_in = [s.sem(f"w_in{i}") for i in range(RAW)]
        a_in = [s.sem(f"a_in{i}") for i in range(2)]
        bias_in = s.sem("bias_in")
        first_in = [s.sem(f"first_in{k}") for k in range(PIECES)]
        first_hi_done, first_lo_done = s.sem("first_hi_done"), s.sem("first_lo_done")
        w_hi_done, w_lo_done = s.sem("w_hi_done"), s.sem("w_lo_done")
        a_hi_done, a_lo_done = s.sem("a_hi_done"), s.sem("a_lo_done")
        product_done, v32_done, o_hi_done, o_lo_done = s.sem("product_done"), s.sem("v32_done"), s.sem("o_hi_done"), s.sem("o_lo_done")
        stored = [s.sem(f"stored{i}") for i in range(2)]
        STORES = 1 if kind == "v" else 4
        act_v = actT.rearrange("(c p) t -> p c t", p=P)


        def ln_before(t, j):
            return LN * t + max(j - 1, 0)

        with nc.Block() as block:
            @block.gpsimd
            def _(pool):
                if LN:
                    nc.gpsimd.memset(ident[:], 0.0).then_inc(zeroed, 1)
                    pool.wait_ge(zeroed, 1)
                    nc.gpsimd.affine_select(out=ident[:], in_=ident[:], compare_op=ALU.not_equal, fill=1.0, base=0,
                                            pattern=[[-1, P]], channel_multiplier=1).then_inc(ident_ready, 1)

                def load(t, b):
                    pool.dma_start(a_raw[:, b], act_v[:, :, bass.ds(t * HALF, HALF)]).then_inc(a_in[b], 16)

                for k in range(PIECES):
                    cs = slice(k * CP, (k + 1) * CP)
                    pool.dma_start(a_raw[:, 0, cs], act_v[:, cs, 0:HALF]).then_inc(first_in[k], 16)
                if kind == "v":
                    pool.dma_start(bias_sb[:], row_broadcast(bias, H)).then_inc(bias_in, 16)
                else:
                    pool.dma_start(bias_sb[:], bias).then_inc(bias_in, 16)
                pool.wait_ge(w_hi_done, C)
                load(1, 1)
                with pool.Fori(0, NB // 2 - 1) as i:
                    for b in range(2):
                        pool.wait_ge(a_lo_done, 2 * i + b + 1)
                        load(2 * i + b + 2, b)

            @block.sync
            def _(sp):
                for b in range(2):
                    sp.sem_inc(stored[b], 1)
                    if LN:
                        sp.sem_inc(xT_stored[b], 1)
                for c in range(C):
                    if c >= RAW:
                        sp.wait_ge(w_lo_done, c - RAW + 1)
                    sp.dma_start(w_raw[:, c % RAW], wT[c * P:(c + 1) * P, :]).then_inc(w_in[c % RAW], 16)

                def load_x(t, j):
                    sp.dma_start(xin[:, j % 2], x[bass.ds((LN * t + j) * P, P), :]).then_inc(x_in[j % 2], 16)

                def layernorm(t, g, last):
                    j = g // 2
                    if g % 2:
                        sp.wait_ge(xT_done, LN * t + j + 1)
                        sp.sem_inc(sp_passed, 1)
                        sp.dma_start(xnT_v[:, :, bass.ds((LN * t + j) * P, P)], xT[:, j % 2]).then_inc(xT_stored[j % 2], 16)
                    elif not last or j + 2 < LN:
                        sp.wait_ge(xn_done, LN * t + j + 1)
                        load_x(t, j + 2)

                if LN:
                    load_x(0, 0)
                    load_x(0, 1)

                def store(i, last):
                    for b in range(2):
                        for g in range(G):
                            if LN and g:
                                layernorm(2 * i + b, g - 1, last and b == 1)
                            sp.wait_ge(o_lo_done, (2 * i + b) * G + g + 1)
                            q = g % 2
                            if kind == "v":
                                row = (2 * i + b) * HALF + (g // (H // HALF)) * P
                                h0 = (g % (H // HALF)) * (HALF // HD)
                                sp.dma_start(out[bass.ds(row, P), h0:h0 + HALF // HD, :],
                                             f32(o[:, q]).rearrange("p h two d -> p h (two d)")).then_inc(stored[q], 16)
                                continue
                            if S == 2 * HALF:
                                bh, t0 = i * NH + 2 * g, b * HALF
                            else:
                                bh, t0 = (2 * i + b) * NH + 2 * g, 0
                            for hh in range(2):
                                for k, tile in enumerate((o_hi, o_lo)):
                                    if kind == "k":
                                        dst = out[bass.ds(bh + hh, 1), k * HD:(k + 1) * HD, t0:t0 + HALF]
                                        dst = dst.rearrange("o d t -> (o d) t")
                                    else:
                                        dst = out[bass.ds(bh + hh, 1), k, :, t0:t0 + HALF].rearrange("o d t -> (o d) t")
                                    sp.dma_start(dst, f32(tile[hh * HD:(hh + 1) * HD, q])).then_inc(stored[q], 16)
                        if LN:
                            layernorm(2 * i + b, G - 1, last and b == 1)

                with sp.Fori(0, NB // 2 - 1) as i:
                    store(i, False)
                store(NB // 2 - 1, True)
                for q in range(2):
                    sp.wait_ge(stored[q], 16 * STORES * NB * G // 2 + 1)
                    if LN:
                        sp.wait_ge(xT_stored[q], 16 * LN * NB // 2 + 1)

            @block.scalar
            def _(act):
                def split(t, b, n):
                    act.wait_ge(a_in[b], 16 * (n + b))
                    if not (isinstance(t, int) and t < 2):
                        act.wait_ge(product_done, (t - 1) * G + 1)
                    nc.scalar.copy(a_hi[:, b], a_raw[:, b]).then_inc(a_hi_done, 1)

                def evacuate(t, b):
                    for g in range(G):
                        n, q = t * G + g, g % 2
                        act.wait_ge(stored[q], 16 * STORES * (t * (G // 2) + g // 2) + 1)
                        if kind == "v":
                            act.wait_ge(v32_done, n + 1)
                            nc.scalar.copy(o[:, q, :, 0], v32[:, q].rearrange("p (h d) -> p h d", d=HD)).then_inc(o_hi_done, 1)
                        else:
                            act.wait_ge(product_done, n + 2)
                            nc.scalar.activation(o_hi[:, q], acc[:, g % BANKS], ACT.Identity,
                                                 bias=bias_sb[:, g:g + 1]).then_inc(o_hi_done, 1)
                        if LN and g % 2 == 0:
                            act.wait_ge(mv_done, LN * t + g // 2 + 1)
                            b_x = g // 2 % 2
                            nc.scalar.activation(std[:, b_x], mv[:, b_x, 1:2], ACT.Sqrt, bias=eps[:]).then_inc(std_done, 1)
                        if LN and g % 2:
                            j = g // 2
                            act.wait_ge(t_done, LN * t + j + 2)
                            act.wait_ge(xT_stored[j % 2], 16 * (LN // 2 * t + j // 2) + 1)
                            nc.scalar.copy(xT[:, j % 2], tps[:, j % 2]).then_inc(xT_done, 1)

                for c in range(C):
                    if c % CP == 0:
                        act.wait_ge(first_in[c // CP], 16)
                        nc.scalar.copy(a_hi[:, 0, c:c + CP], a_raw[:, 0, c:c + CP]).then_inc(first_hi_done, 1)
                    act.wait_ge(w_in[c % RAW], 16 * (c // RAW + 1))
                    nc.scalar.copy(w_hi[:, c], w_raw[:, c % RAW]).then_inc(w_hi_done, 1)
                if LN:
                    act.wait_ge(eps_ready, 1)
                act.wait_ge(bias_in, 16)
                with act.Fori(0, NB // 2 - 1) as i:
                    split(2 * i + 1, 1, i)
                    evacuate(2 * i, 0)
                    split(2 * i + 2, 0, i + 1)
                    evacuate(2 * i + 1, 1)
                split(NB - 1, 1, NB // 2 - 1)
                evacuate(NB - 2, 0)
                evacuate(NB - 1, 1)

            @block.vector
            def _(dve):
                def split(t, b):
                    dve.wait_ge(a_hi_done, t)
                    nc.vector.tensor_tensor(a_lo[:, b], a_raw[:, b], f32(a_hi[:, b]), ALU.subtract).then_inc(a_lo_done, 1)

                def evacuate(t, b):
                    for g in range(G):
                        n, q = t * G + g, g % 2
                        if kind == "v":
                            half = g % (H // HALF)
                            dve.wait_ge(product_done, n + 2)
                            nc.vector.tensor_tensor(v32[:, q], acc[:, g % BANKS],
                                                    bias_sb[:, half * HALF:(half + 1) * HALF], ALU.add).then_inc(v32_done, 1)
                            dve.wait_ge(o_hi_done, n + 1)
                            nc.vector.tensor_tensor(o[:, q, :, 1], v32[:, q].rearrange("p (h d) -> p h d", d=HD),
                                                    f32(o[:, q, :, 0]), ALU.subtract).then_inc(o_lo_done, 1)
                        else:
                            dve.wait_ge(o_hi_done, n + 1)
                            nc.vector.scalar_tensor_tensor(
                                out=o_lo[:, q], in0=acc[:, g % BANKS], scalar=bias_sb[:, g:g + 1], in1=f32(o_hi[:, q]),
                                op0=ALU.add, op1=ALU.subtract).then_inc(o_lo_done, 1)
                        if LN and g % 2 == 0:
                            layernorm(t, g // 2)

                def layernorm(t, j):
                    n, b = LN * t + j, j % 2
                    dve.wait_ge(x_in[b], 16 * (LN // 2 * t + j // 2 + 1))
                    for k in range(HV):
                        nc.vector.bn_stats(stats[:, b, k], xin[:, b, k * HALF:(k + 1) * HALF]).then_inc(stats_done, 1)
                    dve.wait_ge(stats_done, HV * (n + 1))
                    dve.sem_inc(stats_passed, 1)
                    nc.vector.bn_aggr(mv[:, b], stats[:, b]).then_inc(mv_done, 1)
                    dve.wait_ge(std_done, n + 1)
                    nc.vector.reciprocal(rstd[:, b], std[:, b]).then_inc(rstd_done, 1)
                    dve.wait_ge(rstd_done, n + 1)
                    dve.wait_ge(t_done, ln_before(t, j) + 1)
                    nc.vector.tensor_scalar(xn[:, b], xin[:, b], mv[:, b, 0:1], rstd[:, b],
                                            ALU.subtract, ALU.mult).then_inc(xn_done, 1)

                for c in range(C):
                    if c % CP == 0:
                        dve.wait_ge(first_hi_done, c // CP + 1)
                        nc.vector.tensor_tensor(a_lo[:, 0, c:c + CP], a_raw[:, 0, c:c + CP], f32(a_hi[:, 0, c:c + CP]),
                                                ALU.subtract).then_inc(a_lo_done if c == C - CP else first_lo_done, 1)
                    dve.wait_ge(w_hi_done, c + 1)
                    nc.vector.tensor_tensor(w_lo[:, c], w_raw[:, c % RAW], f32(w_hi[:, c]), ALU.subtract).then_inc(w_lo_done, 1)
                if LN:
                    nc.vector.memset(eps[:], EPS).then_inc(eps_ready, 1)
                dve.wait_ge(bias_in, 16)
                with dve.Fori(0, NB // 2 - 1) as i:
                    split(2 * i + 1, 1)
                    evacuate(2 * i, 0)
                    split(2 * i + 2, 0)
                    evacuate(2 * i + 1, 1)
                split(NB - 1, 1)
                evacuate(NB - 2, 0)
                evacuate(NB - 1, 1)

            @block.tensor
            def _(pe):
                def tiles(t, b, first):
                    if not first:
                        pe.wait_ge(a_lo_done, t + 1)
                    for g in range(G):
                        if not first or g >= BANKS:
                            pe.wait_ge(o_lo_done, t * G + g - BANKS + 1)
                        for c in range(C):
                            if first and g == 0:
                                if c == C - CP:
                                    pe.wait_ge(a_lo_done, 1)
                                elif c % CP == 0:
                                    pe.wait_ge(first_lo_done, c // CP + 1)
                                pe.wait_ge(w_lo_done, c + 1)
                            if kind == "v":
                                r, half = g // (H // HALF), g % (H // HALF)
                                hi, lo = (a[:, b, c, r * P:(r + 1) * P] for a in (a_hi, a_lo))
                                mhi, mlo = (w[:, c, half * HALF:(half + 1) * HALF] for w in (w_hi, w_lo))
                            else:
                                hi, lo = (w[:, c, g * P:(g + 1) * P] for w in (w_hi, w_lo))
                                mhi, mlo = a_hi[:, b, c], a_lo[:, b, c]
                            o_ = acc[:, g % BANKS]
                            nc.tensor.matmul(o_, hi, mhi, start=(c == 0), stop=False)
                            nc.tensor.matmul(o_, hi, mlo, start=False, stop=False)
                            last = nc.tensor.matmul(o_, lo, mhi, start=False, stop=(c == C - 1))
                        last.then_inc(product_done, 1)
                        if LN and g % 2:
                            j = g // 2
                            pe.wait_ge(xn_done, LN * t + j + 1)
                            pe.wait_ge(xT_done, ln_before(t, j))
                            for c in range(C):
                                last = nc.tensor.transpose(tps[:, j % 2, c], xn[:, j % 2, c * P:(c + 1) * P], ident[:])
                            last.then_inc(t_done, 1)

                pe.sem_inc(product_done, 1)
                if LN:
                    pe.sem_inc(t_done, 1)
                    pe.wait_ge(ident_ready, 1)
                tiles(0, 0, True)
                tiles(1, 1, False)
                with pe.Fori(1, NB // 2) as i:
                    tiles(2 * i, 0, False)
                    tiles(2 * i + 1, 1, False)


def attention_pass(nc, kst, qst, vst, mask, ctxst, sums, B, S):
    NHB = kst.shape[0]
    NH, C, HV = NHB // B, S // P, S // HALF
    NPAIR = NHB // 2
    with ExitStack() as st:
        s = Scope(nc, st, "att")
        kt = s.sb("kt", [P, 2, S], F32R)
        qh, ql = s.sb("qh", [P, 2, S], F32R), s.sb("ql", [P, 2, S], F32R)
        v = s.sb("v", [P, 2, C, 4 * HD], F32R)
        e32, p32 = s.sb("e32", [P, 2, S]), s.sb("p32", [P, 2, S])
        p_hi, p_lo = s.sb("p_hi", [P, 2, S], F32R), s.sb("p_lo", [P, 2, S], F32R)
        c32 = s.sb("c32", [P, 2, S])
        m_int, m32, upper = s.sb("m_int", [P, B, C], I32), s.sb("m32", [P, B, C]), s.sb("upper", [P, B, C])
        sc = s.ps("sc", [P, 2, S])
        o = s.ps("o", [P, 2, S])
        kq_in = [s.sem(f"kq_in{i}") for i in range(2)]
        v_in = [s.sem(f"v_in{i}") for i in range(2)]
        mask_in, m_done, upper_ready, const_ready = s.sem("mask_in"), s.sem("m_done"), s.sem("upper_ready"), s.sem("const_ready")
        scores_done, exp_done, clip_done, hi_done, lo_done = s.sem("scores_done"), s.sem("exp_done"), s.sem("clip_done"), s.sem("hi_done"), s.sem("lo_done")
        values_done, c_done = s.sem("values_done"), s.sem("c_done")
        stored = [s.sem(f"stored{i}") for i in range(2)]
        U = 2 * C
        AHEAD = 3
        vst_v = vst.rearrange("(b c p) h d -> b p c h d", b=B, p=P)

        def stationary(b, c, k):
            return v[:, b, c, 2 * k * HD:2 * (k + 1) * HD]

        with nc.Block() as block:
            @block.sync
            def _(sp):
                sp.dma_start(m_int[:], mask).then_inc(mask_in, 16)

                def load(i, bt):
                    for b in range(2):
                        bh = bt * NH + 2 * i + b
                        reused = not (isinstance(bh, int) and bh < 2)
                        if reused:
                            sp.wait_ge(scores_done, (bh - 1) * C)
                        sp.dma_start(f32(kt[:, b]), kst[bass.ds(bh, 1)].rearrange("o p t -> (o p) t")).then_inc(kq_in[b], 16)
                        for k, q in enumerate((qh, ql)):
                            for r in range(2):
                                sp.dma_start(f32(q[r * HD:(r + 1) * HD, b]),
                                             qst[bass.ds(bh, 1), k].rearrange("o p t -> (o p) t")).then_inc(kq_in[b], 16)
                        if reused:
                            sp.wait_ge(values_done, (bh - 1) * C)
                        for k in range(2):
                            src = vst_v[bt, :, :, bass.ds(2 * i + b, 1), k * HD:(k + 1) * HD]
                            sp.dma_start(f32(v[:, b, :, (2 * k + b) * HD:(2 * k + b + 1) * HD]),
                                         src.rearrange("p c o d -> p c (o d)")).then_inc(v_in[b], 16)

                load(0, 0)
                for bt in range(B):
                    with sp.Fori(0 if bt else 1, NH // 2) as i:
                        load(i, bt)

            @block.gpsimd
            def _(pool):
                for bt in range(B):
                    with pool.Fori(0, NH // 2) as i:
                        for b in range(2):
                            head = bt * NH + 2 * i + b
                            pool.wait_ge(c_done, head + 1)
                            pool.dma_start(ctxst[bass.ds((2 * i + b) * HD, HD), bt * S:(bt + 1) * S],
                                           c32[b * HD:(b + 1) * HD, b]).then_inc(stored[b], 16)
                            other = (1 - b) * HD
                            pool.dma_start(sums[bass.ds(2 * i + b, 1), bt * S:(bt + 1) * S], c32[other:other + 1, b]).then_inc(stored[b], 16)
                for b in range(2):
                    pool.wait_ge(stored[b], 32 * NPAIR)

            def pairs(eng, body):
                n = NH // 2
                body(0, 0, 0, True)
                for bt in range(B):
                    first = 0 if bt else 1
                    if n - 1 > first:
                        with eng.Fori(first, n - 1) as i:
                            body(bt * n + i, bt, bt, False)
                    body(bt * n + n - 1, bt, bt + 1 if bt < B - 1 else None, False)

            @block.tensor
            def _(pe):
                def scores(pair, u):
                    b, c = (u % U) // C, u % C
                    if c == 0:
                        pe.wait_ge(kq_in[b], 5 * 16 * (pair + 1))
                    n = pair * U + u
                    if not (isinstance(n, int) and n < 2):
                        pe.wait_ge(exp_done, n - 1)
                    for h in range(HV):
                        cols = slice(h * HALF, (h + 1) * HALF)
                        nc.tensor.matmul(sc[:, u % 2, cols], kt[:, b, c * P:(c + 1) * P], qh[:, b, cols], start=True, stop=False)
                        last = nc.tensor.matmul(sc[:, u % 2, cols], kt[:, b, c * P:(c + 1) * P], ql[:, b, cols], start=False, stop=True)
                    last.then_inc(scores_done, 1)

                def values(pair, u, first):
                    b, c = u // C, u % C
                    if c == 0:
                        pe.wait_ge(v_in[b], 32 * (pair + 1))
                        if not first:
                            pe.wait_ge(c_done, 2 * pair + b - 1)
                    pe.wait_ge(lo_done, pair * U + u + 1)
                    for h in range(HV):
                        cols = slice(h * HALF, (h + 1) * HALF)
                        nc.tensor.matmul(o[:, b, cols], stationary(b, c, 0), p_hi[:, u % 2, cols], start=(c == 0), stop=False)
                        nc.tensor.matmul(o[:, b, cols], stationary(b, c, 0), p_lo[:, u % 2, cols], start=False, stop=False)
                        last = nc.tensor.matmul(o[:, b, cols], stationary(b, c, 1), p_hi[:, u % 2, cols], start=False, stop=(c == C - 1))
                    last.then_inc(values_done, 1)

                pe.wait_ge(const_ready, 1)
                for u in range(AHEAD):
                    scores(0, u)

                def body(pair, bt, next_bt, first):
                    for u in range(U):
                        if u + AHEAD < U:
                            scores(pair, u + AHEAD)
                        elif next_bt is not None:
                            scores(pair + 1, u + AHEAD - U)
                        values(pair, u, first)
                pairs(pe, body)

            @block.scalar
            def _(act):
                def exponential(n, u):
                    act.wait_ge(scores_done, n + 1)
                    if not (isinstance(n, int) and n < 2):
                        act.wait_ge(clip_done, n - 1)
                    nc.scalar.activation(e32[:, u % 2], sc[:, u % 2], ACT.Exp, scale=1.0 / math.sqrt(HD)).then_inc(exp_done, 1)

                def high(n, u):
                    act.wait_ge(clip_done, n + 1)
                    if not (isinstance(n, int) and n < 2):
                        act.wait_ge(values_done, n - 1)
                    nc.scalar.copy(p_hi[:, u % 2], p32[:, u % 2]).then_inc(hi_done, 1)

                exponential(0, 0)

                def body(pair, bt, next_bt, first):
                    for u in range(U):
                        n = pair * U + u
                        if u < U - 1 or next_bt is not None:
                            exponential(n + 1, u + 1)
                        high(n, u)
                pairs(act, body)

            @block.vector
            def _(dve):
                def clip(n, u, bt):
                    dve.wait_ge(exp_done, n + 1)
                    if not (isinstance(n, int) and n < 2):
                        dve.wait_ge(lo_done, n - 1)
                    nc.vector.tensor_scalar(p32[:, u % 2], e32[:, u % 2], math.exp(-CLIP), upper[:, bt, u % C:u % C + 1],
                                            ALU.max, ALU.min).then_inc(clip_done, 1)

                def low(n, u):
                    dve.wait_ge(hi_done, n + 1)
                    nc.vector.tensor_tensor(p_lo[:, u % 2], p32[:, u % 2], f32(p_hi[:, u % 2]), ALU.subtract).then_inc(lo_done, 1)

                def context(pair, b):
                    dve.wait_ge(values_done, (2 * pair + b + 1) * C)
                    dve.wait_ge(stored[b], 32 * pair)
                    nc.vector.tensor_copy(c32[:, b], o[:, b]).then_inc(c_done, 1)

                for b in range(2):
                    z = (1 - b) * HD
                    nc.vector.memset(f32(v[:, b, :, z:z + HD]), float(np.float32(1.0 + 1e-8)))
                    last = nc.vector.memset(f32(v[:, b, :, z + 2 * HD:z + 3 * HD]), 0.0)
                last.then_inc(const_ready, 1)
                dve.wait_ge(mask_in, 16)
                nc.vector.tensor_copy(m32[:], m_int[:]).then_inc(m_done, 1)
                dve.wait_ge(m_done, 1)
                nc.vector.tensor_scalar(m32[:], m32[:], 0.5, math.exp(CLIP), ALU.is_gt, ALU.mult).then_inc(m_done, 1)
                dve.wait_ge(m_done, 2)
                nc.vector.tensor_scalar(upper[:], m32[:], math.exp(-CLIP), None, ALU.max).then_inc(upper_ready, 1)
                dve.wait_ge(upper_ready, 1)
                clip(0, 0, 0)

                def body(pair, bt, next_bt, first):
                    for u in range(U):
                        n = pair * U + u
                        if u + 1 < U:
                            clip(n + 1, u + 1, bt)
                        elif next_bt is not None:
                            clip(n + 1, 0, next_bt)
                        low(n, u)
                        if u == 2 and not first:
                            context(pair - 1, 1)
                        if u == C + 2:
                            context(pair, 0)

                pairs(dve, body)
                context(NPAIR - 1, 1)


def reciprocal_pass(nc, sums, rsums):
    with ExitStack() as st:
        s = Scope(nc, st, "rec")
        n = sums.shape[0] * sums.shape[1] // P
        t, r = s.sb("t", [P, n]), s.sb("r", [P, n])
        loaded, inverted, stored = s.sem("loaded"), s.sem("inverted"), s.sem("stored")
        src = sums.rearrange("h (k n) -> (h k) n", n=n)
        dst = rsums.rearrange("h (k n) -> (h k) n", n=n)
        with nc.Block() as block:
            @block.sync
            def _(sp):
                sp.dma_start(t[:], src).then_inc(loaded, 16)
                sp.wait_ge(inverted, 1)
                sp.dma_start(dst, r[:]).then_inc(stored, 16)
                sp.wait_ge(stored, 16)

            @block.vector
            def _(dve):
                dve.wait_ge(loaded, 16)
                nc.vector.reciprocal(r[:], t[:]).then_inc(inverted, 1)


def directory(E):
    n_at, base_at, last_at, row_at = 0, E, 2 * E, 2 * E + 1
    return n_at, base_at, last_at, row_at


def table_regions(E):
    return E + 4


def output_pass(nc, ctxst, rsums, woT, bo, gamma, beta, rscale, x, gateT, acc, h2st, table, dirst):
    H, T = ctxst.shape
    C, NT, E, HV = H // P, T // P, gateT.shape[1], H // HALF
    NCOL = 3
    n_at, base_at, last_at, row_at = directory(E)
    with ExitStack() as st:
        s = Scope(nc, st, "out")
        w_raw = s.sb("w_raw", [P, 4, H])
        w_hi, w_lo = s.sb("w_hi", [P, C, H], F32R), s.sb("w_lo", [P, C, H], F32R)
        c_raw, r_t, cn = s.sb("c_raw", [P, 2, C, P]), s.sb("r_t", [P, 2, C, P]), s.sb("cn", [P, 2, C, P])
        c_hi, c_lo = s.sb("c_hi", [P, 2, C, P], F32R), s.sb("c_lo", [P, 2, C, P], F32R)
        x_t, d, x1, h2 = s.sb("x_t", [P, 2, H]), s.sb("d", [P, 2, H]), s.sb("x1", [P, 2, H]), s.sb("h2", [P, 2, H])
        shift = s.sb("shift", [P, 1])
        scaled, normed, h2T = s.sb("scaled", [P, H]), s.sb("normed", [P, H]), s.sb("h2T", [P, C, P])
        gamma_sb, beta_sb, gate_sb = s.sb("gamma", [P, H]), s.sb("beta", [P, H]), s.sb("gate", [P, C, E])
        bo_row = s.sb("bo_row", [1, H])
        bo_hi, bo_lo = s.sb("bo_hi", [1, H], F32R), s.sb("bo_lo", [1, H], F32R)
        rs_raw, rs_sb, eps = s.sb("rs_raw", [P, 1]), s.sb("rs", [P, 1]), s.sb("eps", [P, 1])
        ident, ones, before = s.sb("ident", [P, P]), s.sb("ones", [P, P]), s.sb("before", [P, P])
        ones_row = s.sb("ones_row", [1, P], F32R)
        stats, mv, std, rstd = s.sb("stats", [P, 2, HV, 6]), s.sb("mv", [P, 2, 2]), s.sb("std", [P, 2, 1]), s.sb("rstd", [P, 2, 1])
        logits, top, top_i, top_f, diff = s.sb("logits", [P, E]), s.sb("top", [P, TOPK]), s.sb("top_i", [P, TOPK], U32), s.sb("top_f", [P, TOPK]), s.sb("diff", [P, TOPK])
        e8, esum, rsum, iota_e, rowbase = s.sb("e8", [P, TOPK]), s.sb("esum", [P, 1]), s.sb("rsum", [P, 1]), s.sb("iota_e", [P, E]), s.sb("rowbase", [P, E])
        onehot, prod = s.sb("onehot", [P, 2, TOPK, E]), s.sb("prod", [P, TOPK, E])
        mask, seen = s.sb("mask", [P, 2, E]), s.sb("seen", [P, 2, E])
        token, slot_f, slot = s.sb("token", [P, 1]), s.sb("slot_f", [P, TOPK]), s.sb("slot", [P, 2, TOPK], I32)
        row_e, record = s.sb("row_e", [P, E]), s.sb("record", [P, 2, TOPK, 2])
        fill, zeros = s.sb("fill", [P, P, 2]), s.sb("zeros", [P, H])
        tile_id, cmp, started = s.sb("tile_id", [P, NCOL]), s.sb("cmp", [P, NCOL, E]), s.sb("started", [P, NCOL])
        first_of, row_f, row_i = s.sb("first_of", [P, NCOL]), s.sb("row_f", [P, NCOL]), s.sb("row_i", [P, NCOL], I32)
        cnt, tiles_i, tiles_f, upto, base = s.sb("cnt", [P, E]), s.sb("tiles_i", [P, E], I32), s.sb("tiles_f", [P, E]), s.sb("upto", [P, E]), s.sb("base", [P, E])
        dir_sb = s.sb("dir", [1, row_at + 1], I32)
        o = s.ps("o", [P, 2, H])
        tps, lps, pps = s.ps("tps", [P, C, P]), s.ps("lps", [P, HALF]), s.ps("pps", [P, HALF])

        w_in = [s.sem(f"w_in{i}") for i in range(4)]
        c_in, x_in = [s.sem(f"c_in{i}") for i in range(2)], [s.sem(f"x_in{i}") for i in range(2)]
        consts_in, small_in, set_up, filled = s.sem("consts_in"), s.sem("small_in"), s.sem("set_up"), s.sem("filled")
        masks_ready, rs_ready, bo_ready, fill_ready = s.sem("masks_ready"), s.sem("rs_ready"), s.sem("bo_ready"), s.sem("fill_ready")
        w_hi_done, w_lo_done = s.sem("w_hi_done"), s.sem("w_lo_done")
        cn_done, c_hi_done, c_lo_done, gemm_done, d_done = s.sem("cn_done"), s.sem("c_hi_done"), s.sem("c_lo_done"), s.sem("gemm_done"), s.sem("d_done")
        norm_step, mv_ready, std_ready, x1_done, h2_done = s.sem("norm_step"), s.sem("mv_ready"), s.sem("std_ready"), s.sem("x1_done"), s.sem("h2_done")
        shift_done = s.sem("shift_done")
        t_done, h2T_done, logits_done, diff_done, e8_done = s.sem("t_done"), s.sem("h2T_done"), s.sem("logits_done"), s.sem("diff_done"), s.sem("e8_done")
        route_step, mask_done, record_done, pos_done, slot_step, slot_done = s.sem("route_step"), s.sem("mask_done"), s.sem("record_done"), s.sem("pos_done"), s.sem("slot_step"), s.sem("slot_done")
        stored, scattered = [s.sem(f"stored{i}") for i in range(2)], [s.sem(f"scattered{i}") for i in range(2)]
        pool_passed, dve_passed = s.sem("pool_passed"), s.sem("dve_passed")
        seen_ready, seen_done = s.sem("seen_ready"), s.sem("seen_done")
        count_done, dir_step, dir_done, dir_stored = s.sem("count_done"), s.sem("dir_step"), s.sem("dir_done"), s.sem("dir_stored")

        ctx_v = ctxst.rearrange("(c p) t -> p c t", p=P)
        r_v = rsums.rearrange("(c k) t -> k c t", k=2)
        REGIONS = table_regions(E)
        FILLS = REGIONS * REGION // (P * P)
        CONSTS = 3

        def known(v):
            return isinstance(v, int)

        def tiles(eng, body):
            body(0, 0, 0, True, True, False, False, False)
            body(1, 1, 0, True, True, True, False, False)
            body(2, 0, 1, True, True, True, True, False)
            body(3, 1, 1, True, True, True, True, True)
            with eng.Fori(2, NT // 2 - 1) as h:
                body(2 * h, 0, h, True, True, True, True, True)
                body(2 * h + 1, 1, h, True, True, True, True, True)
            n = NT // 2
            body(NT - 2, 0, n - 1, True, True, True, True, True)
            body(NT - 1, 1, n - 1, True, False, True, True, True)
            body(NT, 0, n, False, False, True, True, True)
            body(NT + 1, 1, n, False, False, False, True, True)
            body(NT + 2, 0, n + 1, False, False, False, False, True)

        with nc.Block() as block:
            @block.sync
            def _(sp):
                def load_context(i, b):
                    sp.dma_start(c_raw[:, b], ctx_v[:, :, bass.ds(i * P, P)]).then_inc(c_in[b], 16)
                    for k in range(2):
                        src = r_v[k, :, bass.ds(i * P, P)].partition_broadcast(HD)
                        sp.dma_start(r_t[k * HD:(k + 1) * HD, b], src).then_inc(c_in[b], 16)

                def load_x(i, b):
                    sp.dma_start(x_t[:, b], x[bass.ds(i * P, P), :]).then_inc(x_in[b], 16)

                load_context(0, 0)
                for c in range(C):
                    if c >= 4:
                        sp.wait_ge(w_lo_done, c - 3)
                    sp.dma_start(w_raw[:, c % 4], woT[c * P:(c + 1) * P, :]).then_inc(w_in[c % 4], 16)
                load_context(1, 1)
                load_x(0, 0)
                load_x(1, 1)

                sp.wait_ge(cn_done, 1)
                load_context(2, 0)

                def body(i, b, more_context, more):
                    if more_context:
                        sp.wait_ge(cn_done, i + 2)
                        load_context(i + 3, 1 - b)
                    sp.wait_ge(x1_done, i + 1)
                    if more:
                        load_x(i + 2, b)
                    sp.dma_start(acc[bass.ds(i * P, P), :], x1[:, b]).then_inc(stored[b], 16)
                    sp.wait_ge(h2_done, i + 1)
                    sp.dma_start(h2st[bass.ds(i * P, P), :], h2[:, b]).then_inc(stored[b], 16)

                with sp.Fori(0, NT // 2 - 2) as h:
                    body(2 * h, 0, True, True)
                    body(2 * h + 1, 1, True, True)
                body(NT - 4, 0, True, True)
                body(NT - 3, 1, False, True)
                body(NT - 2, 0, False, False)
                body(NT - 1, 1, False, False)
                for b in range(2):
                    sp.wait_ge(stored[b], 32 * (NT // 2))
                sp.wait_ge(dir_done, 1)
                sp.dma_start(dirst[0:1, 0:row_at + 1], dir_sb[:]).then_inc(dir_stored, 16)
                for k in range(NCOL):
                    at = row_at + 1 + k * P
                    sp.dma_start(dirst[0:1, at:at + P].rearrange("o (p q) -> (o p) q", q=1), row_i[:, k:k + 1]).then_inc(dir_stored, 16)
                sp.wait_ge(dir_stored, 16 * (NCOL + 1))

            @block.gpsimd
            def _(pool):
                nc.gpsimd.memset(ident[:], 0.0).then_inc(set_up, 1)
                nc.gpsimd.memset(before[:], 1.0).then_inc(set_up, 1)
                nc.gpsimd.memset(ones[:], 1.0).then_inc(masks_ready, 1)
                nc.gpsimd.memset(f32(ones_row[:]), 1.0).then_inc(masks_ready, 1)
                nc.gpsimd.memset(fill[:], 0.0).then_inc(set_up, 1)
                nc.gpsimd.memset(zeros[:], 0.0).then_inc(fill_ready, 1)
                pool.wait_ge(set_up, 3)
                nc.gpsimd.affine_select(out=ident[:], in_=ident[:], compare_op=ALU.not_equal, fill=1.0, base=0,
                                        pattern=[[-1, P]], channel_multiplier=1).then_inc(masks_ready, 1)
                nc.gpsimd.affine_select(out=before[:], in_=before[:], compare_op=ALU.is_gt, fill=0.0, base=0,
                                        pattern=[[1, P]], channel_multiplier=-1).then_inc(masks_ready, 1)
                nc.gpsimd.iota(iota_e[:], pattern=[[1, E]], base=0, channel_multiplier=0,
                               allow_small_or_imprecise_dtypes=True).then_inc(masks_ready, 1)
                nc.gpsimd.iota(token[:], pattern=[[0, 1]], base=0, channel_multiplier=1,
                               allow_small_or_imprecise_dtypes=True).then_inc(masks_ready, 1)
                nc.gpsimd.iota(tile_id[:], pattern=[[P, NCOL]], base=0, channel_multiplier=1,
                               allow_small_or_imprecise_dtypes=True).then_inc(masks_ready, 1)
                nc.gpsimd.iota(fill[:].bitcast(I32)[:, :, 0], pattern=[[1, P]], base=T, channel_multiplier=0).then_inc(fill_ready, 1)
                for dst, src in ((gamma_sb, row_broadcast(gamma, H)), (beta_sb, row_broadcast(beta, H)),
                                 (gate_sb, gateT.rearrange("(c p) e -> p c e", p=P))):
                    pool.dma_start(dst[:], src).then_inc(consts_in, 16)
                pool.wait_ge(fill_ready, 2)
                for k in range(FILLS):
                    rows = table[k * P * P:(k + 1) * P * P, :].rearrange("(p r) w -> p (r w)", p=P)
                    pool.dma_start(rows, fill[:].rearrange("p r w -> p (r w)")).then_inc(filled, 16)
                for dst in (acc, h2st):
                    pool.dma_start(dst[T:T + P, :], zeros[:]).then_inc(filled, 16)
                pool.wait_ge(filled, 16 * (FILLS + 2))

                def scatter(j, b):
                    pool.wait_ge(slot_done, j + 1)
                    pool.sem_inc(pool_passed, 1)
                    for k in range(TOPK):
                        nc.gpsimd.indirect_dma_start(
                            out=table[:, :], out_offset=bass.IndirectOffsetOnAxis(ap=slot[:, b, k:k + 1], axis=0),
                            in_=record[:, b, k, :], in_offset=None).then_inc(scattered[b], 16)

                with pool.Fori(0, NT // 2) as h:
                    scatter(2 * h, 0)
                    scatter(2 * h + 1, 1)
                for b in range(2):
                    pool.wait_ge(scattered[b], 16 * TOPK * (NT // 2))

            @block.tensor
            def _(pe):
                def product(i, b, h):
                    if h == 0:
                        pe.wait_ge(c_lo_done, i + 1)
                        if not (known(i) and i < 2):
                            pe.wait_ge(d_done, i - 1)
                    first = known(i) and i == 0 and h == 0
                    cols = slice(h * HALF, (h + 1) * HALF)
                    for c in range(C):
                        if first:
                            pe.wait_ge(w_lo_done, c + 1)
                        nc.tensor.matmul(o[:, b, cols], c_hi[:, b, c], w_hi[:, c, cols], start=(c == 0), stop=False)
                        nc.tensor.matmul(o[:, b, cols], c_hi[:, b, c], w_lo[:, c, cols], start=False, stop=False)
                        nc.tensor.matmul(o[:, b, cols], c_lo[:, b, c], w_hi[:, c, cols], start=False, stop=False)
                    if first:
                        pe.wait_ge(bo_ready, 2)
                        pe.wait_ge(masks_ready, 7)
                    nc.tensor.matmul(o[:, b, cols], ones_row[:], bo_hi[:, cols], start=False, stop=False)
                    nc.tensor.matmul(o[:, b, cols], ones_row[:], bo_lo[:, cols], start=False, stop=True).then_inc(gemm_done, 1)

                def transpose(j, b):
                    pe.wait_ge(h2_done, j + 1)
                    for c in range(C):
                        last = nc.tensor.transpose(tps[:, c], h2[:, b, c * P:(c + 1) * P], ident[:])
                    last.then_inc(t_done, 1)

                def logits_of(j):
                    if known(j) and j < 1:
                        pe.wait_ge(consts_in, 16 * CONSTS)
                    else:
                        pe.wait_ge(diff_done, j)
                    pe.wait_ge(h2T_done, j + 1)
                    for c in range(C):
                        last = nc.tensor.matmul(lps[:, 0:E], h2T[:, c], gate_sb[:, c], start=(c == 0), stop=(c == C - 1))
                    last.then_inc(logits_done, 1)

                def positions(j, b):
                    pe.wait_ge(mask_done, j + 1)
                    nc.tensor.matmul(pps[:, 0:E], before[:], mask[:, b], start=True, stop=False)
                    nc.tensor.matmul(pps[:, 0:E], ones[:], seen[:, b], start=False, stop=True).then_inc(pos_done, 1)

                def body(i, b, n, gemm, more, norm, router, slots):
                    if router:
                        transpose(i - 2, b)
                    if gemm:
                        product(i, b, 0)
                    if slots:
                        positions(i - 3, 1 - b)
                    if router:
                        logits_of(i - 2)
                    if gemm:
                        for h in range(1, HV):
                            product(i, b, h)
                tiles(pe, body)
                pe.wait_ge(slot_done, NT)
                nc.tensor.matmul(pps[:, 0:E], ones[:], seen[:, NT % 2], start=True, stop=True).then_inc(count_done, 1)

            @block.scalar
            def _(act):
                act.dma_start(bo_row[:], bo).then_inc(small_in, 16)
                act.dma_start(rs_raw[:], rscale.broadcast_to([P, 1])).then_inc(small_in, 16)
                for c in range(C):
                    act.wait_ge(w_in[c % 4], 16 * (c // 4 + 1))
                    nc.scalar.copy(w_hi[:, c], w_raw[:, c % 4]).then_inc(w_hi_done, 1)
                    if c == 1:
                        act.wait_ge(cn_done, 1)
                        nc.scalar.copy(c_hi[:, 0], cn[:, 0]).then_inc(c_hi_done, 1)
                act.wait_ge(small_in, 32)
                nc.scalar.copy(bo_hi[:], bo_row[:]).then_inc(bo_ready, 1)
                act.wait_ge(rs_ready, 2)

                def root(j, k):
                    act.wait_ge(mv_ready, 2 * j + k + 1)
                    nc.scalar.activation(std[:, k], mv[:, k, 1:2], ACT.Sqrt, bias=eps[:]).then_inc(std_ready, 1)

                def body(i, b, n, gemm, more, norm, router, slots):
                    if router:
                        act.wait_ge(t_done, i - 1)
                        nc.scalar.copy(h2T[:], tps[:]).then_inc(h2T_done, 1)
                    if norm:
                        root(i - 1, 0)
                    if more:
                        act.wait_ge(cn_done, i + 2)
                        if not (known(i) and i < 1):
                            act.wait_ge(gemm_done, HV * i)
                        nc.scalar.copy(c_hi[:, 1 - b], cn[:, 1 - b]).then_inc(c_hi_done, 1)
                    if norm:
                        root(i - 1, 1)
                        act.wait_ge(shift_done, i)
                        if not (known(i) and i < 3):
                            act.wait_ge(t_done, i - 2)
                        nc.scalar.activation(h2[:, 1 - b], x1[:, 1 - b], ACT.Identity, bias=shift[:],
                                             scale=rstd[:, 1]).then_inc(h2_done, 1)
                    if router:
                        act.wait_ge(diff_done, i - 1)
                        nc.scalar.activation(e8[:], diff[:], ACT.Exp, accum_out=esum[:]).then_inc(e8_done, 1)
                    if gemm:
                        act.wait_ge(gemm_done, HV * i + HV)
                        if not (known(i) and i < 2):
                            act.wait_ge(x1_done, i - 1)
                        nc.scalar.activation(d[:, b], o[:, b], ACT.Copy, scale=rs_sb[:]).then_inc(d_done, 1)
                tiles(act, body)

            @block.vector
            def _(dve):
                def divide(b, n):
                    dve.wait_ge(c_in[b], 48 * (n + 1))
                    nc.vector.tensor_tensor(cn[:, b], c_raw[:, b], r_t[:, b], ALU.mult).then_inc(cn_done, 1)

                def context_low(i, b):
                    dve.wait_ge(c_hi_done, i + 1)
                    nc.vector.tensor_tensor(c_lo[:, b], cn[:, b], f32(c_hi[:, b]), ALU.subtract).then_inc(c_lo_done, 1)

                def carry_wait():
                    dve.sem_inc(dve_passed, 1)

                NORM_STEPS = 2 * (HV + 1) + 2

                def moments(i, k, src, at, meanwhile):
                    for h in range(HV):
                        nc.vector.bn_stats(stats[:, k, h], src[:, h * HALF:(h + 1) * HALF]).then_inc(norm_step, 1)
                    dve.wait_ge(norm_step, NORM_STEPS * i + at + HV)
                    carry_wait()
                    nc.vector.bn_aggr(mv[:, k], stats[:, k]).then_inc(mv_ready, 1)
                    meanwhile()
                    dve.wait_ge(std_ready, 2 * i + k + 1)
                    nc.vector.reciprocal(rstd[:, k], std[:, k]).then_inc(norm_step, 1)
                    dve.wait_ge(norm_step, NORM_STEPS * i + at + HV + 1)

                def normalize(i, b, nth, more):
                    dve.wait_ge(d_done, i + 1)
                    moments(i, 0, d[:, b], 0, (lambda: divide(b, nth)) if more else (lambda: None))
                    nc.vector.scalar_tensor_tensor(out=scaled[:], in0=d[:, b], scalar=mv[:, 0, 0:1], in1=gamma_sb[:],
                                                   op0=ALU.subtract, op1=ALU.mult).then_inc(norm_step, 1)
                    dve.wait_ge(norm_step, NORM_STEPS * i + HV + 2)
                    dve.wait_ge(x_in[b], 16 * nth)
                    nc.vector.scalar_tensor_tensor(out=normed[:], in0=scaled[:], scalar=rstd[:, 0], in1=x_t[:, b],
                                                   op0=ALU.mult, op1=ALU.add).then_inc(norm_step, 1)
                    dve.wait_ge(norm_step, NORM_STEPS * i + HV + 3)
                    if not (known(i) and i < 2):
                        dve.wait_ge(stored[b], 32 * nth - 32)
                    nc.vector.tensor_tensor(x1[:, b], normed[:], beta_sb[:], ALU.add).then_inc(x1_done, 1)
                    dve.wait_ge(x1_done, i + 1)
                    moments(i, 1, x1[:, b], HV + 3, (lambda: context_low(i + 2, b)) if more else (lambda: None))
                    nc.vector.tensor_scalar(shift[:], mv[:, 1, 0:1], rstd[:, 1], -1.0, ALU.mult, ALU.mult).then_inc(shift_done, 1)

                def slot_rows(j, b):
                    dve.wait_ge(pos_done, j + 1)
                    nc.vector.tensor_tensor(row_e[:], pps[:, 0:E], rowbase[:], ALU.add).then_inc(slot_step, 1)

                def slot_products(j, b):
                    dve.wait_ge(slot_step, 3 * j + 1)
                    nc.vector.tensor_tensor(prod[:], onehot[:, b], row_e[:].unsqueeze(1).broadcast_to([P, TOPK, E]), ALU.mult).then_inc(slot_step, 1)

                def slot_sums(j, b):
                    dve.wait_ge(slot_step, 3 * j + 2)
                    nc.vector.tensor_reduce(slot_f[:], prod[:], AX.X, ALU.add).then_inc(slot_step, 1)

                def slot_numbers(j, b):
                    dve.wait_ge(slot_step, 3 * j + 3)
                    nc.vector.tensor_copy(slot[:, b], slot_f[:]).then_inc(slot_done, 1)

                ROUTE_STEPS = 6

                def route(j, b, done_before, before):
                    def step(k):
                        dve.wait_ge(route_step, ROUTE_STEPS * j + k)
                    dve.wait_ge(logits_done, j + 1)
                    nc.vector.tensor_copy(logits[:], lps[:, 0:E]).then_inc(route_step, 1)
                    if before:
                        slot_rows(*before)
                    step(1)
                    carry_wait()
                    nc.vector.max(top[:], logits[:]).then_inc(route_step, 1)
                    if before:
                        slot_products(*before)
                    step(2)
                    carry_wait()
                    nc.vector.max_index(top_i[:], top[:], logits[:]).then_inc(route_step, 1)
                    nc.vector.tensor_scalar(diff[:], top[:], top[:, 0:1], None, ALU.subtract).then_inc(diff_done, 1)
                    if before:
                        slot_sums(*before)
                    step(3)
                    nc.vector.tensor_copy(top_f[:], top_i[:]).then_inc(route_step, 1)
                    if before:
                        slot_numbers(*before)
                    step(4)
                    nc.vector.tensor_tensor(onehot[:, b], top_f[:].unsqueeze(2).broadcast_to([P, TOPK, E]),
                                            iota_e[:].unsqueeze(1).broadcast_to([P, TOPK, E]), ALU.is_equal).then_inc(route_step, 1)
                    step(5)
                    nc.vector.tensor_reduce(mask[:, b], onehot[:, b].rearrange("p k e -> p e k"), AX.X, ALU.add).then_inc(mask_done, 1)
                    dve.wait_ge(mask_done, j + 1)
                    if not (known(j) and j < 1):
                        dve.wait_ge(pos_done, j)
                    nc.vector.tensor_tensor(seen[:, 1 - b], seen[:, b], mask[:, b], ALU.add).then_inc(seen_done, 1)
                    dve.wait_ge(seen_done, j + 1)
                    dve.wait_ge(e8_done, j + 1)
                    nc.vector.reciprocal(rsum[:], esum[:]).then_inc(route_step, 1)
                    step(6)
                    dve.wait_ge(scattered[b], 16 * TOPK * done_before)
                    nc.vector.tensor_scalar(record[:, b, :, 1], e8[:], rsum[:], None, ALU.mult).then_inc(record_done, 1)
                    nc.vector.tensor_copy(record[:].bitcast(I32)[:, b, :, 0], token[:].broadcast_to([P, TOPK])).then_inc(record_done, 1)
                    dve.wait_ge(record_done, 3 * j + 2)
                    nc.vector.tensor_scalar(token[:], token[:], float(P), None, ALU.add).then_inc(record_done, 1)

                nc.vector.memset(eps[:], EPS).then_inc(rs_ready, 1)
                nc.vector.memset(seen[:, 0], 0.0).then_inc(seen_ready, 1)
                dve.wait_ge(c_in[0], 48)
                for c in range(C):
                    if c == 1:
                        divide(0, 0)
                        context_low(0, 0)
                    dve.wait_ge(w_hi_done, c + 1)
                    nc.vector.tensor_tensor(w_lo[:, c], w_raw[:, c % 4], f32(w_hi[:, c]), ALU.subtract).then_inc(w_lo_done, 1)
                dve.wait_ge(small_in, 32)
                nc.vector.tensor_scalar(rs_sb[:], rs_raw[:], 0.0, RES_SCALE_MAX, ALU.max, ALU.min).then_inc(rs_ready, 1)
                dve.wait_ge(bo_ready, 1)
                nc.vector.tensor_tensor(bo_lo[:], bo_row[:], f32(bo_hi[:]), ALU.subtract).then_inc(bo_ready, 1)
                dve.wait_ge(masks_ready, 7)
                nc.vector.tensor_scalar(rowbase[:], iota_e[:], float(REGION), float(REGION), ALU.mult, ALU.add).then_inc(seen_ready, 1)
                dve.wait_ge(seen_ready, 2)
                dve.wait_ge(consts_in, 16 * CONSTS)

                def body(i, b, n, gemm, more, norm, router, slot):
                    if norm:
                        normalize(i - 1, 1 - b, n + b, more)
                    elif more:
                        divide(1 - b, n + b)
                        context_low(i + 1, 1 - b)
                    before = (i - 3, 1 - b) if slot else None
                    if router:
                        route(i - 2, b, n - 1, before)
                    elif slot:
                        for part in (slot_rows, slot_products, slot_sums, slot_numbers):
                            part(*before)
                tiles(dve, body)

                steps = [0]

                def step(instruction):
                    instruction.then_inc(dir_step, 1)
                    steps[0] += 1
                    dve.wait_ge(dir_step, steps[0])

                dve.wait_ge(count_done, 1)
                step(nc.vector.tensor_scalar(cnt[:], pps[:, 0:E], float(P - 1), None, ALU.add))
                step(nc.vector.tensor_copy(tiles_i[:], cnt[:]))
                step(nc.vector.tensor_scalar(tiles_i[:], tiles_i[:], P.bit_length() - 1, None, ALU.arith_shift_right))
                step(nc.vector.tensor_copy(tiles_f[:], tiles_i[:]))
                step(nc.vector.tensor_scalar(tiles_f[:], tiles_f[:], 1.0, None, ALU.max))
                step(nc.vector.tensor_tensor_scan(upto[:], ones[:, 0:E], tiles_f[:], 0.0, ALU.mult, ALU.add))
                step(nc.vector.tensor_tensor(base[:], upto[:], tiles_f[:], ALU.subtract))
                step(nc.vector.tensor_tensor(cmp[:], base[:].unsqueeze(1).broadcast_to([P, NCOL, E]),
                                             tile_id[:].unsqueeze(2).broadcast_to([P, NCOL, E]), ALU.is_le))
                step(nc.vector.tensor_reduce(started[:], cmp[:], AX.X, ALU.add))
                step(nc.vector.tensor_tensor(cmp[:], cmp[:], base[:].unsqueeze(1).broadcast_to([P, NCOL, E]), ALU.mult))
                step(nc.vector.tensor_reduce(first_of[:], cmp[:], AX.X, ALU.max))
                step(nc.vector.tensor_tensor(row_f[:], tile_id[:], first_of[:], ALU.subtract))
                step(nc.vector.tensor_scalar(row_f[:], row_f[:], float(P), None, ALU.mult))
                step(nc.vector.tensor_scalar(started[:], started[:], float(REGION), None, ALU.mult))
                step(nc.vector.tensor_tensor(row_f[:], row_f[:], started[:], ALU.add))
                step(nc.vector.tensor_copy(row_i[:], row_f[:]))
                step(nc.vector.tensor_copy(dir_sb[0:1, n_at:n_at + E], tiles_f[0:1, :]))
                step(nc.vector.tensor_copy(dir_sb[0:1, base_at:base_at + E], base[0:1, :]))
                step(nc.vector.tensor_scalar(dir_sb[0:1, last_at:last_at + 1], upto[0:1, E - 1:E], -1.0, None, ALU.add))
                nc.vector.memset(dir_sb[0:1, row_at:row_at + 1], 0).then_inc(dir_done, 1)


def experts_pass(nc, h2st, table, dirst, w_gate, w_up, w_down, acc):
    E, H, I = w_gate.shape
    C, CI, HV = H // P, I // P, H // HALF
    n_at, base_at, last_at, row_at = directory(E)
    NDIR = dirst.shape[1]
    MAX_TILES = NDIR - row_at - 1
    with ExitStack() as st:
        s = Scope(nc, st, "moe")
        raw_g, raw_u, raw_d = s.sb("raw_g", [P, C, I]), s.sb("raw_u", [P, C, I]), s.sb("raw_d", [P, CI, H])
        gu_hi, gu_lo = s.sb("gu_hi", [P, 2, 2, C, I], F32R), s.sb("gu_lo", [P, 2, 2, C, I], F32R)
        d_hi, d_lo = s.sb("d_hi", [P, 2, CI, H], F32R), s.sb("d_lo", [P, 2, CI, H], F32R)
        tokens, xT_hi, xT_lo = s.sb("tokens", [P, H]), s.sb("xT_hi", [P, C, P], F32R), s.sb("xT_lo", [P, C, P], F32R)
        silu, hidden = s.sb("silu", [P, I]), s.sb("hidden", [P, I])
        hT_hi, hT_lo = s.sb("hT_hi", [P, CI, P], F32R), s.sb("hT_lo", [P, CI, P], F32R)
        y = s.sb("y", [P, H])
        ident, rec_g, rec_s = s.sb("ident", [P, P]), s.sb("rec_g", [P, 2]), s.sb("rec_s", [P, 2])
        dir_sb = s.sb("dir", [1, NDIR], I32)
        gate_ps, up_ps, hT_ps = s.ps("gate", [P, HALF]), s.ps("up", [P, HALF]), s.ps("hT", [P, HALF // P, P])[:, 0:CI]
        xT_ps, y_ps = s.ps("xT", [P, C, P]), s.ps("y", [P, H])

        raw_in = [s.sem(f"raw_in{i}") for i in range(3)]
        dir_in, set_up, ready, pool_passed, sp_passed = s.sem("dir_in"), s.sem("set_up"), s.sem("ready"), s.sem("pool_passed"), s.sem("sp_passed")
        w_hi_done, w_lo_done = s.sem("w_hi_done"), s.sem("w_lo_done")
        rec_g_in, rec_s_in, gathered, added = s.sem("rec_g_in"), s.sem("rec_s_in"), s.sem("gathered"), s.sem("added")
        xT_done, xT_hi_done, xT_lo_done = s.sem("xT_done"), s.sem("xT_hi_done"), s.sem("xT_lo_done")
        gu_done, silu_done, hidden_done = s.sem("gu_done"), s.sem("silu_done"), s.sem("hidden_done")
        hT_done, hT_hi_done, hT_lo_done = s.sem("hT_done"), s.sem("hT_hi_done"), s.sem("hT_lo_done")
        down_done, y_done = s.sem("down_done"), s.sem("y_done")


        def pieces(b):
            for k, raw in enumerate((raw_g, raw_u)):
                for c in range(0, C, 2):
                    yield raw[:, c:c + 2], raw_in[k], gu_hi[:, b, k, c:c + 2], gu_lo[:, b, k, c:c + 2]
            for c in range(CI):
                yield raw_d[:, c], raw_in[2], d_hi[:, b, c], d_lo[:, b, c]
        PIECES = C + CI
        EARLY = 3

        def experts(eng, body, peel=False):
            if peel:
                body(0, 0, True, True)
                body(1, 1, True, True)
            with eng.Fori(1 if peel else 0, E // 2 - 1) as h:
                body(2 * h, 0, True, True)
                body(2 * h + 1, 1, True, True)
            body(E - 2, 0, True, False)
            body(E - 1, 1, False, False)

        def expert_tiles(eng, e, first_tile, tile):
            n = eng.value_load(dir_sb[0:1, bass.ds(n_at + e, 1)], min_val=1, max_val=REGION // P)
            base = eng.value_load(dir_sb[0:1, bass.ds(base_at + e, 1)], min_val=0, max_val=MAX_TILES - 64)
            first_tile(base)
            with eng.If(n > 1):
                with eng.Fori(1, n) as j:
                    tile(base + j)

        with nc.Block() as block:
            @block.sync
            def _(sp):
                sp.dma_start(dir_sb[:], dirst).then_inc(dir_in, 16)
                for k, (raw, src) in enumerate(((raw_g, w_gate), (raw_u, w_up), (raw_d, w_down))):
                    sp.dma_start(raw[:], src[0].rearrange("(c p) i -> p c i", p=P)).then_inc(raw_in[k], 16)
                sp.wait_ge(dir_in, 16)
                last_tile = sp.value_load(dir_sb[0:1, last_at:last_at + 1], min_val=E - 1, max_val=MAX_TILES - 2)

                def load_weights(e):
                    split_then = (C // 2, C, PIECES)
                    for k, (raw, src) in enumerate(((raw_g, w_gate), (raw_u, w_up), (raw_d, w_down))):
                        sp.wait_ge(w_lo_done, PIECES * (e - 1) + split_then[k])
                        sp.sem_inc(sp_passed, 1)
                        sp.dma_start(raw[:], src[bass.ds(e, 1)].rearrange("o (c p) i -> p (o c) i", p=P)).then_inc(raw_in[k], 16)

                def record(dst, t, sem):
                    row = sp.value_load(dir_sb[0:1, bass.ds(row_at + 1 + t, 1)], min_val=0, max_val=table.shape[0] - P)
                    sp.dma_start(dst[:], table[bass.ds(row, P), :]).then_inc(sem, 16)

                record(rec_g, 0, rec_g_in)
                for t in range(2):
                    sp.wait_ge(gathered, 16 * (t + 1))
                    record(rec_g, t + 1, rec_g_in)
                load_weights(1)

                def tile(t, is_first=False):
                    if not is_first:
                        sp.wait_ge(added, 16 * t)
                    sp.sem_inc(sp_passed, 1)
                    record(rec_s, t - 1, rec_s_in)
                    sp.wait_ge(gathered, 16 * (t + 3))
                    sp.sem_inc(sp_passed, 1)
                    record(rec_g, t + 3, rec_g_in)

                def expert(e, b, has_next, has_second):
                    def first(t):
                        tile(t, isinstance(e, int) and e == 0)
                        if has_second:
                            load_weights(e + 2)
                    expert_tiles(sp, e, first, tile)
                experts(sp, expert, peel=True)
                sp.wait_ge(added, 16 * last_tile + 16)
                record(rec_s, last_tile, rec_s_in)
                sp.wait_ge(rec_g_in, 16 * last_tile + 64)
                sp.sem_inc(sp_passed, 1)
                sp.wait_ge(added, 16 * last_tile + 32)
                sp.sem_inc(sp_passed, 1)

            @block.gpsimd
            def _(pool):
                nc.gpsimd.memset(ident[:], 0.0).then_inc(set_up, 1)
                pool.wait_ge(set_up, 1)
                nc.gpsimd.affine_select(out=ident[:], in_=ident[:], compare_op=ALU.not_equal, fill=1.0, base=0,
                                        pattern=[[-1, P]], channel_multiplier=1).then_inc(ready, 1)
                pool.wait_ge(dir_in, 16)
                last_tile = pool.value_load(dir_sb[0:1, last_at:last_at + 1], min_val=E - 1, max_val=MAX_TILES - 2)

                def gather(t):
                    pool.wait_ge(rec_g_in, 16 * (t + 1))
                    pool.wait_ge(xT_done, t)
                    pool.sem_inc(pool_passed, 1)
                    nc.gpsimd.indirect_dma_start(
                        out=tokens[:], out_offset=None, in_=h2st[:, :],
                        in_offset=bass.IndirectOffsetOnAxis(ap=rec_g[:].bitcast(I32)[:, 0:1], axis=0)).then_inc(gathered, 16)

                def add(t):
                    pool.wait_ge(y_done, t + 3)
                    pool.sem_inc(pool_passed, 1)
                    nc.gpsimd.indirect_dma_start(
                        out=acc[:, :], out_offset=bass.IndirectOffsetOnAxis(ap=rec_s[:].bitcast(I32)[:, 0:1], axis=0),
                        in_=y[:], in_offset=None, compute_op=ALU.add).then_inc(added, 16)

                gather(0)
                gather(1)
                with pool.Fori(0, last_tile + 1) as t:
                    gather(t + 2)
                    add(t - 1)
                add(last_tile)

            @block.tensor
            def _(pe):
                pe.sem_inc(hT_done, 1)
                pe.wait_ge(ready, 4)
                pe.wait_ge(dir_in, 16)

                def transpose_tokens(t):
                    pe.wait_ge(gathered, 16 * (t + 1))
                    for c in range(C):
                        last = nc.tensor.transpose(xT_ps[:, c], tokens[:, c * P:(c + 1) * P], ident[:])
                    last.then_inc(xT_done, 1)

                def down(t, b):
                    pe.wait_ge(hT_lo_done, t + 2)
                    pe.wait_ge(y_done, t + 2)
                    for h in range(HV):
                        cols = slice(h * HALF, (h + 1) * HALF)
                        for c in range(CI):
                            nc.tensor.matmul(y_ps[:, cols], hT_hi[:, c], d_hi[:, b, c, cols], start=(c == 0), stop=False)
                            nc.tensor.matmul(y_ps[:, cols], hT_hi[:, c], d_lo[:, b, c, cols], start=False, stop=False)
                            last = nc.tensor.matmul(y_ps[:, cols], hT_lo[:, c], d_hi[:, b, c, cols], start=False, stop=(c == CI - 1))
                    last.then_inc(down_done, 1)

                def tile(t, b, b_before, e=None):
                    pe.wait_ge(xT_lo_done, t + 1)
                    pe.wait_ge(hidden_done, t + 1)
                    for k, o in enumerate((gate_ps, up_ps)):
                        if e is not None:
                            pe.wait_ge(w_lo_done, PIECES * e + (k + 1) * (C // 2))
                        for c in range(C):
                            nc.tensor.matmul(o[:, 0:I], xT_hi[:, c], gu_hi[:, b, k, c], start=(c == 0), stop=False)
                            nc.tensor.matmul(o[:, 0:I], xT_hi[:, c], gu_lo[:, b, k, c], start=False, stop=False)
                            last = nc.tensor.matmul(o[:, 0:I], xT_lo[:, c], gu_hi[:, b, k, c], start=False, stop=(c == C - 1))
                        last.then_inc(gu_done, 1)
                    transpose_tokens(t + 1)
                    down(t - 1, b_before)
                    pe.wait_ge(hidden_done, t + 2)
                    for c in range(CI):
                        last = nc.tensor.transpose(hT_ps[:, c], hidden[:, c * P:(c + 1) * P], ident[:])
                    last.then_inc(hT_done, 1)
                    if e is not None:
                        pe.wait_ge(w_lo_done, PIECES * e + PIECES)

                transpose_tokens(0)

                def expert(e, b, has_next, has_second):
                    expert_tiles(pe, e, lambda t: tile(t, b, 1 - b, e), lambda t: tile(t, b, b))
                experts(pe, expert)
                last_tile = pe.value_load(dir_sb[0:1, last_at:last_at + 1], min_val=E - 1, max_val=MAX_TILES - 2)
                down(last_tile, (E - 1) % 2)

            @block.scalar
            def _(act):
                def split(e, b, lo, hi):
                    for n, (raw, loaded, high, low) in enumerate(pieces(b)):
                        if lo <= n < hi:
                            act.wait_ge(loaded, 16 * (e + 1))
                            nc.scalar.copy(high, raw).then_inc(w_hi_done, 1)

                def tokens_high(t):
                    act.wait_ge(xT_done, t + 1)
                    nc.scalar.copy(xT_hi[:], xT_ps[:]).then_inc(xT_hi_done, 1)

                def output(t):
                    act.wait_ge(down_done, t + 2)
                    act.wait_ge(rec_s_in, 16 * (t + 2))
                    nc.scalar.activation(y[:], y_ps[:], ACT.Copy, scale=rec_s[:, 1:2]).then_inc(y_done, 1)

                def tile(t, e=None, b=None):
                    act.wait_ge(gu_done, 2 * t + 1)
                    act.wait_ge(hidden_done, t + 1)
                    nc.scalar.activation(silu[:], gate_ps[:, 0:I], ACT.Silu).then_inc(silu_done, 1)
                    tokens_high(t + 1)
                    if e is not None:
                        split(e, b, 0, EARLY)
                    output(t - 1)
                    act.wait_ge(hT_done, t + 2)
                    nc.scalar.copy(hT_hi[:], hT_ps).then_inc(hT_hi_done, 1)
                    if e is not None:
                        split(e, b, EARLY, PIECES)

                act.sem_inc(y_done, 1)
                act.wait_ge(dir_in, 16)
                split(0, 0, 0, PIECES)
                tokens_high(0)

                def expert(e, b, has_next, has_second):
                    if has_next:
                        expert_tiles(act, e, lambda t: tile(t, e + 1, 1 - b), tile)
                    else:
                        expert_tiles(act, e, tile, tile)
                experts(act, expert)
                last_tile = act.value_load(dir_sb[0:1, last_at:last_at + 1], min_val=E - 1, max_val=MAX_TILES - 2)
                output(last_tile)

            @block.vector
            def _(dve):
                def split(e, b, lo, hi):
                    for n, (raw, loaded, high, low) in enumerate(pieces(b)):
                        if lo <= n < hi:
                            dve.wait_ge(w_hi_done, PIECES * e + n + 1)
                            nc.vector.tensor_tensor(low, raw, f32(high), ALU.subtract).then_inc(w_lo_done, 1)

                def tokens_low(t):
                    dve.wait_ge(xT_hi_done, t + 1)
                    nc.vector.tensor_tensor(xT_lo[:], xT_ps[:], f32(xT_hi[:]), ALU.subtract).then_inc(xT_lo_done, 1)

                def tile(t, e=None, b=None):
                    dve.wait_ge(silu_done, t + 1)
                    dve.wait_ge(gu_done, 2 * t + 2)
                    dve.wait_ge(hT_done, t + 1)
                    nc.vector.tensor_tensor(hidden[:], silu[:], up_ps[:, 0:I], ALU.mult).then_inc(hidden_done, 1)
                    tokens_low(t + 1)
                    if e is not None:
                        split(e, b, 0, EARLY)
                    dve.wait_ge(hT_hi_done, t + 1)
                    nc.vector.tensor_tensor(hT_lo[:], hT_ps, f32(hT_hi[:]), ALU.subtract).then_inc(hT_lo_done, 1)
                    if e is not None:
                        split(e, b, EARLY, PIECES)

                dve.sem_inc(hidden_done, 1)
                dve.sem_inc(hT_lo_done, 1)
                nc.vector.memset(f32(d_hi[:, 1]), 0.0).then_inc(ready, 1)
                nc.vector.memset(f32(d_lo[:, 1]), 0.0).then_inc(ready, 1)
                nc.vector.memset(f32(hT_hi[:]), 0.0)
                nc.vector.memset(f32(hT_lo[:]), 0.0).then_inc(ready, 1)
                dve.wait_ge(dir_in, 16)
                split(0, 0, 0, PIECES)
                tokens_low(0)

                def expert(e, b, has_next, has_second):
                    if has_next:
                        expert_tiles(dve, e, lambda t: tile(t, e + 1, 1 - b), tile)
                    else:
                        expert_tiles(dve, e, tile, tile)
                experts(dve, expert)


def cross_attention_and_experts(nc, x, ctxT, mask, wqT, bq, wkT, bk, wvT, bv, woT, bo, gamma, beta, rscale,
                                gateT, w_gate, w_up, w_down, out):
    H, T = ctxT.shape
    B, E = mask.shape[1], w_gate.shape[0]
    S, NH = T // B, H // HD

    def scratch(name, shape, dt=F32):
        return nc.dram_tensor(name, shape, dt, kind="Internal").ap()

    xnT = scratch("xnT", (H, T))
    kst, qst, vst = scratch("kst", (B * NH, 2 * HD, S)), scratch("qst", (B * NH, 2, HD, S)), scratch("vst", (T, NH, 2 * HD))
    ctxst, sums, rsums = scratch("ctxst", (H, T)), scratch("sums", (NH, T)), scratch("rsums", (NH, T))
    h2st, table = scratch("h2st", (T + P, H)), scratch("table", (table_regions(E) * REGION, 2))
    dirst = scratch("dirst", (1, directory(E)[-1] + 1 + 3 * P), I32)
    projection_pass(nc, "k", ctxT, wkT, bk, kst, x, xnT)
    projection_pass(nc, "v", ctxT, wvT, bv, vst)
    projection_pass(nc, "q", xnT, wqT, bq, qst)
    attention_pass(nc, kst, qst, vst, mask, ctxst, sums, B, S)
    reciprocal_pass(nc, sums, rsums)
    output_pass(nc, ctxst, rsums, woT, bo, gamma, beta, rscale, x, gateT, out, h2st, table, dirst)
    experts_pass(nc, h2st, table, dirst, w_gate, w_up, w_down, out)


def kernel(**inputs):
    from concourse import bacc
    from concourse.bass_utils import run_bass_kernel_spmd

    given = {name: np.asarray(value) for name, value in inputs.items()}
    x, mask = given["x"], given["mask_BxS2_ik0"]
    B, S, H = x.shape
    T = B * S

    def transposed(name):
        return given[name].reshape(-1, H).T

    def by_feature(name):
        return given[name].reshape(H // P, P).T

    def row(name):
        return given[name].reshape(1, -1)

    laid = {
        "x": x.reshape(T, H), "ctxT": transposed("ctx_2048"),
        "mask": mask.reshape(B, S // P, P).transpose(2, 0, 1),
        "wqT": transposed("L0_xattn_Wq"), "bq": by_feature("L0_xattn_bq"),
        "wkT": transposed("L0_xattn_Wk"), "bk": by_feature("L0_xattn_bk"),
        "wvT": transposed("L0_xattn_Wv"), "bv": row("L0_xattn_bv"),
        "woT": transposed("L0_xattn_Wo"), "bo": row("L0_xattn_bo"),
        "gamma": row("L0_xattn_ln_gamma"), "beta": row("L0_xattn_ln_beta"),
        "rscale": given["L0_xattn_residual_scale"].reshape(1, 1),
        "gateT": transposed("L0_ffn_gate_weight"),
        "w_gate": given["L0_ffn_w_gate"], "w_up": given["L0_ffn_w_up"], "w_down": given["L0_ffn_w_down"],
    }
    nc = bacc.Bacc("TRN2", target_bir_lowering=False, num_devices=1)
    arrays, args = {}, {}
    for name, a in laid.items():
        a = np.ascontiguousarray(a)
        arrays[f"in_{name}"] = a
        args[name] = nc.dram_tensor(f"in_{name}", a.shape, mybir.dt.from_np(a.dtype), kind="ExternalInput").ap()
    out = nc.dram_tensor("out", (T + P, H), F32, kind="ExternalOutput").ap()
    cross_attention_and_experts(nc, out=out, **args)
    result = run_bass_kernel_spmd(nc, [arrays], core_ids=[0])
    return result.results[0]["out"][:T].reshape(B, S, H)
```
